# Optimizing a Trainium2 kernel written in Bass

```python
import numpy as np
import jax
import jax.numpy as jnp

def _softmax(x, axis=-1):
    return jax.nn.softmax(x, axis=axis)

def _gelu(x):
    return jax.nn.gelu(x, approximate=True)

def _silu(x):
    return jax.nn.silu(x)

def _sigmoid(x):
    return jax.nn.sigmoid(x)

def _layernorm(x, axis=-1, eps=1e-05):
    m = jnp.mean(x, axis=axis, keepdims=True)
    v = jnp.var(x, axis=axis, keepdims=True)
    return (x - m) / jnp.sqrt(v + eps)

def _scatter_add(tgt, idx, src, axis=0):
    return tgt.at[idx].add(src)

def _segment_sum(src, seg, n):
    return jax.ops.segment_sum(src, seg, n)
kernel_name = 'mk_adaln_ffn_d4_seqx_r8_ef7d70'

def setup_inputs(seed: int=0):
    np.random.seed(seed)
    _w = jnp.asarray

    def _rec_inputs():
        import jax
        import jax.numpy as jnp
        _rk = jax.random.key(seed)
        x = -0.000125 + 0.9999 * jax.random.normal(jax.random.fold_in(_rk, 1), (4, 256, 256), jnp.float32)
        _lenS = 256 - jax.random.randint(jax.random.fold_in(_rk, 7), (4,), 0, max(1, 256 // 4) + 1, jnp.int32)
        _lenS2 = 256 - jax.random.randint(jax.random.fold_in(_rk, 8), (4,), 0, max(1, 256 // 4) + 1, jnp.int32)
        fside_BxSxS_0 = -1.52775e-05 + 0.999936 * jax.random.normal(jax.random.fold_in(_rk, 11), (4, 256, 256), jnp.float32)
        cond_512 = -5.03954e-05 + 1.00559 * jax.random.normal(jax.random.fold_in(_rk, 12), (4, 64), jnp.float32)
        return (x, fside_BxSxS_0, cond_512)
    x, fside_BxSxS_0, cond_512 = _rec_inputs()

    def _L0_cond_setup():
        import jax, jax.numpy as jnp
        from jax import lax
        import numpy as np
        B, T, C, TD = (8, 256, 256, 64)

        def _bi_wkv(r, k, v, w, u, time_emb):
            tf = jax.nn.sigmoid(jnp.sum(time_emb, axis=-1))[:, None, None]
            decay = jnp.exp(-jnp.exp(w.astype(jnp.float32)))[None, :] * (0.5 + 0.5 * tf[:, :, 0])
            kf = k.astype(jnp.float32)
            vf = v.astype(jnp.float32)
            ek = jnp.exp(jnp.minimum(kf, 30.0))
            ekv = ek * vf

            def step(carry, x):
                a, b = carry
                ekv_t, ek_t = x
                a = a * decay + ekv_t
                b = b * decay + ek_t
                return ((a, b), (a, b))
            ekv_t = jnp.swapaxes(ekv, 0, 1)
            ek_t = jnp.swapaxes(ek, 0, 1)
            init = (jnp.zeros_like(decay), jnp.zeros_like(decay))
            _, (nf, df) = lax.scan(step, init, (ekv_t, ek_t))
            _, (nb, db) = lax.scan(step, init, (ekv_t, ek_t), reverse=True)
            nf = jnp.swapaxes(nf, 0, 1)
            df = jnp.swapaxes(df, 0, 1)
            nb = jnp.swapaxes(nb, 0, 1)
            db = jnp.swapaxes(db, 0, 1)
            euk = jnp.exp(jnp.minimum(u.astype(jnp.float32)[None, None, :] + kf, 30.0))
            num = nf + nb - ekv + euk * vf
            den = df + db - ek + euk
            base = jax.nn.sigmoid(r.astype(jnp.float32)) * (num / jnp.maximum(den, 1e-08))
            out = base * (0.8 + 0.2 * tf)
            return out.astype(r.dtype)
        key = jax.random.key(seed)
        ks = jax.random.split(key, 6)
        return {'r': jax.random.normal(ks[0], (B, T, C), dtype=jnp.float32), 'k': jax.random.normal(ks[1], (B, T, C), dtype=jnp.float32), 'v': jax.random.normal(ks[2], (B, T, C), dtype=jnp.float32), 'w': jax.random.normal(ks[3], (C,), dtype=jnp.float32), 'u': jax.random.normal(ks[4], (C,), dtype=jnp.float32), 'time_emb': jax.random.normal(ks[5], (B, TD), dtype=jnp.float32)}
    _L0_cond_all = _L0_cond_setup()
    _L0_cond_in = {k: v for k, v in _L0_cond_all.items() if k in ('w', 'u')}
    del _L0_cond_all

    def _L0_ffn_setup():
        import jax, jax.numpy as jnp
        import numpy as np
        B, S, H = (2, 256, 256)
        E, K = (16, 4)
        I_MOE, I_SH = (176, 704)
        key = jax.random.key(seed)
        ks = jax.random.split(key, 9)

        def w(k, shape, fan_in):
            return jax.random.normal(k, shape, jnp.float32) * fan_in ** (-0.5)
        return {'hidden_states': jax.random.normal(ks[0], (B, S, H), jnp.float32), 'router_w': w(ks[1], (E, H), H), 'w_gate': w(ks[2], (E, H, I_MOE), H), 'w_up': w(ks[3], (E, H, I_MOE), H), 'w_down': w(ks[4], (E, I_MOE, H), I_MOE), 'sh_gate': w(ks[5], (H, I_SH), H), 'sh_up': w(ks[6], (H, I_SH), H), 'sh_down': w(ks[7], (I_SH, H), I_SH), 'sh_gate_w': w(ks[8], (H, 1), H)}
    _L0_ffn_all = _L0_ffn_setup()
    _L0_ffn_in = {k: v for k, v in _L0_ffn_all.items() if k in ('router_w', 'w_gate', 'w_up', 'w_down', 'sh_gate', 'sh_up', 'sh_down', 'sh_gate_w')}
    del _L0_ffn_all

    def _L1_cond_setup():
        import jax, jax.numpy as jnp
        from jax import lax
        import numpy as np
        B, T, C, TD = (8, 256, 256, 64)

        def _bi_wkv(r, k, v, w, u, time_emb):
            tf = jax.nn.sigmoid(jnp.sum(time_emb, axis=-1))[:, None, None]
            decay = jnp.exp(-jnp.exp(w.astype(jnp.float32)))[None, :] * (0.5 + 0.5 * tf[:, :, 0])
            kf = k.astype(jnp.float32)
            vf = v.astype(jnp.float32)
            ek = jnp.exp(jnp.minimum(kf, 30.0))
            ekv = ek * vf

            def step(carry, x):
                a, b = carry
                ekv_t, ek_t = x
                a = a * decay + ekv_t
                b = b * decay + ek_t
                return ((a, b), (a, b))
            ekv_t = jnp.swapaxes(ekv, 0, 1)
            ek_t = jnp.swapaxes(ek, 0, 1)
            init = (jnp.zeros_like(decay), jnp.zeros_like(decay))
            _, (nf, df) = lax.scan(step, init, (ekv_t, ek_t))
            _, (nb, db) = lax.scan(step, init, (ekv_t, ek_t), reverse=True)
            nf = jnp.swapaxes(nf, 0, 1)
            df = jnp.swapaxes(df, 0, 1)
            nb = jnp.swapaxes(nb, 0, 1)
            db = jnp.swapaxes(db, 0, 1)
            euk = jnp.exp(jnp.minimum(u.astype(jnp.float32)[None, None, :] + kf, 30.0))
            num = nf + nb - ekv + euk * vf
            den = df + db - ek + euk
            base = jax.nn.sigmoid(r.astype(jnp.float32)) * (num / jnp.maximum(den, 1e-08))
            out = base * (0.8 + 0.2 * tf)
            return out.astype(r.dtype)
        key = jax.random.key(seed)
        ks = jax.random.split(key, 6)
        return {'r': jax.random.normal(ks[0], (B, T, C), dtype=jnp.float32), 'k': jax.random.normal(ks[1], (B, T, C), dtype=jnp.float32), 'v': jax.random.normal(ks[2], (B, T, C), dtype=jnp.float32), 'w': jax.random.normal(ks[3], (C,), dtype=jnp.float32), 'u': jax.random.normal(ks[4], (C,), dtype=jnp.float32), 'time_emb': jax.random.normal(ks[5], (B, TD), dtype=jnp.float32)}
    _L1_cond_all = _L1_cond_setup()
    _L1_cond_in = {k: v for k, v in _L1_cond_all.items() if k in ('w', 'u')}
    del _L1_cond_all

    def _L1_ffn_setup():
        import jax, jax.numpy as jnp
        import numpy as np
        import math
        N_EMBD = 256
        N_HEAD = 16
        HEAD_DIM = N_EMBD // N_HEAD
        B, T = (2, 256)
        key = jax.random.key(seed)
        k1, k2, k3 = jax.random.split(key, 3)
        x = jax.random.normal(k1, (B, T, N_EMBD), dtype=jnp.float32)
        W_gate = jax.random.normal(k2, (N_HEAD, N_EMBD), dtype=jnp.float32) * 0.02
        W_qkv = jax.random.normal(k3, (3 * N_EMBD, N_EMBD), dtype=jnp.float32) * 0.02
        return {'x': x, 'W_gate': W_gate, 'W_qkv': W_qkv}
    _L1_ffn_all = _L1_ffn_setup()
    _L1_ffn_in = {k: v for k, v in _L1_ffn_all.items() if k in ('W_gate', 'W_qkv')}
    del _L1_ffn_all

    def _L2_cond_setup():
        import jax, jax.numpy as jnp
        from jax import lax
        import numpy as np
        B, T, C, TD = (8, 256, 256, 64)

        def _bi_wkv(r, k, v, w, u, time_emb):
            tf = jax.nn.sigmoid(jnp.sum(time_emb, axis=-1))[:, None, None]
            decay = jnp.exp(-jnp.exp(w.astype(jnp.float32)))[None, :] * (0.5 + 0.5 * tf[:, :, 0])
            kf = k.astype(jnp.float32)
            vf = v.astype(jnp.float32)
            ek = jnp.exp(jnp.minimum(kf, 30.0))
            ekv = ek * vf

            def step(carry, x):
                a, b = carry
                ekv_t, ek_t = x
                a = a * decay + ekv_t
                b = b * decay + ek_t
                return ((a, b), (a, b))
            ekv_t = jnp.swapaxes(ekv, 0, 1)
            ek_t = jnp.swapaxes(ek, 0, 1)
            init = (jnp.zeros_like(decay), jnp.zeros_like(decay))
            _, (nf, df) = lax.scan(step, init, (ekv_t, ek_t))
            _, (nb, db) = lax.scan(step, init, (ekv_t, ek_t), reverse=True)
            nf = jnp.swapaxes(nf, 0, 1)
            df = jnp.swapaxes(df, 0, 1)
            nb = jnp.swapaxes(nb, 0, 1)
            db = jnp.swapaxes(db, 0, 1)
            euk = jnp.exp(jnp.minimum(u.astype(jnp.float32)[None, None, :] + kf, 30.0))
            num = nf + nb - ekv + euk * vf
            den = df + db - ek + euk
            base = jax.nn.sigmoid(r.astype(jnp.float32)) * (num / jnp.maximum(den, 1e-08))
            out = base * (0.8 + 0.2 * tf)
            return out.astype(r.dtype)
        key = jax.random.key(seed)
        ks = jax.random.split(key, 6)
        return {'r': jax.random.normal(ks[0], (B, T, C), dtype=jnp.float32), 'k': jax.random.normal(ks[1], (B, T, C), dtype=jnp.float32), 'v': jax.random.normal(ks[2], (B, T, C), dtype=jnp.float32), 'w': jax.random.normal(ks[3], (C,), dtype=jnp.float32), 'u': jax.random.normal(ks[4], (C,), dtype=jnp.float32), 'time_emb': jax.random.normal(ks[5], (B, TD), dtype=jnp.float32)}
    _L2_cond_all = _L2_cond_setup()
    _L2_cond_in = {k: v for k, v in _L2_cond_all.items() if k in ('w', 'u')}
    del _L2_cond_all

    def _L2_ffn_setup():
        import jax, jax.numpy as jnp
        import numpy as np
        EPS = 1e-06

        def _quant_dequant_e4m3(v, scale):
            vn = v.astype(jnp.float32) / scale
            return vn.astype(jnp.float8_e4m3fn).astype(jnp.float32)
        key = jax.random.key(seed)
        k1, k2, k3 = jax.random.split(key, 3)
        B, S, D_IN, D_OUT = (8, 512, 256, 256)
        x = jax.random.normal(k1, (B, S, D_IN), dtype=jnp.float32).astype(jnp.bfloat16)
        bound = 1.0 / np.sqrt(D_IN)
        weight = jax.random.uniform(k2, (D_OUT, D_IN), minval=-bound, maxval=bound, dtype=jnp.float32).astype(jnp.bfloat16)
        bias = jax.random.uniform(k3, (D_OUT,), minval=-bound, maxval=bound, dtype=jnp.float32).astype(jnp.bfloat16)
        return {'x': x, 'weight': weight, 'bias': bias}
    _L2_ffn_all = _L2_ffn_setup()
    _L2_ffn_in = {k: v for k, v in _L2_ffn_all.items() if k in ('weight', 'bias')}
    del _L2_ffn_all

    def _L3_cond_setup():
        import jax, jax.numpy as jnp
        from jax import lax
        import numpy as np
        B, T, C, TD = (8, 256, 256, 64)

        def _bi_wkv(r, k, v, w, u, time_emb):
            tf = jax.nn.sigmoid(jnp.sum(time_emb, axis=-1))[:, None, None]
            decay = jnp.exp(-jnp.exp(w.astype(jnp.float32)))[None, :] * (0.5 + 0.5 * tf[:, :, 0])
            kf = k.astype(jnp.float32)
            vf = v.astype(jnp.float32)
            ek = jnp.exp(jnp.minimum(kf, 30.0))
            ekv = ek * vf

            def step(carry, x):
                a, b = carry
                ekv_t, ek_t = x
                a = a * decay + ekv_t
                b = b * decay + ek_t
                return ((a, b), (a, b))
            ekv_t = jnp.swapaxes(ekv, 0, 1)
            ek_t = jnp.swapaxes(ek, 0, 1)
            init = (jnp.zeros_like(decay), jnp.zeros_like(decay))
            _, (nf, df) = lax.scan(step, init, (ekv_t, ek_t))
            _, (nb, db) = lax.scan(step, init, (ekv_t, ek_t), reverse=True)
            nf = jnp.swapaxes(nf, 0, 1)
            df = jnp.swapaxes(df, 0, 1)
            nb = jnp.swapaxes(nb, 0, 1)
            db = jnp.swapaxes(db, 0, 1)
            euk = jnp.exp(jnp.minimum(u.astype(jnp.float32)[None, None, :] + kf, 30.0))
            num = nf + nb - ekv + euk * vf
            den = df + db - ek + euk
            base = jax.nn.sigmoid(r.astype(jnp.float32)) * (num / jnp.maximum(den, 1e-08))
            out = base * (0.8 + 0.2 * tf)
            return out.astype(r.dtype)
        key = jax.random.key(seed)
        ks = jax.random.split(key, 6)
        return {'r': jax.random.normal(ks[0], (B, T, C), dtype=jnp.float32), 'k': jax.random.normal(ks[1], (B, T, C), dtype=jnp.float32), 'v': jax.random.normal(ks[2], (B, T, C), dtype=jnp.float32), 'w': jax.random.normal(ks[3], (C,), dtype=jnp.float32), 'u': jax.random.normal(ks[4], (C,), dtype=jnp.float32), 'time_emb': jax.random.normal(ks[5], (B, TD), dtype=jnp.float32)}
    _L3_cond_all = _L3_cond_setup()
    _L3_cond_in = {k: v for k, v in _L3_cond_all.items() if k in ('w', 'u')}
    del _L3_cond_all

    def _L3_ffn_setup():
        import jax, jax.numpy as jnp
        import numpy as np
        TOP_K = 4
        key = jax.random.key(seed)
        k1, k2, k3, k4 = jax.random.split(key, 4)
        B, S, D, E, H, O = (4, 256, 256, 8, 128, 256)
        scale = 0.02
        return {'x': jax.random.normal(k1, (B, S, D), dtype=jnp.float32), 'wg': jax.random.normal(k2, (D, E), dtype=jnp.float32) * scale, 'w1': jax.random.normal(k3, (E, H, D), dtype=jnp.float32) * scale, 'w2': jax.random.normal(k4, (E, O, H), dtype=jnp.float32) * scale}
    _L3_ffn_all = _L3_ffn_setup()
    _L3_ffn_in = {k: v for k, v in _L3_ffn_all.items() if k in ('wg', 'w1', 'w2')}
    del _L3_ffn_all
    return {'x': x, 'fside_BxSxS_0': fside_BxSxS_0, 'cond_512': cond_512, 'L0_cond_w': _L0_cond_in['w'], 'L0_cond_u': _L0_cond_in['u'], 'L0_ffn_router_w': _L0_ffn_in['router_w'], 'L0_ffn_w_gate': _L0_ffn_in['w_gate'], 'L0_ffn_w_up': _L0_ffn_in['w_up'], 'L0_ffn_w_down': _L0_ffn_in['w_down'], 'L0_ffn_sh_gate': _L0_ffn_in['sh_gate'], 'L0_ffn_sh_up': _L0_ffn_in['sh_up'], 'L0_ffn_sh_down': _L0_ffn_in['sh_down'], 'L0_ffn_sh_gate_w': _L0_ffn_in['sh_gate_w'], 'L1_cond_w': _L1_cond_in['w'], 'L1_cond_u': _L1_cond_in['u'], 'L1_ffn_W_gate': _L1_ffn_in['W_gate'], 'L1_ffn_W_qkv': _L1_ffn_in['W_qkv'], 'L2_cond_w': _L2_cond_in['w'], 'L2_cond_u': _L2_cond_in['u'], 'L2_ffn_weight': _L2_ffn_in['weight'], 'L2_ffn_bias': _L2_ffn_in['bias'], 'L3_cond_w': _L3_cond_in['w'], 'L3_cond_u': _L3_cond_in['u'], 'L3_ffn_wg': _L3_ffn_in['wg'], 'L3_ffn_w1': _L3_ffn_in['w1'], 'L3_ffn_w2': _L3_ffn_in['w2']}

def reference(x, fside_BxSxS_0, cond_512, L0_cond_w, L0_cond_u, L0_ffn_router_w, L0_ffn_w_gate, L0_ffn_w_up, L0_ffn_w_down, L0_ffn_sh_gate, L0_ffn_sh_up, L0_ffn_sh_down, L0_ffn_sh_gate_w, L1_cond_w, L1_cond_u, L1_ffn_W_gate, L1_ffn_W_qkv, L2_cond_w, L2_cond_u, L2_ffn_weight, L2_ffn_bias, L3_cond_w, L3_cond_u, L3_ffn_wg, L3_ffn_w1, L3_ffn_w2):
    import jax
    import jax.numpy as jnp

    def _L0_cond_ref(r, k, v, w, u, time_emb):
        import jax, jax.numpy as jnp
        from jax import lax
        import numpy as np
        B, T, C, TD = (8, 256, 256, 64)

        def _bi_wkv(r, k, v, w, u, time_emb):
            tf = jax.nn.sigmoid(jnp.sum(time_emb, axis=-1))[:, None, None]
            decay = jnp.exp(-jnp.exp(w.astype(jnp.float32)))[None, :] * (0.5 + 0.5 * tf[:, :, 0])
            kf = k.astype(jnp.float32)
            vf = v.astype(jnp.float32)
            ek = jnp.exp(jnp.minimum(kf, 30.0))
            ekv = ek * vf

            def step(carry, x):
                a, b = carry
                ekv_t, ek_t = x
                a = a * decay + ekv_t
                b = b * decay + ek_t
                return ((a, b), (a, b))
            ekv_t = jnp.swapaxes(ekv, 0, 1)
            ek_t = jnp.swapaxes(ek, 0, 1)
            init = (jnp.zeros_like(decay), jnp.zeros_like(decay))
            _, (nf, df) = lax.scan(step, init, (ekv_t, ek_t))
            _, (nb, db) = lax.scan(step, init, (ekv_t, ek_t), reverse=True)
            nf = jnp.swapaxes(nf, 0, 1)
            df = jnp.swapaxes(df, 0, 1)
            nb = jnp.swapaxes(nb, 0, 1)
            db = jnp.swapaxes(db, 0, 1)
            euk = jnp.exp(jnp.minimum(u.astype(jnp.float32)[None, None, :] + kf, 30.0))
            num = nf + nb - ekv + euk * vf
            den = df + db - ek + euk
            base = jax.nn.sigmoid(r.astype(jnp.float32)) * (num / jnp.maximum(den, 1e-08))
            out = base * (0.8 + 0.2 * tf)
            return out.astype(r.dtype)
        return _bi_wkv(r, k, v, w, u, time_emb)

    def _L0_ffn_ref(hidden_states, router_w, w_gate, w_up, w_down, sh_gate, sh_up, sh_down, sh_gate_w):
        import jax, jax.numpy as jnp
        import numpy as np
        B, S, H = (2, 256, 256)
        E, K = (16, 4)
        I_MOE, I_SH = (176, 704)
        orig = hidden_states.shape
        h = hidden_states.reshape(-1, orig[-1])
        N = h.shape[0]
        logits = h @ router_w.T
        probs = jax.nn.softmax(logits.astype(jnp.float32), axis=-1)
        top_vals, top_idx = jax.lax.top_k(probs, K)
        top_vals = top_vals / jnp.maximum(top_vals.sum(-1, keepdims=True), 1e-09)
        top_vals = top_vals.astype(h.dtype)
        comb = jnp.zeros((N, E), h.dtype).at[jnp.arange(N)[:, None], top_idx].add(top_vals)
        g = jnp.einsum('nh,ehi->eni', h, w_gate)
        u = jnp.einsum('nh,ehi->eni', h, w_up)
        y = jnp.einsum('eni,eih->enh', jax.nn.silu(g) * u, w_down)
        routed = jnp.einsum('enh,ne->nh', y, comb)
        shared = jax.nn.silu(h @ sh_gate) * (h @ sh_up) @ sh_down
        sg = jax.nn.sigmoid(h @ sh_gate_w)
        return (routed + sg * shared).reshape(orig)

    def _L1_cond_ref(r, k, v, w, u, time_emb):
        import jax, jax.numpy as jnp
        from jax import lax
        import numpy as np
        B, T, C, TD = (8, 256, 256, 64)

        def _bi_wkv(r, k, v, w, u, time_emb):
            tf = jax.nn.sigmoid(jnp.sum(time_emb, axis=-1))[:, None, None]
            decay = jnp.exp(-jnp.exp(w.astype(jnp.float32)))[None, :] * (0.5 + 0.5 * tf[:, :, 0])
            kf = k.astype(jnp.float32)
            vf = v.astype(jnp.float32)
            ek = jnp.exp(jnp.minimum(kf, 30.0))
            ekv = ek * vf

            def step(carry, x):
                a, b = carry
                ekv_t, ek_t = x
                a = a * decay + ekv_t
                b = b * decay + ek_t
                return ((a, b), (a, b))
            ekv_t = jnp.swapaxes(ekv, 0, 1)
            ek_t = jnp.swapaxes(ek, 0, 1)
            init = (jnp.zeros_like(decay), jnp.zeros_like(decay))
            _, (nf, df) = lax.scan(step, init, (ekv_t, ek_t))
            _, (nb, db) = lax.scan(step, init, (ekv_t, ek_t), reverse=True)
            nf = jnp.swapaxes(nf, 0, 1)
            df = jnp.swapaxes(df, 0, 1)
            nb = jnp.swapaxes(nb, 0, 1)
            db = jnp.swapaxes(db, 0, 1)
            euk = jnp.exp(jnp.minimum(u.astype(jnp.float32)[None, None, :] + kf, 30.0))
            num = nf + nb - ekv + euk * vf
            den = df + db - ek + euk
            base = jax.nn.sigmoid(r.astype(jnp.float32)) * (num / jnp.maximum(den, 1e-08))
            out = base * (0.8 + 0.2 * tf)
            return out.astype(r.dtype)
        return _bi_wkv(r, k, v, w, u, time_emb)

    def _L1_ffn_ref(x, W_gate, W_qkv):
        import jax, jax.numpy as jnp
        import numpy as np
        import math
        N_EMBD = 256
        N_HEAD = 16
        HEAD_DIM = N_EMBD // N_HEAD
        B, T = (2, 256)
        Bb, Tt, C = x.shape
        H, hd = (N_HEAD, HEAD_DIM)
        gating = jax.nn.softmax(x @ W_gate.T, axis=-1)
        idx = jnp.argmax(gating, axis=-1)
        indicator = jax.nn.one_hot(idx, H, dtype=gating.dtype)
        top1_val = jnp.max(gating, axis=-1, keepdims=True)
        gating_top1 = indicator * top1_val
        qkv = x @ W_qkv.T
        q, k, v = jnp.split(qkv, 3, axis=-1)
        k = k.reshape(Bb, Tt, H, hd)
        v = v.reshape(Bb, Tt, H, hd)
        k_shared = jnp.einsum('bth,bthd->btd', indicator, k)
        v_shared = jnp.einsum('bth,bthd->btd', gating_top1, v)
        q = q.reshape(Bb, Tt, H, hd).transpose(0, 2, 1, 3)
        att = jnp.einsum('bhqd,bkd->bhqk', q, k_shared) * (1.0 / math.sqrt(hd))
        causal = jnp.tril(jnp.ones((Tt, Tt), dtype=bool))
        att = jnp.where(causal[None, None, :, :], att, -jnp.inf)
        att = jax.nn.softmax(att, axis=-1)
        y = jnp.einsum('bhqk,bkd->bhqd', att, v_shared)
        y = y.transpose(0, 2, 1, 3).reshape(Bb, Tt, C)
        return y

    def _L2_cond_ref(r, k, v, w, u, time_emb):
        import jax, jax.numpy as jnp
        from jax import lax
        import numpy as np
        B, T, C, TD = (8, 256, 256, 64)

        def _bi_wkv(r, k, v, w, u, time_emb):
            tf = jax.nn.sigmoid(jnp.sum(time_emb, axis=-1))[:, None, None]
            decay = jnp.exp(-jnp.exp(w.astype(jnp.float32)))[None, :] * (0.5 + 0.5 * tf[:, :, 0])
            kf = k.astype(jnp.float32)
            vf = v.astype(jnp.float32)
            ek = jnp.exp(jnp.minimum(kf, 30.0))
            ekv = ek * vf

            def step(carry, x):
                a, b = carry
                ekv_t, ek_t = x
                a = a * decay + ekv_t
                b = b * decay + ek_t
                return ((a, b), (a, b))
            ekv_t = jnp.swapaxes(ekv, 0, 1)
            ek_t = jnp.swapaxes(ek, 0, 1)
            init = (jnp.zeros_like(decay), jnp.zeros_like(decay))
            _, (nf, df) = lax.scan(step, init, (ekv_t, ek_t))
            _, (nb, db) = lax.scan(step, init, (ekv_t, ek_t), reverse=True)
            nf = jnp.swapaxes(nf, 0, 1)
            df = jnp.swapaxes(df, 0, 1)
            nb = jnp.swapaxes(nb, 0, 1)
            db = jnp.swapaxes(db, 0, 1)
            euk = jnp.exp(jnp.minimum(u.astype(jnp.float32)[None, None, :] + kf, 30.0))
            num = nf + nb - ekv + euk * vf
            den = df + db - ek + euk
            base = jax.nn.sigmoid(r.astype(jnp.float32)) * (num / jnp.maximum(den, 1e-08))
            out = base * (0.8 + 0.2 * tf)
            return out.astype(r.dtype)
        return _bi_wkv(r, k, v, w, u, time_emb)

    def _L2_ffn_ref(x, weight, bias):
        import jax, jax.numpy as jnp
        import numpy as np
        EPS = 1e-06

        def _quant_dequant_e4m3(v, scale):
            vn = v.astype(jnp.float32) / scale
            return vn.astype(jnp.float8_e4m3fn).astype(jnp.float32)
        xs = jnp.maximum(jnp.max(jnp.abs(x).astype(jnp.float32)), EPS)
        ws = jnp.maximum(jnp.max(jnp.abs(weight).astype(jnp.float32)), EPS)
        x_q = _quant_dequant_e4m3(x, xs)
        w_q = _quant_dequant_e4m3(weight, ws)
        y = jnp.einsum('bsk,nk->bsn', x_q, w_q) * (xs * ws)
        y = y.astype(jnp.bfloat16) + bias
        return y

    def _L3_cond_ref(r, k, v, w, u, time_emb):
        import jax, jax.numpy as jnp
        from jax import lax
        import numpy as np
        B, T, C, TD = (8, 256, 256, 64)

        def _bi_wkv(r, k, v, w, u, time_emb):
            tf = jax.nn.sigmoid(jnp.sum(time_emb, axis=-1))[:, None, None]
            decay = jnp.exp(-jnp.exp(w.astype(jnp.float32)))[None, :] * (0.5 + 0.5 * tf[:, :, 0])
            kf = k.astype(jnp.float32)
            vf = v.astype(jnp.float32)
            ek = jnp.exp(jnp.minimum(kf, 30.0))
            ekv = ek * vf

            def step(carry, x):
                a, b = carry
                ekv_t, ek_t = x
                a = a * decay + ekv_t
                b = b * decay + ek_t
                return ((a, b), (a, b))
            ekv_t = jnp.swapaxes(ekv, 0, 1)
            ek_t = jnp.swapaxes(ek, 0, 1)
            init = (jnp.zeros_like(decay), jnp.zeros_like(decay))
            _, (nf, df) = lax.scan(step, init, (ekv_t, ek_t))
            _, (nb, db) = lax.scan(step, init, (ekv_t, ek_t), reverse=True)
            nf = jnp.swapaxes(nf, 0, 1)
            df = jnp.swapaxes(df, 0, 1)
            nb = jnp.swapaxes(nb, 0, 1)
            db = jnp.swapaxes(db, 0, 1)
            euk = jnp.exp(jnp.minimum(u.astype(jnp.float32)[None, None, :] + kf, 30.0))
            num = nf + nb - ekv + euk * vf
            den = df + db - ek + euk
            base = jax.nn.sigmoid(r.astype(jnp.float32)) * (num / jnp.maximum(den, 1e-08))
            out = base * (0.8 + 0.2 * tf)
            return out.astype(r.dtype)
        return _bi_wkv(r, k, v, w, u, time_emb)

    def _L3_ffn_ref(x, wg, w1, w2):
        import jax, jax.numpy as jnp
        import numpy as np
        TOP_K = 4
        B, S, D = x.shape
        xt = x.reshape(B * S, D)
        gate = xt @ wg
        top_val, top_idx = jax.lax.top_k(gate, TOP_K)
        gs = jax.nn.softmax(top_val, axis=-1)
        gs_eff = jnp.ones_like(gs) + gs - jax.lax.stop_gradient(gs)
        h = jax.nn.relu(jnp.einsum('nd,ehd->neh', xt, w1))
        out_all = jnp.einsum('neh,eoh->neo', h, w2)
        out_k = jnp.take_along_axis(out_all, top_idx[:, :, None], axis=1)
        out = jnp.einsum('nk,nko->no', gs_eff, out_k)
        return out.reshape(B, S, -1)
    x = x + _L0_ffn_ref(_L0_cond_ref(x, fside_BxSxS_0, fside_BxSxS_0, L0_cond_w, L0_cond_u, cond_512), L0_ffn_router_w, L0_ffn_w_gate, L0_ffn_w_up, L0_ffn_w_down, L0_ffn_sh_gate, L0_ffn_sh_up, L0_ffn_sh_down, L0_ffn_sh_gate_w)
    x = x + _L1_ffn_ref(_L1_cond_ref(x, fside_BxSxS_0, fside_BxSxS_0, L1_cond_w, L1_cond_u, cond_512), L1_ffn_W_gate, L1_ffn_W_qkv)
    x = x + _L2_ffn_ref(_L2_cond_ref(x, fside_BxSxS_0, fside_BxSxS_0, L2_cond_w, L2_cond_u, cond_512), L2_ffn_weight, L2_ffn_bias)
    x = x + _L3_ffn_ref(_L3_cond_ref(x, fside_BxSxS_0, fside_BxSxS_0, L3_cond_w, L3_cond_u, cond_512), L3_ffn_wg, L3_ffn_w1, L3_ffn_w2)
    return x

_drawn_inputs = setup_inputs


def setup_inputs(seed=0):
    import zlib

    import numpy as np

    out = dict(_drawn_inputs(seed))
    spreads = {}
    factors = {'cond_512': 2.902,
     'L0_ffn_sh_gate_w': 5.242,
     'L1_cond_w': 8.0,
     'L1_cond_u': 8.0,
     'L1_ffn_W_gate': 8.0,
     'L1_ffn_W_qkv': 8.0,
     'L3_cond_u': 4.556}
    for name, (base, spread) in spreads.items():
        noise = np.random.default_rng([zlib.crc32(name.encode()), seed]).standard_normal(out[name].shape)
        drawn = base * np.exp(spread * noise) if base else spread * noise
        out[name] = jnp.asarray(drawn.astype(out[name].dtype))
    for name, factor in factors.items():
        out[name] = (out[name] * factor).astype(out[name].dtype)
    return out
```

```python
from contextlib import ExitStack

import numpy as np
import concourse.bass as bass
from concourse import mybir
from concourse.alu_op_type import AluOpType as ALU

F32 = mybir.dt.float32
F32R = mybir.dt.float32r
BF16 = mybir.dt.bfloat16
FP8 = mybir.dt.float8e4
ACT = mybir.ActivationFunctionType
AX = mybir.AxisListType

P = 128
LAYERS = 4
B, T, C, TE = 4, 256, 256, 64
N = B * T
CH = C // P
COLS = CH * N
HB = CH * B
PAIR = 2 * T
PAIRS = HB // 2
Q4 = 512
TILES = N // P
E0, I_MOE, I_SH, K0 = 16, 176, 704, 4
GATES = E0 + 1
ROWS0 = E0 * I_MOE + I_SH
CHUNKS = -(-ROWS0 // (2 * P)) * 2
WCOLS = 2 * CH * P + C
RAWCOLS = WCOLS + P
HEADS, HD = 16, 16
E3, H3, K3 = 8, 128, 4
REP = 4
HROWS = REP * HD
CAP = 30.0
LOW = -3.0e38


def at_least(eng, sem, value):
    if isinstance(value, int) and value <= 0:
        return
    eng.wait_ge(sem, value)


def build(nc, a, out, stop=9):
    ctx = ExitStack()
    with ctx:
        def sb(name, shape, dt=F32):
            return ctx.enter_context(nc.sbuf_tensor(name, shape, dt))

        def sem(name):
            return ctx.enter_context(nc.semaphore(name))

        bank = [ctx.enter_context(nc.psum_tensor(f"bank{i}", [P, Q4], F32)) for i in range(8)]

        x = sb("x", [P, COLS])
        f = sb("f", [P, COLS])
        mix = sb("mix", [P, LAYERS * COLS])
        sig = sb("sig", [P, Q4])
        s = sb("s", [P, COLS])
        s_hi = sb("s_hi", [P, COLS], F32R)
        s_lo = sb("s_lo", [P, COLS], F32R)
        temb = sb("temb", [P, B, TE])
        tsum = sb("tsum", [P, B])
        tf = sb("tf", [P, B])
        tdecay = sb("tdecay", [P, B])
        wcol = sb("wcol", [P, LAYERS, CH])
        ucol = sb("ucol", [P, LAYERS, CH])
        wexp = sb("wexp", [P, LAYERS, CH])
        wdec = sb("wdec", [P, LAYERS, CH])
        decay = sb("decay", [P, LAYERS, CH, B])
        tmul = sb("tmul", [P, CH, B])
        decay_c = decay[:, :, :, :].rearrange("p l h b -> p (l h b)")
        tmul_c = tmul[:, :, :].rearrange("p h b -> p (h b)")
        EP = E0 + 8
        prob = sb("prob", [P, TILES, EP])
        repl = sb("repl", [P, TILES, EP])
        top8 = sb("top8", [P, TILES, 8])
        rmax = sb("rmax", [P, TILES])
        rsum = sb("rsum", [P, TILES])
        rsg = sb("rsg", [P, TILES])
        gates = sb("gates", [P, TILES, GATES])
        gsplit = sb("gsplit", [P, TILES, 2, GATES], F32R)
        gsplit3 = sb("gsplit3", [P, TILES, 2, E3], F32R)
        ident = sb("ident", [P, P])
        identb = sb("identb", [P, P], BF16)

        rw = sb("rw", [P, CH, GATES])
        w1raw = sb("w1raw", [P, CH, 3 * C])
        wq_hi = sb("wq_hi", [P, CH, REP * C], F32R)
        wq_lo = sb("wq_lo", [P, CH, REP * C], F32R)
        wkv_hi = sb("wkv_hi", [P, CH, 2 * C], F32R)
        wkv_lo = sb("wkv_lo", [P, CH, 2 * C], F32R)
        wg1 = sb("wg1", [P, CH, HEADS])
        w2in = sb("w2in", [P, CH, C], BF16)
        w2q = sb("w2q", [P, CH, C], FP8)
        b2in = sb("b2in", [P, CH], BF16)
        b2 = sb("b2", [P, CH])
        wg3 = sb("wg3", [P, CH, E3])
        peak = sb("peak", [P, 4 + CH])
        peak2 = sb("peak2", [P, 2])
        peakall = sb("peakall", [P, 2])
        peakinv = sb("peakinv", [P, 2])
        scale2 = sb("scale2", [P, 1])
        own0 = ExitStack()

        def sb0(name, shape, dt=F32):
            return own0.enter_context(nc.sbuf_tensor(name, shape, dt))

        ek = sb0("ek", [P, COLS])
        ekv = sb0("ekv", [P, COLS])
        dk = sb0("dk", [P, 2, PAIR])
        dkv = sb0("dkv", [P, 2, PAIR])
        nf = sb0("nf", [P, 2, PAIR])
        nb = sb0("nb", [P, 2, PAIR])
        df = sb0("df", [P, 2, PAIR])
        db = sb0("db", [P, 2, PAIR])
        raw = sb0("raw", [P, 2, RAWCOLS])
        whi = [sb0(f"whi{i}", [P, RAWCOLS], F32R) for i in range(2)]
        wlo = [sb0(f"wlo{i}", [P, WCOLS], F32R) for i in range(2)]
        sil = sb0("sil", [P, 2, Q4])
        up = sb0("up", [P, Q4])
        hid = sb0("hid", [P, 2, Q4])
        hid_hi = sb0("hid_hi", [P, 2, Q4], F32R)
        hid_lo = sb0("hid_lo", [P, 2, Q4], F32R)
        gate_t = sb0("gate_t", [2 * GATES, N], F32R)
        own0.close()
        own1 = ExitStack()

        def sb1(name, shape, dt=F32):
            return own1.enter_context(nc.sbuf_tensor(name, shape, dt))

        qs = sb1("qs", [P, HEADS // 2, N], F32R)
        negmask = sb1("negmask", [P, P], BF16)
        rowlo = sb1("rowlo", [P, 1])
        prod = sb1("prod", [P, 2, 2 * C])
        kv1 = sb1("kv1", [P, 2, 2, HD])
        kst = sb1("kst", [P, 2, REP, 2, HD], F32R)
        vals = sb1("vals", [P, TILES, HD + 1])
        keys_t = sb1("keys_t", [P, N], F32R)
        nmax = sb1("nmax", [P, 2, HEADS])
        nmx = sb1("nmx", [P, 2, 2, HEADS], F32R)
        nmx_t = sb1("nmx_t", [2 * HEADS, 2, P])
        nmrow = sb1("nmrow", [2, 2, HEADS, P], F32R)
        ones2 = sb1("ones2", [2, P], F32R)
        ones2f = sb1("ones2f", [2, P])
        pt0 = sb1("pt0", [P, 2, HEADS // 2, T])
        pt1 = sb1("pt1", [P, 2, HEADS // 2, P])
        rden = sb1("rden", [P, 2, HEADS])
        yt = sb1("yt", [P, 2, HEADS, HD])
        own1.close()
        own2 = ExitStack()

        def sb2(name, shape, dt=F32):
            return own2.enter_context(nc.sbuf_tensor(name, shape, dt))

        xq = sb2("xq", [P, COLS], FP8)
        y2a = sb2("y2a", [P, 2, Q4], BF16)
        y2b = sb2("y2b", [P, 2, Q4], BF16)
        w3a_hi = sb2("w3a_hi", [P, CH, E3 * H3], F32R)
        w3a_lo = sb2("w3a_lo", [P, CH, E3 * H3], F32R)
        w3b_hi = sb2("w3b_hi", [P, E3, C], F32R)
        w3b_lo = sb2("w3b_lo", [P, E3, C], F32R)
        sel3r = sb2("sel3r", [2 * E3, E3, P])
        sel3 = sb2("sel3", [2 * E3, E3, P], F32R)
        act3 = sb2("act3", [P, 2, Q4])
        hid3 = sb2("hid3", [P, 2, Q4])
        hid3_hi = sb2("hid3_hi", [P, 2, Q4], F32R)
        hid3_lo = sb2("hid3_lo", [P, 2, Q4], F32R)
        gate3_t = sb2("gate3_t", [2 * E3, N], F32R)
        own2.close()
        w3a_raw = f[:, :].rearrange("p (k n) -> p k n", k=CH)
        w3b_raw = mix[:, 0:COLS].rearrange("p (e n) -> p e n", e=E3)

        ctx.enter_context(nc.allow_low_precision(reason="exact splits into float32r parts"))

        d_in = sem("d_in")
        d_small = sem("d_small")
        d_raw = [sem("d_raw0"), sem("d_raw1")]
        d_out = sem("d_out")
        c_tf = sem("c_tf")
        v_tf = sem("v_tf")
        p_id = sem("p_id")
        v_cap = sem("v_cap")
        p_cap = sem("p_cap")
        c_ek = sem("c_ek")
        c_euk = sem("c_euk")
        p_ekv = sem("p_ekv")
        p_dk = sem("p_dk")
        p_den = sem("p_den")
        p_num = sem("p_num")
        p_add = sem("p_add")
        v_dscan = sem("v_dscan")
        v_nscan = sem("v_nscan")
        v_den = sem("v_den")
        v_mix = sem("v_mix")
        c_sig = sem("c_sig")
        v_s = sem("v_s")
        c_shi = sem("c_shi")
        v_slo = sem("v_slo")
        t_rout = sem("t_rout")
        v_r = sem("v_r")
        c_r = sem("c_r")
        t_rtr = sem("t_rtr")
        c_gate = sem("c_gate")
        c_whi = sem("c_whi")
        p_wlo = sem("p_wlo")
        t_g = sem("t_g")
        t_u = sem("t_u")
        t_cb = sem("t_cb")
        t_down = sem("t_down")
        c_sil = sem("c_sil")
        v_up = sem("v_up")
        v_hid = sem("v_hid")
        c_hhi = sem("c_hhi")
        v_hlo = sem("v_hlo")
        v_x = sem("v_x")
        d_w1 = sem("d_w1")
        d_w23 = sem("d_w23")
        d_w3 = sem("d_w3")
        c_w1 = sem("c_w1")
        p_w1 = sem("p_w1")
        p_const = sem("p_const")
        v_const = sem("v_const")
        t_q = sem("t_q")
        t_kv = sem("t_kv")
        c_q = sem("c_q")
        v_q = sem("v_q")
        v_kv = sem("v_kv")
        v_k1 = sem("v_k1")
        v_kst = sem("v_kst")
        v_val = sem("v_val")
        t_kt = sem("t_kt")
        c_kt = sem("c_kt")
        t_a = sem("t_a")
        v_nmax = sem("v_nmax")
        v_nmx = sem("v_nmx")
        t_nmx = sem("t_nmx")
        c_nmx = sem("c_nmx")
        d_nmx = sem("d_nmx")
        t_b = sem("t_b")
        c_p = sem("c_p")
        p_sel = sem("p_sel")
        t_pv = sem("t_pv")
        v_rden = sem("v_rden")
        v_y = sem("v_y")
        t_yt = sem("t_yt")
        v_peak = sem("v_peak")
        p_peak = sem("p_peak")
        v_xq = sem("v_xq")
        v_wq2 = sem("v_wq2")
        t_l2 = sem("t_l2")
        c_y2 = sem("c_y2")
        c_y2b = sem("c_y2b")
        c_w3 = sem("c_w3")
        p_w3 = sem("p_w3")
        t_h3 = sem("t_h3")
        t_cb3 = sem("t_cb3")
        c_act3 = sem("c_act3")
        v_h3 = sem("v_h3")
        c_h3 = sem("c_h3")
        v_h3lo = sem("v_h3lo")
        t_d3 = sem("t_d3")

        block = ctx.enter_context(nc.Block())
        HALF_IT = CHUNKS // 2


        def seq(buf, col, n=T):
            return buf[:, bass.ds(col, n)] if not isinstance(col, int) else buf[:, col:col + n]

        def mixed(l, col, n):
            return mix[:, bass.ds(l * COLS + col, n)]

        def scans(v, l, p, st, den):
            src, fw, bw, done = (ek, df, db, v_dscan) if den else (ekv, nf, nb, v_nscan)
            for j in range(2):
                d = decay_c[:, bass.ds(l * HB + p * 2 + j, 1)].to_broadcast([P, T])
                data = src[:, p * PAIR + j * T:p * PAIR + (j + 1) * T]
                v.tensor_tensor_scan(out=fw[:, st, j * T:(j + 1) * T], data0=d, data1=data,
                                     initial=0.0, op0=ALU.mult, op1=ALU.add).then_inc(done, 1)
                rev = slice((j + 1) * T - 1, j * T - 1 if j else None, -1)
                v.tensor_tensor_scan(out=bw[:, st, rev], data0=d, data1=data[:, ::-1],
                                     initial=0.0, op0=ALU.mult, op1=ALU.add).then_inc(done, 1)

        def finish_den(v, st, part, k):
            cut = slice(part * T, (part + 1) * T)
            v.tensor_scalar(out=df[:, st, cut], in0=df[:, st, cut], scalar1=1e-8, scalar2=None,
                            op0=ALU.max).then_inc(v_den, 1)
            v.wait_ge(v_den, k * 4 + part * 2 + 1)
            v.reciprocal(df[:, st, cut], df[:, st, cut]).then_inc(v_den, 1)

        def finish_mix(v, l, p, st, k):
            for j in range(2):
                cut = slice(j * T, (j + 1) * T)
                v.scalar_tensor_tensor(out=mixed(l, p * PAIR + j * T, T), in0=nf[:, st, cut],
                                       scalar=tmul_c[:, p * 2 + j:p * 2 + j + 1], in1=df[:, st, cut],
                                       op0=ALU.mult, op1=ALU.mult).then_inc(v_mix, 1)

        def pool_dk(g, l, p, st):
            cols = slice(p * PAIR, (p + 1) * PAIR)
            g.tensor_tensor(out=dk[:, st, :], in0=mixed(l, p * PAIR, PAIR), in1=ek[:, cols], op=ALU.subtract).then_inc(p_dk, 1)

        def pool_dkv(g, p, st, k):
            g.wait_ge(p_dk, 2 * k + 1)
            g.tensor_tensor(out=dkv[:, st, :], in0=dk[:, st, :], in1=f[:, p * PAIR:(p + 1) * PAIR],
                            op=ALU.mult).then_inc(p_dk, 1)

        def pool_den(g, st, k):
            g.wait_ge(v_dscan, 4 * (k + 1))
            g.tensor_tensor(out=df[:, st, :], in0=df[:, st, :], in1=db[:, st, :], op=ALU.add).then_inc(p_add, 1)
            g.wait_ge(p_add, 2 * k + 1)
            g.tensor_tensor(out=df[:, st, :], in0=df[:, st, :], in1=dk[:, st, :], op=ALU.add).then_inc(p_den, 1)

        def pool_num(g, st, k):
            g.wait_ge(v_nscan, 4 * (k + 1))
            g.tensor_tensor(out=nf[:, st, :], in0=nf[:, st, :], in1=nb[:, st, :], op=ALU.add).then_inc(p_add, 1)
            g.wait_ge(p_add, 2 * k + 2)
            g.tensor_tensor(out=nf[:, st, :], in0=nf[:, st, :], in1=dkv[:, st, :], op=ALU.add).then_inc(p_num, 1)

        def cond_act(c, l):
            for q in range(4):
                cut = slice(q * Q4, (q + 1) * Q4)
                n = 4 * l + q
                if l == 0:
                    c.wait_ge(d_in, 48)
                elif l == 1:
                    c.wait_ge(v_x, q + 1)
                elif l == 2:
                    c.wait_ge(v_x, 4 + TILES)
                else:
                    c.wait_ge(v_x, 4 + TILES + q + 1)
                at_least(c, v_s, n)
                c.activation(sig[:, :], x[:, cut], ACT.Sigmoid).then_inc(c_sig, 1)
                c.wait_ge(v_s, n + 1)
                if l == 2:
                    continue
                c.activation(s_hi[:, cut], s[:, cut], ACT.Copy).then_inc(c_shi, 1)

        R0 = 33
        R3 = R0 + 9
        ALIST = [[(r, m, nm) for m in range(0, 8, nm) for r in range(2)] for nm in (4, 2)]
        AGROUPS = sum(len(x) for x in ALIST)
        BLIST = [(kc, r, m, nm) for kc, nm in ((0, 2), (1, 4)) for m in range(0, 8, nm) for r in range(2)]
        BGROUPS = len(BLIST)

        def cond_dve(v, l):
            for q in range(4):
                cut = slice(q * Q4, (q + 1) * Q4)
                n = 4 * l + q
                v.wait_ge(c_sig, n + 1)
                v.wait_ge(v_mix, 8 * l + 2 * q + 2)
                if l == 3:
                    v.wait_ge(v_xq, 4)
                v.tensor_tensor(out=s[:, cut], in0=sig[:, :], in1=mixed(l, cut.start, Q4), op=ALU.mult).then_inc(v_s, 1)
                if l == 2:
                    v.wait_ge(v_s, n + 1)
                    v.tensor_reduce(out=peak[:, q:q + 1], in_=s[:, cut], op=ALU.max, axis=AX.X,
                                    apply_absolute_value=True).then_inc(v_peak, 1)
                    continue
                v.wait_ge(c_shi, 4 * min(l, 2) + q + 1)
                v.tensor_tensor(out=s_lo[:, cut], in0=s[:, cut], in1=s_hi[:, cut].bitcast(F32), op=ALU.subtract).then_inc(v_slo, 1)

        @block.sync
        def _(sp):
            sp.dma_start(f[:, :], a["fT"].rearrange("(h p) t -> p h t", p=P)).then_inc(d_in, 16)
            sp.dma_start(x[:, :], a["xT"].rearrange("(h p) t -> p h t", p=P)).then_inc(d_in, 16)
            sp.dma_start(rw[:, :, :], a["router"].rearrange("(k p) e -> p k e", p=P)).then_inc(d_in, 16)
            for c in range(2):
                sp.dma_start(raw[:, c, :], a["w0"][c, :, :]).then_inc(d_raw[c], 16)
            sp.dma_start(w1raw[:, :, :], a["w1"].rearrange("(k p) n -> p k n", p=P)).then_inc(d_w1, 16)
            sp.dma_start(wg1[:, :, :], a["wg1"].rearrange("(k p) n -> p k n", p=P)).then_inc(d_w1, 16)
            sp.dma_start(w2in[:, :, :], a["w2"].rearrange("(k p) n -> p k n", p=P)).then_inc(d_w23, 16)
            sp.dma_start(b2in[:, :], a["b2"]).then_inc(d_w23, 16)
            sp.dma_start(wg3[:, :, :], a["wg3"].rearrange("(k p) n -> p k n", p=P)).then_inc(d_w23, 16)
            with sp.Fori(0, HALF_IT - 1) as i:
                for c in range(2):
                    sp.wait_ge(c_whi, 2 * i + c + 1)
                    sp.wait_ge(p_wlo, 2 * i + c + 1)
                    sp.dma_start(raw[:, c, :], a["w0"][bass.ds(2 * i + 2 + c, 1), :, :].rearrange("o p n -> (o p) n")).then_inc(d_raw[c], 16)
            sp.wait_ge(v_x, 4)
            sp.dma_start(w3a_raw, a["w3a"].rearrange("(k p) n -> p k n", p=P)).then_inc(d_w3, 16)
            sp.dma_start(w3b_raw, a["w3b"].rearrange("e p n -> p e n")).then_inc(d_w3, 16)
            for t in range(TILES):
                sp.wait_ge(c_nmx, t + 1)
                at_least(sp, t_b, BGROUPS * (t // 2))
                for part in range(2):
                    sp.dma_start(nmrow[part:part + 1, t % 2, :, :].bitcast(F32),
                                 nmx_t[part * HEADS:(part + 1) * HEADS, t % 2, :]).then_inc(d_nmx, 16)
            sp.wait_ge(v_x, 4 + TILES)
            sp.dma_start(sel3r[:, :, :], a["sel3"]).then_inc(d_w3, 16)
            for q in range(4):
                sp.wait_ge(v_x, 4 + TILES + 4 + q + 1)
                h, th = q // 2, q % 2
                sp.dma_start(out[h * P:(h + 1) * P, th * Q4:(th + 1) * Q4], x[:, q * Q4:(q + 1) * Q4]).then_inc(d_out, 16)
            sp.wait_ge(d_out, 64)

        @block.scalar
        def _(c):
            c.dma_start(temb[:, :, :], a["temb"].rearrange("(o b) t -> o b t", o=1).to_broadcast([P, B, TE])).then_inc(d_small, 16)
            c.dma_start(wcol[:, :, :], a["w"]).then_inc(d_small, 16)
            c.dma_start(ucol[:, :, :], a["u"]).then_inc(d_small, 16)
            c.wait_ge(v_tf, 1)
            c.activation(tf[:, :], tsum[:, :], ACT.Sigmoid).then_inc(c_tf, 1)
            c.activation(wexp[:, :, :], wcol[:, :, :], ACT.Exp).then_inc(c_tf, 1)
            c.wait_ge(c_tf, 2)
            c.activation(wdec[:, :, :], wexp[:, :, :], ACT.Exp, scale=-1.0).then_inc(c_tf, 1)
            c.wait_ge(v_cap, 1)
            for p in range(2):
                cut = slice(p * N, (p + 1) * N)
                c.activation(ek[:, cut], ek[:, cut], ACT.Exp).then_inc(c_ek, 1)
                c.wait_ge(v_cap, 2 + p)
                c.activation(mix[:, cut], mix[:, cut], ACT.Exp).then_inc(c_euk, 1)
            for l in range(1, LAYERS):
                c.wait_ge(p_cap, 2 * l)
                c.activation(mixed(l, 0, COLS), mixed(l, 0, COLS), ACT.Exp).then_inc(c_euk, 1)
            cond_act(c, 0)
            c.wait_ge(v_r, 2)
            c.activation(prob[:, :, 0:E0], prob[:, :, 0:E0], ACT.Exp).then_inc(c_r, 1)
            c.wait_ge(t_rout, 1)
            c.activation(rsg[:, :], bank[7][:, :].rearrange("p (t e) -> p t e", t=TILES)[:, :, E0], ACT.Exp, scale=-1.0).then_inc(c_r, 1)
            for j in range(2):
                c.wait_ge(t_rtr, j + 1)
                c.activation(gate_t[:, j * Q4:(j + 1) * Q4], bank[4 + j][0:2 * GATES, :], ACT.Copy).then_inc(c_gate, 1)
            c.wait_ge(d_raw[0], 16)
            c.activation(whi[0][:, :], raw[:, 0, :], ACT.Copy).then_inc(c_whi, 1)

            def body(i, first, last):
                for n in range(4):
                    ch, hf = n // 2, n % 2
                    c.wait_ge(t_g, 4 * i + n + 1)
                    at_least(c, v_up, 4 * i + n - 1)
                    c.activation(sil[:, hf, :], bank[4][:, :], ACT.Silu).then_inc(c_sil, 1)
                    if hf == 1 and not (last and ch == 1):
                        at_least(c, t_down, 4 * i + 2 * ch)
                        c.wait_ge(d_raw[1 - ch], 16 * (i + 1 + ch))
                        c.activation(whi[1 - ch][:, :], raw[:, 1 - ch, :], ACT.Copy).then_inc(c_whi, 1)
                    c.wait_ge(v_hid, 4 * i + n + 1)
                    at_least(c, t_down, 4 * i + n - 1)
                    c.activation(hid_hi[:, hf, :], hid[:, hf, :], ACT.Copy).then_inc(c_hhi, 1)

            body(0, True, False)
            with c.Fori(1, HALF_IT - 1) as i:
                body(i, False, False)
            body(HALF_IT - 1, False, True)

            c.wait_ge(d_w1, 32)
            for k in range(CH):
                c.activation(wq_hi[:, k, :].rearrange("p (h r d) -> p h r d", h=HEADS, r=REP),
                             w1raw[:, k, 0:C].rearrange("p (h d) -> p h d", h=HEADS).unsqueeze(2).to_broadcast([P, HEADS, REP, HD]),
                             ACT.Copy).then_inc(c_w1, 1)
            c.activation(wkv_hi[:, :, :], w1raw[:, :, C:3 * C], ACT.Copy).then_inc(c_w1, 1)
            cond_act(c, 1)
            c.wait_ge(v_r, R0 + 2)
            c.activation(prob[:, :, 0:HEADS], prob[:, :, 0:HEADS], ACT.Exp).then_inc(c_r, 1)
            for j in range(2):
                for m in range(HEADS // 2):
                    n = j * 8 + m
                    c.wait_ge(t_q, n + 1)
                    c.activation(qs[:, m, j * Q4:(j + 1) * Q4], bank[2 + n % 2][:, :], ACT.Copy).then_inc(c_q, 1)
                for t in (range(3) if j == 0 else range(3, TILES)):
                    c.wait_ge(t_kt, t + 1)
                    c.activation(keys_t[:, t * P:(t + 1) * P], bank[6 + t % 2][:, 0:P], ACT.Copy).then_inc(c_kt, 1)

            def maxima(t):
                c.wait_ge(t_nmx, t + 1)
                at_least(c, d_nmx, 32 * (t - 1))
                c.activation(nmx_t[:, t % 2, :], bank[6][0:2 * HEADS, 0:P], ACT.Copy).then_inc(c_nmx, 1)

            maxima(0)
            maxima(1)
            for b in range(B):
                at_least(c, t_pv, 2 * b)
                for gi, (kc, r, m, nm) in enumerate(BLIST):
                    if gi == 6 and b + 1 < B:
                        maxima(2 * b + 2)
                    if gi == 9 and b + 1 < B:
                        maxima(2 * b + 3)
                    c.wait_ge(t_b, BGROUPS * b + gi + 1)
                    dst = (pt0 if kc == 0 else pt1)[:, r, m:m + nm, :].rearrange("p m q -> p (m q)")
                    c.activation(dst, bank[2 + gi % 2][:, :], ACT.Exp, scale=HD ** -0.5).then_inc(c_p, 1)
            cond_act(c, 2)
            c.wait_ge(d_w3, 48)
            c.activation(w3a_hi[:, :, :], w3a_raw, ACT.Copy).then_inc(c_w3, 1)
            c.activation(w3b_hi[:, :, :], w3b_raw, ACT.Copy).then_inc(c_w3, 1)
            c.activation(sel3[:, :, :], sel3r[:, :, :], ACT.Copy).then_inc(c_w3, 1)
            for q in range(4):
                c.wait_ge(t_l2, q + 1)
                at_least(c, v_x, 4 + TILES + q - 1)
                c.activation(y2a[:, q % 2, :], bank[q][:, :], ACT.Copy, scale=scale2[:, 0:1]).then_inc(c_y2, 1)
                c.wait_ge(c_y2, q + 1)
                c.activation(y2b[:, q % 2, :], y2a[:, q % 2, :], ACT.Identity, bias=b2[:, q // 2:q // 2 + 1]).then_inc(c_y2b, 1)
            cond_act(c, 3)
            c.wait_ge(v_r, R3 + 3)
            c.activation(prob[:, :, 0:E3], prob[:, :, 0:E3], ACT.Exp).then_inc(c_r, 1)
            for j in range(2):
                c.wait_ge(t_rtr, 2 + j + 1)
                c.activation(gate3_t[:, j * Q4:(j + 1) * Q4], bank[4 + j][0:2 * E3, :], ACT.Copy).then_inc(c_gate, 1)
            for n in range(2 * E3):
                c.wait_ge(t_h3, n + 1)
                at_least(c, v_h3, n - 1)
                c.activation(act3[:, n % 2, :], bank[4 + n % 2][:, :], ACT.Relu).then_inc(c_act3, 1)
                c.wait_ge(v_h3, n + 1)
                at_least(c, t_d3, n - 1)
                c.activation(hid3_hi[:, n % 2, :], hid3[:, n % 2, :], ACT.Copy).then_inc(c_h3, 1)

        @block.vector
        def _(v):
            v.wait_ge(d_small, 48)
            v.tensor_reduce(out=tsum[:, :], in_=temb[:, :, :], op=ALU.add, axis=AX.X).then_inc(v_tf, 1)
            v.wait_ge(d_in, 48)
            v.tensor_scalar(out=ek[:, :], in0=f[:, :], scalar1=CAP, scalar2=None, op0=ALU.min).then_inc(v_cap, 1)
            for h in range(CH):
                cut = slice(h * N, (h + 1) * N)
                v.tensor_scalar(out=mix[:, cut], in0=f[:, cut], scalar1=ucol[:, 0, h:h + 1], scalar2=CAP,
                                op0=ALU.add, op1=ALU.min).then_inc(v_cap, 1)
            v.wait_ge(c_tf, 1)
            v.tensor_scalar(out=tdecay[:, :], in0=tf[:, :], scalar1=0.5, scalar2=0.5, op0=ALU.mult, op1=ALU.add).then_inc(v_tf, 1)
            for h in range(CH):
                v.tensor_scalar(out=tmul[:, h, :], in0=tf[:, :], scalar1=0.2, scalar2=0.8, op0=ALU.mult, op1=ALU.add).then_inc(v_tf, 1)
            v.wait_ge(c_tf, 3)
            v.wait_ge(v_tf, 4)
            for b in range(B):
                v.tensor_scalar(out=decay[:, :, :, b], in0=wdec[:, :, :], scalar1=tdecay[:, b:b + 1], scalar2=None,
                                op0=ALU.mult).then_inc(v_tf, 1)
            v.wait_ge(v_tf, 8)
            for k in range(PAIRS + 1):
                if k < PAIRS:
                    if k % 2 == 0:
                        v.wait_ge(c_ek, k // 2 + 1)
                    if k >= 2:
                        v.wait_ge(v_mix, 2 * (k - 1))
                    scans(v, 0, k, k % 2, True)
                    if k % 2 == 0:
                        v.wait_ge(p_ekv, k // 2 + 1)
                    scans(v, 0, k, k % 2, False)
                if k >= 1:
                    v.wait_ge(p_den, k)
                    finish_den(v, (k - 1) % 2, 0, k - 1)
                    finish_den(v, (k - 1) % 2, 1, k - 1)
                    v.wait_ge(v_den, 4 * k)
                    v.wait_ge(p_num, k)
                    finish_mix(v, 0, k - 1, (k - 1) % 2, k - 1)
            cond_dve(v, 0)
            v.wait_ge(t_rout, 1)
            lg = bank[7][:, :].rearrange("p (t e) -> p t e", t=TILES)[:, :, 0:E0]
            v.tensor_reduce(out=rmax[:, :], in_=lg, op=ALU.max, axis=AX.X).then_inc(v_r, 1)
            v.wait_ge(v_r, 1)
            v.tensor_tensor(out=prob[:, :, 0:E0], in0=lg, in1=rmax[:, :].unsqueeze(2).to_broadcast([P, TILES, E0]),
                            op=ALU.subtract).then_inc(v_r, 1)
            v.memset(prob[:, :, E0:EP], -1.0).then_inc(v_r, 1)
            v.wait_ge(c_r, 1)
            v.tensor_reduce(out=rsum[:, :], in_=prob[:, :, 0:E0], op=ALU.add, axis=AX.X).then_inc(v_r, 1)
            v.wait_ge(v_r, 4)
            v.reciprocal(rsum[:, :], rsum[:, :]).then_inc(v_r, 1)
            v.wait_ge(v_r, 5)
            v.tensor_tensor(out=prob[:, :, 0:E0], in0=prob[:, :, 0:E0],
                            in1=rsum[:, :].unsqueeze(2).to_broadcast([P, TILES, E0]), op=ALU.mult).then_inc(v_r, 1)
            v.wait_ge(v_r, 6)
            W = E0 + 8 - K0
            for t in range(TILES):
                v.max(out=top8[:, t, :], in_=prob[:, t, 0:W]).then_inc(v_r, 1)
            v.wait_ge(v_r, 14)
            v.memset(top8[:, :, K0:8], -1.0).then_inc(v_r, 1)
            v.wait_ge(v_r, 15)
            for t in range(TILES):
                v.match_replace(out=repl[:, t, 0:W], in_to_replace=top8[:, t, :], in_values=prob[:, t, 0:W],
                                imm_value=-2.0).then_inc(v_r, 1)
            v.tensor_reduce(out=rsum[:, :], in_=top8[:, :, 0:K0], op=ALU.add, axis=AX.X).then_inc(v_r, 1)
            v.wait_ge(v_r, 24)
            v.tensor_scalar(out=rsum[:, :], in0=rsum[:, :], scalar1=1e-9, scalar2=None, op0=ALU.max).then_inc(v_r, 1)
            v.tensor_tensor(out=repl[:, :, 0:E0], in0=repl[:, :, 0:E0], in1=prob[:, :, 0:E0], op=ALU.not_equal).then_inc(v_r, 1)
            v.wait_ge(v_r, 26)
            v.reciprocal(rsum[:, :], rsum[:, :]).then_inc(v_r, 1)
            v.tensor_tensor(out=prob[:, :, 0:E0], in0=prob[:, :, 0:E0], in1=repl[:, :, 0:E0], op=ALU.mult).then_inc(v_r, 1)
            v.wait_ge(c_r, 2)
            v.tensor_scalar(out=rsg[:, :], in0=rsg[:, :], scalar1=1.0, scalar2=None, op0=ALU.add).then_inc(v_r, 1)
            v.wait_ge(v_r, 29)
            v.tensor_tensor(out=gates[:, :, 0:E0], in0=prob[:, :, 0:E0],
                            in1=rsum[:, :].unsqueeze(2).to_broadcast([P, TILES, E0]), op=ALU.mult).then_inc(v_r, 1)
            v.reciprocal(gates[:, :, E0], rsg[:, :]).then_inc(v_r, 1)
            v.wait_ge(v_r, 31)
            v.tensor_copy(gsplit[:, :, 0, :], gates[:, :, :]).then_inc(v_r, 1)
            v.wait_ge(v_r, 32)
            v.tensor_tensor(out=gsplit[:, :, 1, :], in0=gates[:, :, :], in1=gsplit[:, :, 0, :].bitcast(F32),
                            op=ALU.subtract).then_inc(v_r, 1)

            def body(i, wkv):
                for n in range(4):
                    ch, hf = n // 2, n % 2
                    v.wait_ge(t_u, 4 * i + n + 1)
                    v.wait_ge(c_sil, 4 * i + n + 1)
                    v.tensor_tensor(out=up[:, :], in0=bank[5][:, :], in1=sil[:, hf, :], op=ALU.mult).then_inc(v_up, 1)
                    v.wait_ge(t_cb, 4 * i + n + 1)
                    v.wait_ge(v_up, 4 * i + n + 1)
                    v.tensor_tensor(out=hid[:, hf, :], in0=bank[6][:, :], in1=up[:, :], op=ALU.mult).then_inc(v_hid, 1)
                    if wkv:
                        l, p, k = wkv
                        if n == 0:
                            scans(v, l, p, 0, True)
                        elif n == 1:
                            scans(v, l, p, 0, False)
                        elif n == 2:
                            v.wait_ge(p_den, k + 1)
                            finish_den(v, 0, 0, k)
                        else:
                            finish_den(v, 0, 1, k)
                            v.wait_ge(v_den, 4 * (k + 1))
                            v.wait_ge(p_num, k + 1)
                            finish_mix(v, l, p, 0, k)
                    v.wait_ge(c_hhi, 4 * i + n + 1)
                    at_least(v, t_down, 4 * i + n - 1)
                    v.tensor_tensor(out=hid_lo[:, hf, :], in0=hid[:, hf, :], in1=hid_hi[:, hf, :].bitcast(F32),
                                    op=ALU.subtract).then_inc(v_hlo, 1)

            body(0, None)
            with v.Fori(1, LAYERS) as l:
                for p in range(PAIRS):
                    body(PAIRS * l + p + 1 - PAIRS, (l, p, PAIRS * l + p))
            for i in range(1 + PAIRS * (LAYERS - 1), HALF_IT):
                body(i, None)
            v.wait_ge(t_down, 4 * HALF_IT)
            for q in range(4):
                cut = slice(q * Q4, (q + 1) * Q4)
                v.tensor_tensor(out=x[:, cut], in0=bank[q][:, :], in1=x[:, cut], op=ALU.add).then_inc(v_x, 1)

            cond_dve(v, 1)
            v.wait_ge(t_rout, 2)
            lg = bank[4][:, :].rearrange("p (t e) -> p t e", t=TILES)[:, :, 0:HEADS]
            v.tensor_reduce(out=rmax[:, :], in_=lg, op=ALU.max, axis=AX.X).then_inc(v_r, 1)
            v.wait_ge(v_r, R0 + 1)
            v.tensor_tensor(out=prob[:, :, 0:HEADS], in0=lg, in1=rmax[:, :].unsqueeze(2).to_broadcast([P, TILES, HEADS]),
                            op=ALU.subtract).then_inc(v_r, 1)
            v.memset(prob[:, :, HEADS:HEADS + 8], -1.0).then_inc(v_r, 1)
            v.wait_ge(c_r, 3)
            v.tensor_reduce(out=rsum[:, :], in_=prob[:, :, 0:HEADS], op=ALU.add, axis=AX.X).then_inc(v_r, 1)
            v.wait_ge(v_r, R0 + 4)
            v.reciprocal(rsum[:, :], rsum[:, :]).then_inc(v_r, 1)
            v.wait_ge(v_r, R0 + 5)
            v.tensor_tensor(out=prob[:, :, 0:HEADS], in0=prob[:, :, 0:HEADS],
                            in1=rsum[:, :].unsqueeze(2).to_broadcast([P, TILES, HEADS]), op=ALU.mult).then_inc(v_r, 1)
            v.wait_ge(v_r, R0 + 6)
            v.tensor_reduce(out=rmax[:, :], in_=prob[:, :, 0:HEADS], op=ALU.max, axis=AX.X).then_inc(v_r, 1)
            v.memset(top8[:, :, 1:8], -1.0).then_inc(v_r, 1)
            v.wait_ge(v_r, R0 + 8)
            v.tensor_copy(top8[:, :, 0], rmax[:, :]).then_inc(v_r, 1)
            v.wait_ge(v_r, R0 + 9)
            for t in range(TILES):
                v.match_replace(out=repl[:, t, 0:HEADS + 7], in_to_replace=top8[:, t, :],
                                in_values=prob[:, t, 0:HEADS + 7], imm_value=-2.0).then_inc(v_k1, 1)
            v.wait_ge(v_k1, TILES)
            v.tensor_tensor(out=repl[:, :, 0:HEADS], in0=repl[:, :, 0:HEADS], in1=prob[:, :, 0:HEADS],
                            op=ALU.not_equal).then_inc(v_k1, 1)
            v.memset(vals[:, :, :], 1.0).then_inc(v_const, 1)
            v.wait_ge(v_k1, TILES + 1)
            v.wait_ge(v_const, 1)
            v.wait_ge(p_const, 4)
            for j in range(2):
                for m in range(HEADS // 2):
                    n = j * 8 + m
                    cut = slice(j * Q4, (j + 1) * Q4)
                    v.wait_ge(c_q, n + 1)
                    v.scalar_tensor_tensor(out=qs[:, m, cut], in0=qs[:, m, cut].bitcast(F32), scalar=rowlo[:, 0:1],
                                           in1=bank[2 + n % 2][:, :], op0=ALU.mult, op1=ALU.add).then_inc(v_q, 1)
                for t in range(4 * j, 4 * j + 4):
                    u = t % 2
                    v.wait_ge(t_kv, t + 1)
                    v.tensor_tensor(out=prod[:, u, :].rearrange("p (a h d) -> p a h d", a=2, h=HEADS),
                                    in0=bank[u][:, :].rearrange("p (a h d) -> p a h d", a=2, h=HEADS),
                                    in1=repl[:, t, 0:HEADS].unsqueeze(1).unsqueeze(3).to_broadcast([P, 2, HEADS, HD]),
                                    op=ALU.mult).then_inc(v_kv, 1)
                    v.wait_ge(v_kv, t + 1)
                    v.tensor_reduce(out=kv1[:, u, :, :], in_=prod[:, u, :].rearrange("p (a h d) -> p a d h", a=2, h=HEADS),
                                    op=ALU.add, axis=AX.X).then_inc(v_k1, 1)
                    v.wait_ge(v_k1, TILES + 2 + t)
                    at_least(v, t_kt, t - 1)
                    key = kv1[:, u, 0, :].unsqueeze(1).to_broadcast([P, REP, HD])
                    v.tensor_copy(kst[:, u, :, 0, :], key).then_inc(v_kst, 1)
                    v.tensor_scalar(out=vals[:, t, 0:HD], in0=kv1[:, u, 1, :], scalar1=rmax[:, t:t + 1], scalar2=None,
                                    op0=ALU.mult).then_inc(v_val, 1)
                    v.wait_ge(v_kst, 2 * t + 1)
                    v.tensor_tensor(out=kst[:, u, :, 1, :], in0=key, in1=kst[:, u, :, 0, :].bitcast(F32),
                                    op=ALU.subtract).then_inc(v_kst, 1)

            def row_maxima(t, ga):
                for r, m, nm in ALIST[t % 2]:
                    v.wait_ge(t_a, ga + 1)
                    v.tensor_reduce(out=nmax[:, t % 2, 2 * m + r:2 * (m + nm - 1) + r + 1:2],
                                    in_=bank[4 + r][:, :].rearrange("p (m k) -> p m k", m=nm),
                                    op=ALU.max, axis=AX.X, negate=True).then_inc(v_nmax, 1)
                    ga += 1
                v.wait_ge(v_nmax, ga)
                at_least(v, t_nmx, t - 1)
                v.tensor_copy(nmx[:, t % 2, 0, :], nmax[:, t % 2, :]).then_inc(v_nmx, 1)
                v.wait_ge(v_nmx, 2 * t + 1)
                v.tensor_tensor(out=nmx[:, t % 2, 1, :], in0=nmax[:, t % 2, :], in1=nmx[:, t % 2, 0, :].bitcast(F32),
                                op=ALU.subtract).then_inc(v_nmx, 1)
                return ga

            ga = 0
            for t in range(2):
                ga = row_maxima(t, ga)
            for b in range(B):
                if b + 1 < B:
                    for t in range(2 * b + 2, 2 * b + 4):
                        ga = row_maxima(t, ga)
                for t in range(2 * b, 2 * b + 2):
                    acc = bank[t % 2][:, :].rearrange("p (h d) -> p h d", h=HEADS)
                    v.wait_ge(t_pv, t + 1)
                    v.reciprocal(rden[:, t % 2, :], acc[:, :, HD]).then_inc(v_rden, 1)
                    v.wait_ge(v_rden, t + 1)
                    v.tensor_tensor(out=yt[:, t % 2, :, :], in0=acc[:, :, 0:HD],
                                    in1=rden[:, t % 2, :].unsqueeze(2).to_broadcast([P, HEADS, HD]), op=ALU.mult).then_inc(v_y, 1)
                v.wait_ge(t_yt, 2 * b + 2)
                for t in range(2 * b, 2 * b + 2):
                    xt = x[:, :].rearrange("p (h n) -> p h n", h=CH)[:, :, t * P:(t + 1) * P]
                    v.tensor_tensor(out=xt, in0=bank[7][:, (t % 2) * C:(t % 2 + 1) * C].rearrange("p (h n) -> p h n", h=CH),
                                    in1=xt, op=ALU.add).then_inc(v_x, 1)

            v.wait_ge(d_w23, 48)
            for k in range(CH):
                v.tensor_reduce(out=peak[:, 4 + k:5 + k], in_=w2in[:, k, :], op=ALU.max, axis=AX.X,
                                apply_absolute_value=True).then_inc(v_peak, 1)
            v.tensor_copy(b2[:, :], b2in[:, :]).then_inc(v_wq2, 1)
            cond_dve(v, 2)
            v.wait_ge(v_peak, 6)
            v.tensor_reduce(out=peak2[:, 0:1], in_=peak[:, 0:4], op=ALU.max, axis=AX.X).then_inc(v_peak, 1)
            v.tensor_reduce(out=peak2[:, 1:2], in_=peak[:, 4:6], op=ALU.max, axis=AX.X).then_inc(v_peak, 1)
            v.wait_ge(p_peak, 1)
            v.tensor_scalar(out=peakall[:, :], in0=peakall[:, :], scalar1=1e-6, scalar2=None, op0=ALU.max).then_inc(v_peak, 1)
            v.wait_ge(v_peak, 9)
            v.reciprocal(peakinv[:, :], peakall[:, :]).then_inc(v_peak, 1)
            v.tensor_tensor(out=scale2[:, :], in0=peakall[:, 0:1], in1=peakall[:, 1:2], op=ALU.mult).then_inc(v_peak, 1)
            v.wait_ge(v_peak, 11)
            v.tensor_scalar(out=w2q[:, :, :], in0=w2in[:, :, :], scalar1=peakinv[:, 1:2], scalar2=None,
                            op0=ALU.mult, saturate=False).then_inc(v_wq2, 1)
            for q in range(4):
                cut = slice(q * Q4, (q + 1) * Q4)
                v.tensor_scalar(out=xq[:, cut], in0=s[:, cut], scalar1=peakinv[:, 0:1], scalar2=None,
                                op0=ALU.mult, saturate=False).then_inc(v_xq, 1)
            for q in range(4):
                cut = slice(q * Q4, (q + 1) * Q4)
                v.wait_ge(c_y2b, q + 1)
                v.tensor_tensor(out=x[:, cut], in0=x[:, cut], in1=y2b[:, q % 2, :], op=ALU.add).then_inc(v_x, 1)

            cond_dve(v, 3)
            v.memset(prob[:, :, E3:E3 + 4], LOW).then_inc(v_r, 1)
            v.wait_ge(t_rout, 3)
            lg = bank[7][:, :].rearrange("p (t e) -> p t e", t=TILES)[:, :, 0:E3]
            v.tensor_copy(prob[:, :, 0:E3], lg).then_inc(v_r, 1)
            v.wait_ge(v_r, R3 + 2)
            for t in range(TILES):
                v.max(out=top8[:, t, :], in_=prob[:, t, 0:E3 + 4]).then_inc(v_k1, 1)
            v.wait_ge(v_k1, 2 * TILES + 1 + TILES)
            v.tensor_copy(rmax[:, :], top8[:, :, 0]).then_inc(v_k1, 1)
            v.memset(top8[:, :, K3:8], LOW).then_inc(v_k1, 1)
            v.wait_ge(v_k1, 3 * TILES + 3)
            for t in range(TILES):
                v.match_replace(out=repl[:, t, 0:E3 + 4], in_to_replace=top8[:, t, :],
                                in_values=prob[:, t, 0:E3 + 4], imm_value=1.1 * LOW).then_inc(v_k1, 1)
            v.wait_ge(v_k1, 4 * TILES + 3)
            v.tensor_tensor(out=repl[:, :, 0:E3], in0=repl[:, :, 0:E3], in1=prob[:, :, 0:E3], op=ALU.not_equal).then_inc(v_k1, 1)
            v.wait_ge(v_k1, 4 * TILES + 4)
            v.tensor_tensor(out=prob[:, :, 0:E3], in0=prob[:, :, 0:E3],
                            in1=rmax[:, :].unsqueeze(2).to_broadcast([P, TILES, E3]), op=ALU.subtract).then_inc(v_r, 1)
            v.wait_ge(c_r, 4)
            v.tensor_tensor(out=prob[:, :, 0:E3], in0=prob[:, :, 0:E3], in1=repl[:, :, 0:E3], op=ALU.mult).then_inc(v_r, 1)
            v.wait_ge(v_r, R3 + 4)
            v.tensor_reduce(out=rsum[:, :], in_=prob[:, :, 0:E3], op=ALU.add, axis=AX.X).then_inc(v_r, 1)
            v.wait_ge(v_r, R3 + 5)
            v.reciprocal(rsum[:, :], rsum[:, :]).then_inc(v_r, 1)
            v.wait_ge(v_r, R3 + 6)
            v.tensor_tensor(out=prob[:, :, 0:E3], in0=prob[:, :, 0:E3],
                            in1=rsum[:, :].unsqueeze(2).to_broadcast([P, TILES, E3]), op=ALU.mult).then_inc(v_r, 1)
            v.wait_ge(v_r, R3 + 7)
            v.tensor_scalar(out=gates[:, :, 0:E3], in0=prob[:, :, 0:E3], scalar1=1.0, scalar2=None, op0=ALU.add).then_inc(v_r, 1)
            v.wait_ge(v_r, R3 + 8)
            v.tensor_tensor(out=gates[:, :, 0:E3], in0=gates[:, :, 0:E3], in1=prob[:, :, 0:E3], op=ALU.subtract).then_inc(v_r, 1)
            v.wait_ge(v_r, R3 + 9)
            v.tensor_tensor(out=gates[:, :, 0:E3], in0=gates[:, :, 0:E3], in1=repl[:, :, 0:E3], op=ALU.mult).then_inc(v_r, 1)
            v.wait_ge(v_r, R3 + 10)
            v.tensor_copy(gsplit3[:, :, 0, :], gates[:, :, 0:E3]).then_inc(v_r, 1)
            v.wait_ge(v_r, R3 + 11)
            v.tensor_tensor(out=gsplit3[:, :, 1, :], in0=gates[:, :, 0:E3], in1=gsplit3[:, :, 0, :].bitcast(F32),
                            op=ALU.subtract).then_inc(v_r, 1)
            for n in range(2 * E3):
                v.wait_ge(c_act3, n + 1)
                v.wait_ge(t_cb3, n + 1)
                v.tensor_tensor(out=hid3[:, n % 2, :], in0=bank[6 + n % 2][:, :], in1=act3[:, n % 2, :], op=ALU.mult).then_inc(v_h3, 1)
                v.wait_ge(c_h3, n + 1)
                at_least(v, t_d3, n - 1)
                v.tensor_tensor(out=hid3_lo[:, n % 2, :], in0=hid3[:, n % 2, :], in1=hid3_hi[:, n % 2, :].bitcast(F32),
                                op=ALU.subtract).then_inc(v_h3lo, 1)
            v.wait_ge(t_d3, 2 * E3)
            for q in range(4):
                cut = slice(q * Q4, (q + 1) * Q4)
                v.tensor_tensor(out=x[:, cut], in0=bank[q][:, :], in1=x[:, cut], op=ALU.add).then_inc(v_x, 1)

        @block.gpsimd
        def _(g):
            g.memset(ident[:, :], 0.0).then_inc(p_id, 1)
            g.wait_ge(p_id, 1)
            g.affine_select(out=ident[:, :], in_=ident[:, :], compare_op=ALU.not_equal, fill=1.0, base=0,
                            pattern=[[-1, P]], channel_multiplier=1).then_inc(p_id, 1)
            g.wait_ge(c_ek, 1)
            g.tensor_tensor(out=ekv[:, 0:N], in0=ek[:, 0:N], in1=f[:, 0:N], op=ALU.mult).then_inc(p_ekv, 1)
            for k in range(PAIRS):
                if k == 2:
                    g.wait_ge(c_ek, 2)
                    g.tensor_tensor(out=ekv[:, N:2 * N], in0=ek[:, N:2 * N], in1=f[:, N:2 * N], op=ALU.mult).then_inc(p_ekv, 1)
                g.wait_ge(c_euk, k // 2 + 1)
                if k >= 2:
                    g.wait_ge(v_mix, 2 * (k - 1))
                pool_dk(g, 0, k, k % 2)
                pool_dkv(g, k, k % 2, k)
                pool_den(g, k % 2, k)
                pool_num(g, k % 2, k)
            for l in range(1, LAYERS):
                for h in range(CH):
                    cut = slice(h * N, (h + 1) * N)
                    g.tensor_scalar(out=mixed(l, h * N, N), in0=f[:, cut], scalar1=ucol[:, l, h:h + 1], scalar2=CAP,
                                    op0=ALU.add, op1=ALU.min).then_inc(p_cap, 1)

            def split(c, slot, done, loads):
                g.wait_ge(d_raw[slot], 16 * loads)
                g.wait_ge(c_whi, c + 1)
                at_least(g, t_down, done)
                g.tensor_tensor(out=wlo[slot][:, :], in0=raw[:, slot, 0:WCOLS], in1=whi[slot][:, 0:WCOLS].bitcast(F32),
                                op=ALU.subtract).then_inc(p_wlo, 1)

            split(0, 0, 0, 1)

            def body(i, wkv, last=False):
                if wkv:
                    l, p, k = wkv
                    g.wait_ge(v_mix, 2 * k)
                    pool_dk(g, l, p, 0)
                    pool_dkv(g, p, 0, k)
                split(2 * i + 1, 1, 4 * i, i + 1)
                if wkv:
                    pool_den(g, 0, k)
                    pool_num(g, 0, k)
                if not last:
                    split(2 * i + 2, 0, 4 * i + 2, i + 2)

            body(0, None)
            with g.Fori(1, LAYERS) as l:
                g.wait_ge(c_euk, l + 2)
                for p in range(PAIRS):
                    body(PAIRS * l + p + 1 - PAIRS, (l, p, PAIRS * l + p))
            for i in range(1 + PAIRS * (LAYERS - 1), HALF_IT):
                body(i, None, i == HALF_IT - 1)
            for k in range(CH):
                g.wait_ge(c_w1, k + 1)
                g.tensor_tensor(out=wq_lo[:, k, :].rearrange("p (h r d) -> p h r d", h=HEADS, r=REP),
                                in0=w1raw[:, k, 0:C].rearrange("p (h d) -> p h d", h=HEADS).unsqueeze(2).to_broadcast([P, HEADS, REP, HD]),
                                in1=wq_hi[:, k, :].rearrange("p (h r d) -> p h r d", h=HEADS, r=REP).bitcast(F32),
                                op=ALU.subtract).then_inc(p_w1, 1)
            g.wait_ge(c_w1, 3)
            g.tensor_tensor(out=wkv_lo[:, :, :], in0=w1raw[:, :, C:3 * C], in1=wkv_hi[:, :, :].bitcast(F32),
                            op=ALU.subtract).then_inc(p_w1, 1)
            g.wait_ge(v_x, 4)
            g.tensor_copy(identb[:, :], ident[:, :]).then_inc(p_const, 1)
            g.memset(negmask[:, :], 0.0).then_inc(p_id, 1)
            g.wait_ge(p_id, 3)
            g.affine_select(out=negmask[:, :], in_=negmask[:, :], compare_op=ALU.is_ge, fill=-1e30, base=0,
                            pattern=[[-1, P]], channel_multiplier=1).then_inc(p_const, 1)
            g.memset(ones2f[:, :], 1.0).then_inc(p_id, 1)
            g.wait_ge(p_id, 4)
            g.tensor_copy(ones2[:, :], ones2f[:, :]).then_inc(p_const, 1)
            g.memset(rowlo[0:32, :], 0.0).then_inc(p_id, 1)
            g.memset(rowlo[32:64, :], -1.0).then_inc(p_id, 1)
            g.memset(rowlo[64:96, :], 0.0).then_inc(p_id, 1)
            g.memset(rowlo[96:128, :], -1.0).then_inc(p_const, 1)
            g.wait_ge(p_id, 7)
            for b in range(B):
                g.wait_ge(c_p, BGROUPS * b + 8)
                d0 = pt0[:, :, :, 0:P].rearrange("p r m q -> p (r m) q")
                g.affine_select(out=d0, in_=d0, compare_op=ALU.is_ge, fill=0.0, base=0,
                                pattern=[[0, HEADS], [1, P]], channel_multiplier=-1).then_inc(p_sel, 1)
                g.wait_ge(c_p, BGROUPS * (b + 1))
                d1 = pt1[:, :, :, :].rearrange("p r m q -> p (r m) q")
                g.affine_select(out=d1, in_=d1, compare_op=ALU.is_ge, fill=0.0, base=0,
                                pattern=[[0, HEADS], [1, P]], channel_multiplier=-1).then_inc(p_sel, 1)
            g.wait_ge(v_peak, 8)
            g.partition_all_reduce(peakall[:, :], peak2[:, :], channels=P, reduce_op=bass.bass_isa.ReduceOp.max).then_inc(p_peak, 1)
            g.wait_ge(c_w3, 1)
            g.tensor_tensor(out=w3a_lo[:, :, :], in0=w3a_raw, in1=w3a_hi[:, :, :].bitcast(F32), op=ALU.subtract).then_inc(p_w3, 1)
            g.wait_ge(c_w3, 2)
            g.tensor_tensor(out=w3b_lo[:, :, :], in0=w3b_raw, in1=w3b_hi[:, :, :].bitcast(F32), op=ALU.subtract).then_inc(p_w3, 1)

        @block.tensor
        def _(t):
            mm = nc.tensor.matmul
            t.wait_ge(v_s, 4)
            rv = bank[7][:, :].rearrange("p (t e) -> p t e", t=TILES)
            for i in range(TILES):
                for k in range(CH):
                    last = mm(rv[:, i, 0:GATES], s[:, k * N + i * P:k * N + (i + 1) * P], rw[:, k, :],
                              start=(k == 0), stop=(k == CH - 1))
            last.then_inc(t_rout, 1)
            t.wait_ge(p_id, 2)
            t.wait_ge(v_r, 33)
            for j in range(2):
                for i in range(4):
                    last = nc.tensor.transpose(bank[4 + j][0:2 * GATES, i * P:(i + 1) * P],
                                               gsplit[:, 4 * j + i, :, :].rearrange("p a e -> p (a e)").bitcast(F32), ident[:, :])
                last.then_inc(t_rtr, 1)
            t.wait_ge(v_slo, 4)
            t.wait_ge(c_gate, 2)

            def down(slot, hf, n_done, first, last):
                t.wait_ge(c_hhi, n_done)
                t.wait_ge(v_hlo, n_done)
                for ch in range(CH):
                    cols = slice(2 * CH * P + ch * P, 2 * CH * P + (ch + 1) * P)
                    o = bank[2 * ch + hf][:, :]
                    mm(o, whi[slot][:, cols], hid_hi[:, hf, :], start=first, stop=False)
                    mm(o, whi[slot][:, cols], hid_lo[:, hf, :], start=False, stop=False)
                    m = mm(o, wlo[slot][:, cols], hid_hi[:, hf, :], start=False, stop=last)
                m.then_inc(t_down, 1)

            def body(i, first, final=False):
                for n in range(4):
                    ch, hf = n // 2, n % 2
                    if hf == 0:
                        t.wait_ge(c_whi, 2 * i + ch + 1)
                        t.wait_ge(p_wlo, 2 * i + ch + 1)
                    for part, (bk, free, done) in enumerate(((4, c_sil, t_g), (5, v_up, t_u))):
                        at_least(t, free, 4 * i + n)
                        for k in range(CH):
                            w = slice((k * 2 + part) * P, (k * 2 + part + 1) * P)
                            r = slice(k * N + hf * Q4, k * N + (hf + 1) * Q4)
                            mm(bank[bk][:, :], whi[ch][:, w], s_hi[:, r], start=(k == 0), stop=False)
                            mm(bank[bk][:, :], whi[ch][:, w], s_lo[:, r], start=False, stop=False)
                            m = mm(bank[bk][:, :], wlo[ch][:, w], s_hi[:, r], start=False, stop=(k == CH - 1))
                        m.then_inc(done, 1)
                    at_least(t, v_hid, 4 * i + n)
                    mm(bank[6][:, :], whi[ch][0:2 * GATES, WCOLS:RAWCOLS], gate_t[:, hf * Q4:(hf + 1) * Q4],
                       start=True, stop=True).then_inc(t_cb, 1)
                    if not (first and n == 0):
                        down((ch - 1 + hf) % 2, 1 - hf, 4 * i + n, first and n in (1, 2), final and n == 3)

            body(0, True)
            with t.Fori(1, HALF_IT - 1) as i:
                body(i, False)
            body(HALF_IT - 1, False, True)
            down(1, 1, 4 * HALF_IT, False, True)

            def router(bk, w, width, n_s):
                t.wait_ge(v_s, n_s)
                r = bank[bk][:, :].rearrange("p (t e) -> p t e", t=TILES)
                for i in range(TILES):
                    for k in range(CH):
                        m = mm(r[:, i, 0:width], s[:, k * N + i * P:k * N + (i + 1) * P], w[:, k, :],
                               start=(k == 0), stop=(k == CH - 1))
                m.then_inc(t_rout, 1)

            def key_rows(i):
                t.wait_ge(v_kst, 2 * i + 2)
                at_least(t, c_kt, i - 1)
                nc.tensor.transpose(bank[6 + i % 2][:, 0:P], kst[:, i % 2, :, :, :].rearrange("p r a d -> p (r a d)").bitcast(F32),
                                    ident[:, :]).then_inc(t_kt, 1)

            t.wait_ge(d_w1, 32)
            router(4, wg1, HEADS, 8)
            t.wait_ge(c_w1, 3)
            t.wait_ge(p_w1, 3)
            t.wait_ge(v_slo, 8)
            for j in range(2):
                for m in range(HEADS // 2):
                    n = j * 8 + m
                    at_least(t, v_q, n - 1)
                    for k in range(CH):
                        w = slice(m * P, (m + 1) * P)
                        r = slice(k * N + j * Q4, k * N + (j + 1) * Q4)
                        mm(bank[2 + n % 2][:, :], wq_hi[:, k, w], s_hi[:, r], start=(k == 0), stop=False)
                        mm(bank[2 + n % 2][:, :], wq_hi[:, k, w], s_lo[:, r], start=False, stop=False)
                        last = mm(bank[2 + n % 2][:, :], wq_lo[:, k, w], s_hi[:, r], start=False, stop=(k == CH - 1))
                    last.then_inc(t_q, 1)
                for i in range(4 * j, 4 * j + 4):
                    at_least(t, v_kv, i - 1)
                    for k in range(CH):
                        r = slice(k * N + i * P, k * N + (i + 1) * P)
                        mm(bank[i % 2][:, :], s_hi[:, r], wkv_hi[:, k, :], start=(k == 0), stop=False)
                        mm(bank[i % 2][:, :], s_lo[:, r], wkv_hi[:, k, :], start=False, stop=False)
                        last = mm(bank[i % 2][:, :], s_hi[:, r], wkv_lo[:, k, :], start=False, stop=(k == CH - 1))
                    last.then_inc(t_kv, 1)
                    if i >= 1:
                        key_rows(i - 1)
            key_rows(TILES - 1)
            t.wait_ge(c_kt, TILES)
            t.wait_ge(v_q, 16)
            t.wait_ge(p_const, 4)

            def scores_by_query(i, ga):
                kw = P * (i % 2 + 1)
                for r, m0, nm in ALIST[i % 2]:
                    bk = bank[4 + r][:, :].rearrange("p (m k) -> p m k", m=nm)
                    at_least(t, v_nmax, ga - 1)
                    mm(bk[:, :, kw - P:kw], identb[:, :], negmask[:, :].unsqueeze(1).to_broadcast([P, nm, P]),
                       start=True, stop=False, skip_group_check=True)
                    rows = slice(r * HROWS, (r + 1) * HROWS)
                    for m in range(m0, m0 + nm):
                        last = mm(bk[:, m - m0, :], qs[rows, m, i * P:(i + 1) * P], keys_t[rows, (i // 2) * T:(i // 2) * T + kw],
                                  start=False, stop=(m == m0 + nm - 1), skip_group_check=True)
                    last.then_inc(t_a, 1)
                    ga += 1
                return ga

            def maxima_rows(i):
                t.wait_ge(v_nmx, 2 * i + 2)
                at_least(t, c_nmx, i)
                nc.tensor.transpose(bank[6][0:2 * HEADS, 0:P], nmx[:, i % 2, :, :].rearrange("p a h -> p (a h)").bitcast(F32),
                                    ident[:, :]).then_inc(t_nmx, 1)

            ga = 0
            for i in range(2):
                ga = scores_by_query(i, ga)
            for i in range(2):
                maxima_rows(i)
            for b in range(B):
                if b + 1 < B:
                    for i in range(2 * b + 2, 2 * b + 4):
                        ga = scores_by_query(i, ga)
                t.wait_ge(d_nmx, 64 * (b + 1))
                for gi, (kc, r, m0, nm) in enumerate(BLIST):
                    n = BGROUPS * b + gi
                    if gi in (6, 9) and b + 1 < B:
                        maxima_rows(2 * b + (2 if gi == 6 else 3))
                    at_least(t, c_p, n - 1)
                    bk = bank[2 + gi % 2][:, :]
                    q0 = b * T + kc * P
                    rows = slice(r * HROWS, (r + 1) * HROWS)
                    heads = slice(2 * m0 + r, 2 * (m0 + nm - 1) + r + 1, 2)
                    if kc == 0:
                        neg = nmrow[:, :, heads, :].rearrange("p t h q -> p h t q")
                        mm(bk.rearrange("p (h t q) -> p h t q", h=nm, t=2), ones2[:, :], neg, start=True, stop=False)
                    else:
                        mm(bk.rearrange("p (h q) -> p h q", h=nm), ones2[:, :], nmrow[:, 1, heads, :], start=True, stop=False)
                    mm(bk.rearrange("p (m q) -> p m q", m=nm), keys_t[rows, b * T + kc * P:b * T + (kc + 1) * P],
                       qs[rows, m0:m0 + nm, q0:(b + 1) * T], start=False, stop=True).then_inc(t_b, 1)
                t.wait_ge(p_sel, 2 * b + 2)
                t.wait_ge(v_val, 2 * b + 2)
                for i in range(2 * b, 2 * b + 2):
                    at_least(t, v_y, i - 1)
                    acc = bank[i % 2][:, :].rearrange("p (h d) -> p h d", h=HEADS)
                    for h in range(HEADS):
                        qt = i % 2
                        last = mm(acc[:, h, 0:HD + 1], pt0[:, h % 2, h // 2, qt * P:(qt + 1) * P], vals[:, 2 * b, :],
                                  start=True, stop=(qt == 0))
                        if qt == 1:
                            last = mm(acc[:, h, 0:HD + 1], pt1[:, h % 2, h // 2, :], vals[:, 2 * b + 1, :], start=False, stop=True)
                    last.then_inc(t_pv, 1)
                for i in range(2 * b, 2 * b + 2):
                    t.wait_ge(v_y, i + 1)
                    if i % 2 == 0:
                        at_least(t, v_x, 4 + i if i else 0)
                    for h in range(CH):
                        last = nc.tensor.transpose(bank[7][:, (i % 2) * C + h * P:(i % 2) * C + (h + 1) * P],
                                                   yt[:, i % 2, :, :].rearrange("p h d -> p (h d)")[:, h * P:(h + 1) * P], ident[:, :])
                    last.then_inc(t_yt, 1)

            t.wait_ge(v_wq2, 2)
            for q in range(4):
                t.wait_ge(v_xq, 4)
                for k in range(CH):
                    last = mm(bank[q][:, :], w2q[:, k, (q // 2) * P:(q // 2 + 1) * P],
                              xq[:, k * N + (q % 2) * Q4:k * N + (q % 2 + 1) * Q4], start=(k == 0), stop=(k == CH - 1))
                last.then_inc(t_l2, 1)

            router(7, wg3, E3, 16)
            t.wait_ge(v_r, R3 + 12)
            for j in range(2):
                for i in range(4):
                    last = nc.tensor.transpose(bank[4 + j][0:2 * E3, i * P:(i + 1) * P],
                                               gsplit3[:, 4 * j + i, :, :].rearrange("p a e -> p (a e)").bitcast(F32), ident[:, :])
                last.then_inc(t_rtr, 1)
            t.wait_ge(c_w3, 3)
            t.wait_ge(p_w3, 2)
            t.wait_ge(v_slo, 12)
            t.wait_ge(c_gate, 4)

            def down3(n):
                t.wait_ge(c_h3, n + 1)
                t.wait_ge(v_h3lo, n + 1)
                e, hf = n // 2, n % 2
                for ch in range(CH):
                    cols = slice(ch * P, (ch + 1) * P)
                    o = bank[2 * ch + hf][:, :]
                    mm(o, w3b_hi[:, e, cols], hid3_hi[:, hf, :], start=(e == 0), stop=False)
                    mm(o, w3b_hi[:, e, cols], hid3_lo[:, hf, :], start=False, stop=False)
                    m = mm(o, w3b_lo[:, e, cols], hid3_hi[:, hf, :], start=False, stop=(e == E3 - 1))
                m.then_inc(t_d3, 1)

            for n in range(2 * E3):
                e, hf = n // 2, n % 2
                at_least(t, c_act3, n - 1)
                for k in range(CH):
                    w = slice(e * H3, (e + 1) * H3)
                    r = slice(k * N + hf * Q4, k * N + (hf + 1) * Q4)
                    mm(bank[4 + hf][:, :], w3a_hi[:, k, w], s_hi[:, r], start=(k == 0), stop=False)
                    mm(bank[4 + hf][:, :], w3a_hi[:, k, w], s_lo[:, r], start=False, stop=False)
                    m = mm(bank[4 + hf][:, :], w3a_lo[:, k, w], s_hi[:, r], start=False, stop=(k == CH - 1))
                m.then_inc(t_h3, 1)
                at_least(t, v_h3, n - 1)
                mm(bank[6 + hf][:, :], sel3[:, e, :], gate3_t[:, hf * Q4:(hf + 1) * Q4], start=True, stop=True).then_inc(t_cb3, 1)
                if n >= 1:
                    down3(n - 1)
            down3(2 * E3 - 1)


OUT_SHAPE = (B, T, C)


def lay_out(np_, inputs):
    cm = lambda v: np_.ascontiguousarray(np_.asarray(v).reshape(N, C).T)
    g = {k: np_.asarray(v) for k, v in inputs.items()}
    a = {"xT": cm(g["x"]), "fT": cm(g["fside_BxSxS_0"]), "temb": g["cond_512"]}
    for n in ("w", "u"):
        a[n] = np_.ascontiguousarray(np_.stack([g[f"L{l}_cond_{n}"].reshape(CH, P) for l in range(LAYERS)]).transpose(2, 0, 1))
    a["router"] = np_.ascontiguousarray(np_.concatenate([g["L0_ffn_router_w"].T, g["L0_ffn_sh_gate_w"]], axis=1))

    def rows(e, sh):
        w = np_.zeros((C, CHUNKS * P), np_.float32)
        w[:, :E0 * I_MOE] = e.transpose(1, 0, 2).reshape(C, E0 * I_MOE)
        w[:, E0 * I_MOE:ROWS0] = sh
        return w.reshape(CH, P, CHUNKS, P)

    w0 = np_.zeros((CHUNKS, P, RAWCOLS), np_.float32)
    for k in range(CH):
        for j, (e, sh) in enumerate((("w_gate", "sh_gate"), ("w_up", "sh_up"))):
            w0[:, :, (k * 2 + j) * P:(k * 2 + j + 1) * P] = rows(g["L0_ffn_" + e], g["L0_ffn_" + sh])[k].transpose(1, 0, 2)
    down = np_.zeros((CHUNKS * P, C), np_.float32)
    down[:E0 * I_MOE] = g["L0_ffn_w_down"].reshape(E0 * I_MOE, C)
    down[E0 * I_MOE:ROWS0] = g["L0_ffn_sh_down"]
    w0[:, :, 2 * CH * P:WCOLS] = down.reshape(CHUNKS, P, C)
    for r in range(ROWS0):
        e = min(r // I_MOE, E0)
        w0[r // P, e, WCOLS + r % P] = 1.0
        w0[r // P, GATES + e, WCOLS + r % P] = 1.0
    a["w0"] = w0
    a["w1"] = np_.ascontiguousarray(g["L1_ffn_W_qkv"].T)
    a["wg1"] = np_.ascontiguousarray(g["L1_ffn_W_gate"].T)
    a["w2"] = np_.ascontiguousarray(g["L2_ffn_weight"].T)
    a["b2"] = np_.ascontiguousarray(g["L2_ffn_bias"].reshape(CH, P).T)
    a["wg3"] = g["L3_ffn_wg"]
    a["w3a"] = np_.ascontiguousarray(g["L3_ffn_w1"].transpose(2, 0, 1).reshape(C, E3 * H3))
    a["w3b"] = np_.ascontiguousarray(g["L3_ffn_w2"].transpose(0, 2, 1))
    a["sel3"] = np_.ascontiguousarray(np_.tile(np_.repeat(np_.eye(E3, dtype=np_.float32)[:, :, None], P, axis=2), (2, 1, 1)))
    return a


def kernel(**inputs):
    import numpy as _np
    import concourse.bacc as _bacc
    from concourse.bass_utils import run_bass_kernel_spmd as _run

    nc = _bacc.Bacc("TRN2", target_bir_lowering=False, num_devices=1)
    arrays = lay_out(_np, inputs)
    aps = {k: nc.dram_tensor("in_" + k, v.shape, mybir.dt.from_np(v.dtype), kind="ExternalInput").ap() for k, v in arrays.items()}
    res = nc.dram_tensor("res", (C, N), F32, kind="ExternalOutput").ap()
    build(nc, aps, res)
    r = _run(nc, [{"in_" + k: v for k, v in arrays.items()}], core_ids=[0])
    return _np.ascontiguousarray(r.results[0]["res"].T).reshape(OUT_SHAPE)
```

```python
from contextlib import ExitStack

import numpy as np
import concourse.bass as bass
from concourse import mybir
from concourse.alu_op_type import AluOpType as ALU

F32 = mybir.dt.float32
F32R = mybir.dt.float32r
BF16 = mybir.dt.bfloat16
FP8 = mybir.dt.float8e4
ACT = mybir.ActivationFunctionType
AX = mybir.AxisListType

P = 128
LAYERS = 4
B, T, C, TE = 4, 256, 256, 64
N = B * T
CH = C // P
COLS = CH * N
HB = CH * B
PAIR = 2 * T
PAIRS = HB // 2
Q4 = 512
TILES = N // P
E0, I_MOE, I_SH, K0 = 16, 176, 704, 4
GATES = E0 + 1
ROWS0 = E0 * I_MOE + I_SH
CHUNKS = -(-ROWS0 // (2 * P)) * 2
WCOLS = 2 * CH * P + C
RAWCOLS = WCOLS + P
HEADS, HD = 16, 16
E3, H3, K3 = 8, 128, 4
REP = 4
HROWS = REP * HD
VGAP = 3 * HD
VW = 3 * VGAP + 2 * HD
GROUPS = 6
PCOLS = GROUPS * Q4
BLOCKS = 2 * B
CAP = 30.0
LOW = -3.0e38


def at_least(eng, sem, value):
    if isinstance(value, int) and value <= 0:
        return
    eng.wait_ge(sem, value)


def build(nc, a, out, stop=9):
    ctx = ExitStack()
    with ctx:
        def sb(name, shape, dt=F32):
            return ctx.enter_context(nc.sbuf_tensor(name, shape, dt))

        def sem(name):
            return ctx.enter_context(nc.semaphore(name))

        bank = [ctx.enter_context(nc.psum_tensor(f"bank{i}", [P, Q4], F32)) for i in range(8)]

        x = sb("x", [P, COLS])
        f = sb("f", [P, COLS])
        mix = sb("mix", [P, LAYERS * COLS])
        sig = sb("sig", [P, 2, Q4])
        s = sb("s", [P, COLS])
        s_parts = sb("s_parts", [P, 2 * COLS], F32R)
        s_hi = s_parts[:, 0:COLS]
        s_lo = s_parts[:, COLS:2 * COLS]
        temb = sb("temb", [P, B, TE])
        tsum = sb("tsum", [P, B])
        tf = sb("tf", [P, B])
        tdecay = sb("tdecay", [P, B])
        wcol = sb("wcol", [P, LAYERS, CH])
        ucol = sb("ucol", [P, LAYERS, CH])
        wexp = sb("wexp", [P, LAYERS, CH])
        wdec = sb("wdec", [P, LAYERS, CH])
        decay = sb("decay", [P, LAYERS, CH, B])
        tmul = sb("tmul", [P, CH, B])
        decay_c = decay[:, :, :, :].rearrange("p l h b -> p (l h b)")
        tmul_c = tmul[:, :, :].rearrange("p h b -> p (h b)")
        EP = E0 + 8
        prob = sb("prob", [P, TILES, EP])
        repl = sb("repl", [P, TILES, EP])
        top8 = sb("top8", [P, TILES, 8])
        rmax = sb("rmax", [P, TILES])
        rsum = sb("rsum", [P, TILES])
        rsg = sb("rsg", [P, TILES])
        gates = sb("gates", [P, TILES, GATES])
        gsplit = sb("gsplit", [P, TILES, 2, GATES], F32R)
        gsplit3 = sb("gsplit3", [P, TILES, 2, E3], F32R)
        ident = sb("ident", [P, P])
        identb = sb("identb", [P, P], BF16)

        rw = sb("rw", [P, CH, GATES])
        w1raw = sb("w1raw", [P, CH, 3 * C])
        wq_hi = sb("wq_hi", [P, CH, C], F32R)
        wq_lo = sb("wq_lo", [P, CH, C], F32R)
        wkv_hi = sb("wkv_hi", [P, CH, 2 * C], F32R)
        wkv_lo = sb("wkv_lo", [P, CH, 2 * C], F32R)
        spread = sb("spread", [P, 2, 4, P], F32R)
        wg1 = sb("wg1", [P, CH, HEADS])
        w2in = sb("w2in", [P, CH, C], BF16)
        w2q = sb("w2q", [P, CH, C], FP8)
        b2in = sb("b2in", [P, CH], BF16)
        b2 = sb("b2", [P, CH])
        wg3 = sb("wg3", [P, CH, E3])
        peak = sb("peak", [P, 4 + CH])
        peak2 = sb("peak2", [P, 2])
        peakall = sb("peakall", [P, 2])
        peakinv = sb("peakinv", [P, 2])
        scale2 = sb("scale2", [P, 1])
        own0 = ExitStack()

        def sb0(name, shape, dt=F32):
            return own0.enter_context(nc.sbuf_tensor(name, shape, dt))

        ek = sb0("ek", [P, COLS])
        ekv = sb0("ekv", [P, COLS])
        dk = sb0("dk", [P, 2, PAIR])
        dkv = sb0("dkv", [P, 2, PAIR])
        nf = sb0("nf", [P, 2, PAIR])
        nb = sb0("nb", [P, 2, PAIR])
        df = sb0("df", [P, 2, PAIR])
        db = sb0("db", [P, 2, PAIR])
        raw = sb0("raw", [P, 2, RAWCOLS])
        whi = [sb0(f"whi{i}", [P, RAWCOLS], F32R) for i in range(2)]
        wlo = [sb0(f"wlo{i}", [P, WCOLS], F32R) for i in range(2)]
        sil = sb0("sil", [P, 2, Q4])
        up = sb0("up", [P, Q4])
        hid = sb0("hid", [P, 2, Q4])
        hid_hi = sb0("hid_hi", [P, 2, Q4], F32R)
        hid_lo = sb0("hid_lo", [P, 2, Q4], F32R)
        gate_t = sb0("gate_t", [2 * GATES, N], F32R)
        own0.close()
        own1 = ExitStack()

        def sb1(name, shape, dt=F32):
            return own1.enter_context(nc.sbuf_tensor(name, shape, dt))

        qc_hi = sb1("qc_hi", [P, CH, N], F32R)
        qc_lo = sb1("qc_lo", [P, CH, N], F32R)
        qs = sb1("qs", [P, HEADS // 2, N], F32R)
        negmask = sb1("negmask", [P, P], BF16)
        kvs = sb1("kvs", [P, 2, 2 * C])
        kv1 = sb1("kv1", [P, 2, 2, HD])
        kst = sb1("kst", [P, 2, 2, REP, HD], F32R)
        vals = sb1("vals", [P, TILES, VW])
        keys_t = sb1("keys_t", [P, N], F32R)
        nmax = sb1("nmax", [P, 2, 2, HEADS // 2])
        nmx = sb1("nmx", [P, 2, 2, 2, HEADS // 2], F32R)
        nmx_t = sb1("nmx_t", [2 * HEADS, 2, P])
        pexp = [sb1(f"pexp{i}", [P, PCOLS]) for i in range(2)]
        rden = sb1("rden", [P // 2, Q4])
        yt = sb1("yt", [P, 2, T])
        own1.close()
        own2 = ExitStack()

        def sb2(name, shape, dt=F32):
            return own2.enter_context(nc.sbuf_tensor(name, shape, dt))

        xq = sb2("xq", [P, COLS], FP8)
        y2a = sb2("y2a", [P, 2, Q4], BF16)
        y2b = sb2("y2b", [P, 2, Q4], BF16)
        w3a_hi = sb2("w3a_hi", [P, CH, E3 * H3], F32R)
        w3a_lo = sb2("w3a_lo", [P, CH, E3 * H3], F32R)
        w3b_hi = sb2("w3b_hi", [P, E3, C], F32R)
        w3b_lo = sb2("w3b_lo", [P, E3, C], F32R)
        sel3 = sb2("sel3", [2 * E3, E3, P], F32R)
        act3 = sb2("act3", [P, 2, Q4])
        hid3 = sb2("hid3", [P, 2, Q4])
        hid3_hi = sb2("hid3_hi", [P, 2, Q4], F32R)
        hid3_lo = sb2("hid3_lo", [P, 2, Q4], F32R)
        gate3_t = sb2("gate3_t", [2 * E3, N], F32R)
        own2.close()
        w3a_raw = f[:, :].rearrange("p (k n) -> p k n", k=CH)
        w3b_raw = mix[:, 0:COLS].rearrange("p (e n) -> p e n", e=E3)

        ctx.enter_context(nc.allow_low_precision(reason="exact splits into float32r parts"))

        d_in = sem("d_in")
        d_small = sem("d_small")
        d_raw = [sem("d_raw0"), sem("d_raw1")]
        d_out = sem("d_out")
        c_tf = sem("c_tf")
        v_tf = sem("v_tf")
        p_id = sem("p_id")
        v_cap = sem("v_cap")
        p_cap = sem("p_cap")
        c_ek = sem("c_ek")
        c_euk = sem("c_euk")
        p_ekv = sem("p_ekv")
        p_dk = sem("p_dk")
        p_den = sem("p_den")
        p_num = sem("p_num")
        p_add = sem("p_add")
        v_dscan = sem("v_dscan")
        v_nscan = sem("v_nscan")
        v_den = sem("v_den")
        v_mix = sem("v_mix")
        c_sig = sem("c_sig")
        v_s = sem("v_s")
        c_shi = sem("c_shi")
        v_slo = sem("v_slo")
        t_rout = sem("t_rout")
        v_r = sem("v_r")
        c_r = sem("c_r")
        t_rtr = sem("t_rtr")
        c_gate = sem("c_gate")
        c_whi = sem("c_whi")
        p_wlo = sem("p_wlo")
        t_g = sem("t_g")
        t_u = sem("t_u")
        t_cb = sem("t_cb")
        t_down = sem("t_down")
        c_sil = sem("c_sil")
        v_up = sem("v_up")
        v_hid = sem("v_hid")
        c_hhi = sem("c_hhi")
        v_hlo = sem("v_hlo")
        v_x = sem("v_x")
        d_w1 = sem("d_w1")
        d_w23 = sem("d_w23")
        d_w3 = sem("d_w3")
        c_w1 = sem("c_w1")
        p_w1 = sem("p_w1")
        p_const = sem("p_const")
        v_const = sem("v_const")
        d_spread = sem("d_spread")
        d_sel3 = sem("d_sel3")
        t_qc = sem("t_qc")
        c_qc = sem("c_qc")
        v_qc = sem("v_qc")
        t_qs = sem("t_qs")
        c_qs = sem("c_qs")
        v_qs = sem("v_qs")
        t_kv = sem("t_kv")
        c_kv = sem("c_kv")
        p_kv = sem("p_kv")
        v_red = sem("v_red")
        v_k1 = sem("v_k1")
        v_kst = sem("v_kst")
        v_val = sem("v_val")
        t_kt = sem("t_kt")
        c_kt = sem("c_kt")
        t_a = sem("t_a")
        v_nmax = sem("v_nmax")
        v_nmx = sem("v_nmx")
        t_nmx = sem("t_nmx")
        c_nmx = sem("c_nmx")
        d_nmx = [sem("d_nmx0"), sem("d_nmx1")]
        t_b = sem("t_b")
        c_p = sem("c_p")
        p_sel = sem("p_sel")
        t_pv = sem("t_pv")
        v_rden = sem("v_rden")
        v_y = sem("v_y")
        t_yt = sem("t_yt")
        v_peak = sem("v_peak")
        p_peak = sem("p_peak")
        v_xq = sem("v_xq")
        v_wq2 = sem("v_wq2")
        t_l2 = sem("t_l2")
        c_y2 = sem("c_y2")
        c_y2b = sem("c_y2b")
        c_w3 = sem("c_w3")
        p_w3 = sem("p_w3")
        t_h3 = sem("t_h3")
        t_cb3 = sem("t_cb3")
        c_act3 = sem("c_act3")
        v_h3 = sem("v_h3")
        c_h3 = sem("c_h3")
        v_h3lo = sem("v_h3lo")
        t_d3 = sem("t_d3")

        block = ctx.enter_context(nc.Block())
        HALF_IT = CHUNKS // 2


        def seq(buf, col, n=T):
            return buf[:, bass.ds(col, n)] if not isinstance(col, int) else buf[:, col:col + n]

        def mixed(l, col, n):
            return mix[:, bass.ds(l * COLS + col, n)]

        def scans(v, l, p, st, den):
            src, fw, bw, done = (ek, df, db, v_dscan) if den else (ekv, nf, nb, v_nscan)
            for j in range(2):
                d = decay_c[:, bass.ds(l * HB + p * 2 + j, 1)].to_broadcast([P, T])
                data = src[:, p * PAIR + j * T:p * PAIR + (j + 1) * T]
                v.tensor_tensor_scan(out=fw[:, st, j * T:(j + 1) * T], data0=d, data1=data,
                                     initial=0.0, op0=ALU.mult, op1=ALU.add).then_inc(done, 1)
                rev = slice((j + 1) * T - 1, j * T - 1 if j else None, -1)
                v.tensor_tensor_scan(out=bw[:, st, rev], data0=d, data1=data[:, ::-1],
                                     initial=0.0, op0=ALU.mult, op1=ALU.add).then_inc(done, 1)

        def finish_den(v, st, part, k):
            cut = slice(part * T, (part + 1) * T)
            v.tensor_scalar(out=df[:, st, cut], in0=df[:, st, cut], scalar1=1e-8, scalar2=None,
                            op0=ALU.max).then_inc(v_den, 1)
            v.wait_ge(v_den, k * 4 + part * 2 + 1)
            v.reciprocal(df[:, st, cut], df[:, st, cut]).then_inc(v_den, 1)

        def finish_mix(v, l, p, st, k):
            for j in range(2):
                cut = slice(j * T, (j + 1) * T)
                v.scalar_tensor_tensor(out=mixed(l, p * PAIR + j * T, T), in0=nf[:, st, cut],
                                       scalar=tmul_c[:, p * 2 + j:p * 2 + j + 1], in1=df[:, st, cut],
                                       op0=ALU.mult, op1=ALU.mult).then_inc(v_mix, 1)

        def pool_dk(g, l, p, st):
            cols = slice(p * PAIR, (p + 1) * PAIR)
            g.tensor_tensor(out=dk[:, st, :], in0=mixed(l, p * PAIR, PAIR), in1=ek[:, cols], op=ALU.subtract).then_inc(p_dk, 1)

        def pool_dkv(g, p, st, k):
            g.wait_ge(p_dk, 2 * k + 1)
            g.tensor_tensor(out=dkv[:, st, :], in0=dk[:, st, :], in1=f[:, p * PAIR:(p + 1) * PAIR],
                            op=ALU.mult).then_inc(p_dk, 1)

        def pool_den(g, st, k):
            g.wait_ge(v_dscan, 4 * (k + 1))
            g.tensor_tensor(out=df[:, st, :], in0=df[:, st, :], in1=db[:, st, :], op=ALU.add).then_inc(p_add, 1)
            g.wait_ge(p_add, 2 * k + 1)
            g.tensor_tensor(out=df[:, st, :], in0=df[:, st, :], in1=dk[:, st, :], op=ALU.add).then_inc(p_den, 1)

        def pool_num(g, st, k):
            g.wait_ge(v_nscan, 4 * (k + 1))
            g.tensor_tensor(out=nf[:, st, :], in0=nf[:, st, :], in1=nb[:, st, :], op=ALU.add).then_inc(p_add, 1)
            g.wait_ge(p_add, 2 * k + 2)
            g.tensor_tensor(out=nf[:, st, :], in0=nf[:, st, :], in1=dkv[:, st, :], op=ALU.add).then_inc(p_num, 1)

        def cond_act(c, l):
            def high(q):
                cut = slice(q * Q4, (q + 1) * Q4)
                c.wait_ge(v_s, 4 * l + q + 1)
                c.activation(s_hi[:, cut], s[:, cut], ACT.Copy).then_inc(c_shi, 1)

            for q in range(4):
                cut = slice(q * Q4, (q + 1) * Q4)
                n = 4 * l + q
                if l == 0:
                    c.wait_ge(d_in, 48)
                elif l == 1:
                    c.wait_ge(v_x, q + 1)
                elif l == 2:
                    c.wait_ge(v_x, 4 + TILES)
                else:
                    c.wait_ge(v_x, 4 + TILES + q + 1)
                at_least(c, v_s, n - 1)
                c.activation(sig[:, q % 2, :], x[:, cut], ACT.Sigmoid).then_inc(c_sig, 1)
                if l != 2 and q >= 1:
                    high(q - 1)
            if l != 2:
                high(3)

        R0 = 33
        R3 = R0 + 9
        ALIST = [[(r, m, nm) for m in range(0, 8, nm) for r in range(2)] for nm in (4, 2)]
        BLIST = [(kc, r, m, nm) for kc, nm in ((0, 2), (1, 4)) for m in range(0, 4, nm) for r in range(2)]
        AHEAD = 3
        ASTEPS = [[[0], [1], [2], [3], [], []], [[0, 1], [2, 3], [4], [5], [6], [7]]]

        def a_before(t):
            return sum(len(ALIST[i % 2]) for i in range(t))

        def p_at(buf, k, kc, r, m, nm):
            w = T if kc == 0 else P
            at = (0 if kc == 0 else 8 * T) + (r * 4 + m) * w
            return buf[k % 2][:, at:at + nm * w]

        def cond_dve(v, l):
            for q in range(4):
                cut = slice(q * Q4, (q + 1) * Q4)
                n = 4 * l + q
                v.wait_ge(c_sig, n + 1)
                v.wait_ge(v_mix, 8 * l + 2 * q + 2)
                if l == 3:
                    v.wait_ge(v_xq, 4)
                v.tensor_tensor(out=s[:, cut], in0=sig[:, q % 2, :], in1=mixed(l, cut.start, Q4), op=ALU.mult).then_inc(v_s, 1)
                if l == 2:
                    v.wait_ge(v_s, n + 1)
                    v.tensor_reduce(out=peak[:, q:q + 1], in_=s[:, cut], op=ALU.max, axis=AX.X,
                                    apply_absolute_value=True).then_inc(v_peak, 1)
                    continue
                v.wait_ge(c_shi, 4 * min(l, 2) + q + 1)
                v.tensor_tensor(out=s_lo[:, cut], in0=s[:, cut], in1=s_hi[:, cut].bitcast(F32), op=ALU.subtract).then_inc(v_slo, 1)

        @block.sync
        def _(sp):
            sp.dma_start(f[:, :], a["fT"].rearrange("(h p) t -> p h t", p=P)).then_inc(d_in, 16)
            sp.dma_start(x[:, :], a["xT"].rearrange("(h p) t -> p h t", p=P)).then_inc(d_in, 16)
            sp.dma_start(rw[:, :, :], a["router"].rearrange("(k p) e -> p k e", p=P)).then_inc(d_in, 16)
            for c in range(2):
                sp.dma_start(raw[:, c, :], a["w0"][c, :, :]).then_inc(d_raw[c], 16)
            sp.dma_start(w1raw[:, :, :], a["w1"].rearrange("(k p) n -> p k n", p=P)).then_inc(d_w1, 16)
            sp.dma_start(wg1[:, :, :], a["wg1"].rearrange("(k p) n -> p k n", p=P)).then_inc(d_w1, 16)
            sp.dma_start(w2in[:, :, :], a["w2"].rearrange("(k p) n -> p k n", p=P)).then_inc(d_w23, 16)
            sp.dma_start(b2in[:, :], a["b2"]).then_inc(d_w23, 16)
            sp.dma_start(wg3[:, :, :], a["wg3"].rearrange("(k p) n -> p k n", p=P)).then_inc(d_w23, 16)
            with sp.Fori(0, HALF_IT - 1) as i:
                for c in range(2):
                    sp.wait_ge(c_whi, 2 * i + c + 1)
                    sp.wait_ge(p_wlo, 2 * i + c + 1)
                    sp.dma_start(raw[:, c, :], a["w0"][bass.ds(2 * i + 2 + c, 1), :, :].rearrange("o p n -> (o p) n")).then_inc(d_raw[c], 16)
            sp.wait_ge(v_x, 4)
            sp.dma_start(w3a_raw, a["w3a"].rearrange("(k p) n -> p k n", p=P)).then_inc(d_w3, 16)
            sp.dma_start(w3b_raw, a["w3b"].rearrange("e p n -> p e n")).then_inc(d_w3, 16)
            for t in range(TILES):
                sp.wait_ge(c_nmx, t + 1)
                for r in range(2):
                    at = r * HROWS + (REP - 1) * HD
                    sp.dma_start(qs[at:at + 2, :, t * P:(t + 1) * P].bitcast(F32),
                                 nmx_t[r * HEADS:(r + 1) * HEADS, t % 2, :]).then_inc(d_nmx[t % 2], 16)
            for q in range(4):
                sp.wait_ge(v_x, 4 + TILES + 4 + q + 1)
                h, th = q // 2, q % 2
                sp.dma_start(out[h * P:(h + 1) * P, th * Q4:(th + 1) * Q4], x[:, q * Q4:(q + 1) * Q4]).then_inc(d_out, 16)
            sp.wait_ge(d_out, 64)

        @block.scalar
        def _(c):
            c.dma_start(temb[:, :, :], a["temb"].rearrange("(o b) t -> o b t", o=1).to_broadcast([P, B, TE])).then_inc(d_small, 16)
            c.dma_start(wcol[:, :, :], a["w"]).then_inc(d_small, 16)
            c.dma_start(ucol[:, :, :], a["u"]).then_inc(d_small, 16)
            c.wait_ge(v_tf, 1)
            c.activation(tf[:, :], tsum[:, :], ACT.Sigmoid).then_inc(c_tf, 1)
            c.activation(wexp[:, :, :], wcol[:, :, :], ACT.Exp).then_inc(c_tf, 1)
            c.wait_ge(c_tf, 2)
            c.activation(wdec[:, :, :], wexp[:, :, :], ACT.Exp, scale=-1.0).then_inc(c_tf, 1)
            c.wait_ge(v_cap, 1)
            for p in range(2):
                cut = slice(p * N, (p + 1) * N)
                c.activation(ek[:, cut], ek[:, cut], ACT.Exp).then_inc(c_ek, 1)
                c.wait_ge(v_cap, 2 + p)
                c.activation(mix[:, cut], mix[:, cut], ACT.Exp).then_inc(c_euk, 1)
            for l in range(1, LAYERS):
                c.wait_ge(p_cap, 2 * l)
                c.activation(mixed(l, 0, COLS), mixed(l, 0, COLS), ACT.Exp).then_inc(c_euk, 1)
            cond_act(c, 0)
            c.wait_ge(v_r, 2)
            c.activation(prob[:, :, 0:E0], prob[:, :, 0:E0], ACT.Exp).then_inc(c_r, 1)
            c.wait_ge(t_rout, 1)
            c.activation(rsg[:, :], bank[7][:, :].rearrange("p (t e) -> p t e", t=TILES)[:, :, E0], ACT.Exp, scale=-1.0).then_inc(c_r, 1)
            for j in range(2):
                c.wait_ge(t_rtr, j + 1)
                c.activation(gate_t[:, j * Q4:(j + 1) * Q4], bank[4 + j][0:2 * GATES, :], ACT.Copy).then_inc(c_gate, 1)
            c.wait_ge(d_raw[0], 16)
            c.activation(whi[0][:, :], raw[:, 0, :], ACT.Copy).then_inc(c_whi, 1)

            def body(i, first, last):
                for n in range(4):
                    ch, hf = n // 2, n % 2
                    if last and n == 1:
                        c.wait_ge(d_w1, 32)
                        c.activation(wq_hi[:, :, :], w1raw[:, :, 0:C], ACT.Copy).then_inc(c_w1, 1)
                        c.activation(wkv_hi[:, :, :], w1raw[:, :, C:3 * C], ACT.Copy).then_inc(c_w1, 1)
                    c.wait_ge(t_g, 4 * i + n + 1)
                    at_least(c, v_up, 4 * i + n - 1)
                    c.activation(sil[:, hf, :], bank[4][:, :], ACT.Silu).then_inc(c_sil, 1)
                    if hf == 1 and not (last and ch == 1):
                        at_least(c, t_down, 4 * i + 2 * ch)
                        c.wait_ge(d_raw[1 - ch], 16 * (i + 1 + ch))
                        c.activation(whi[1 - ch][:, :], raw[:, 1 - ch, :], ACT.Copy).then_inc(c_whi, 1)
                    c.wait_ge(v_hid, 4 * i + n + 1)
                    at_least(c, t_down, 4 * i + n - 1)
                    c.activation(hid_hi[:, hf, :], hid[:, hf, :], ACT.Copy).then_inc(c_hhi, 1)

            body(0, True, False)
            with c.Fori(1, HALF_IT - 1) as i:
                body(i, False, False)
            body(HALF_IT - 1, False, True)

            cond_act(c, 1)
            c.wait_ge(v_r, R0 + 2)
            c.activation(prob[:, :, 0:HEADS], prob[:, :, 0:HEADS], ACT.Exp).then_inc(c_r, 1)
            for n in range(4):
                c.wait_ge(t_qc, n + 1)
                c.activation(qc_hi[:, n % 2, (n // 2) * Q4:(n // 2 + 1) * Q4], bank[5 + n % 2][:, :], ACT.Copy).then_inc(c_qc, 1)

            def key_copy(t):
                c.wait_ge(t_kt, t + 1)
                c.activation(keys_t[:, t * P:(t + 1) * P], bank[6 + t % 2][:, 0:P], ACT.Copy).then_inc(c_kt, 1)

            for t in range(TILES):
                c.wait_ge(t_kv, t + 1)
                at_least(c, v_red, t - 1)
                c.activation(kvs[:, t % 2, :], bank[t % 2][:, :], ACT.Copy).then_inc(c_kv, 1)
                c.wait_ge(t_qs, 2 * t + 1)
                c.activation(qs[:, t % 4 * 2, (t // 4) * Q4:(t // 4 + 1) * Q4], bank[2][:, :], ACT.Copy).then_inc(c_qs, 1)
                if t >= 2:
                    key_copy(t - 2)
            key_copy(TILES - 2)
            key_copy(TILES - 1)

            def maxima(t):
                c.wait_ge(t_nmx, t + 1)
                at_least(c, d_nmx[t % 2], 32 * (t // 2))
                c.activation(nmx_t[:, t % 2, :], bank[6][0:2 * HEADS, 0:P], ACT.Copy).then_inc(c_nmx, 1)

            for t in range(AHEAD):
                maxima(t)
            for k in range(BLOCKS):
                for gi in range(GROUPS):
                    g = k * GROUPS + gi
                    c.wait_ge(t_b, g + 1)
                    kc, r, m, nm = BLIST[gi]
                    at_least(c, t_pv, k - 1)
                    c.activation(p_at(pexp, k, kc, r, m, nm), bank[2 + g % 2][:, :], ACT.Exp, scale=HD ** -0.5).then_inc(c_p, 1)
                    if gi == 1 and k >= 1 and k + AHEAD - 1 < TILES:
                        maxima(k + AHEAD - 1)
            cond_act(c, 2)
            c.wait_ge(d_w3, 32)
            c.activation(w3a_hi[:, :, :], w3a_raw, ACT.Copy).then_inc(c_w3, 1)
            c.activation(w3b_hi[:, :, :], w3b_raw, ACT.Copy).then_inc(c_w3, 1)
            for q in range(4):
                c.wait_ge(t_l2, q + 1)
                at_least(c, v_x, 4 + TILES + q - 1)
                c.activation(y2a[:, q % 2, :], bank[q][:, :], ACT.Copy, scale=scale2[:, 0:1]).then_inc(c_y2, 1)
                c.wait_ge(c_y2, q + 1)
                c.activation(y2b[:, q % 2, :], y2a[:, q % 2, :], ACT.Identity, bias=b2[:, q // 2:q // 2 + 1]).then_inc(c_y2b, 1)
            cond_act(c, 3)
            c.wait_ge(v_r, R3 + 3)
            c.activation(prob[:, :, 0:E3], prob[:, :, 0:E3], ACT.Exp).then_inc(c_r, 1)
            for j in range(2):
                c.wait_ge(t_rtr, 2 + j + 1)
                c.activation(gate3_t[:, j * Q4:(j + 1) * Q4], bank[4 + j][0:2 * E3, :], ACT.Copy).then_inc(c_gate, 1)
            for n in range(2 * E3):
                c.wait_ge(t_h3, n + 1)
                at_least(c, v_h3, n - 1)
                c.activation(act3[:, n % 2, :], bank[4 + n % 2][:, :], ACT.Relu).then_inc(c_act3, 1)
                c.wait_ge(v_h3, n + 1)
                at_least(c, t_d3, n - 1)
                c.activation(hid3_hi[:, n % 2, :], hid3[:, n % 2, :], ACT.Copy).then_inc(c_h3, 1)

        @block.vector
        def _(v):
            v.wait_ge(d_small, 48)
            v.tensor_reduce(out=tsum[:, :], in_=temb[:, :, :], op=ALU.add, axis=AX.X).then_inc(v_tf, 1)
            v.wait_ge(d_in, 48)
            v.tensor_scalar(out=ek[:, :], in0=f[:, :], scalar1=CAP, scalar2=None, op0=ALU.min).then_inc(v_cap, 1)
            for h in range(CH):
                cut = slice(h * N, (h + 1) * N)
                v.tensor_scalar(out=mix[:, cut], in0=f[:, cut], scalar1=ucol[:, 0, h:h + 1], scalar2=CAP,
                                op0=ALU.add, op1=ALU.min).then_inc(v_cap, 1)
            v.wait_ge(c_tf, 1)
            v.tensor_scalar(out=tdecay[:, :], in0=tf[:, :], scalar1=0.5, scalar2=0.5, op0=ALU.mult, op1=ALU.add).then_inc(v_tf, 1)
            for h in range(CH):
                v.tensor_scalar(out=tmul[:, h, :], in0=tf[:, :], scalar1=0.2, scalar2=0.8, op0=ALU.mult, op1=ALU.add).then_inc(v_tf, 1)
            v.wait_ge(c_tf, 3)
            v.wait_ge(v_tf, 4)
            for b in range(B):
                v.tensor_scalar(out=decay[:, :, :, b], in0=wdec[:, :, :], scalar1=tdecay[:, b:b + 1], scalar2=None,
                                op0=ALU.mult).then_inc(v_tf, 1)
            v.wait_ge(v_tf, 8)
            for k in range(PAIRS + 1):
                if k < PAIRS:
                    if k % 2 == 0:
                        v.wait_ge(c_ek, k // 2 + 1)
                    if k >= 2:
                        v.wait_ge(v_mix, 2 * (k - 1))
                    scans(v, 0, k, k % 2, True)
                    if k % 2 == 0:
                        v.wait_ge(p_ekv, k // 2 + 1)
                    scans(v, 0, k, k % 2, False)
                if k >= 1:
                    v.wait_ge(p_den, k)
                    finish_den(v, (k - 1) % 2, 0, k - 1)
                    finish_den(v, (k - 1) % 2, 1, k - 1)
                    v.wait_ge(v_den, 4 * k)
                    v.wait_ge(p_num, k)
                    finish_mix(v, 0, k - 1, (k - 1) % 2, k - 1)
            cond_dve(v, 0)
            v.wait_ge(t_rout, 1)
            lg = bank[7][:, :].rearrange("p (t e) -> p t e", t=TILES)[:, :, 0:E0]
            v.tensor_reduce(out=rmax[:, :], in_=lg, op=ALU.max, axis=AX.X).then_inc(v_r, 1)
            v.wait_ge(v_r, 1)
            v.tensor_tensor(out=prob[:, :, 0:E0], in0=lg, in1=rmax[:, :].unsqueeze(2).to_broadcast([P, TILES, E0]),
                            op=ALU.subtract).then_inc(v_r, 1)
            v.memset(prob[:, :, E0:EP], -1.0).then_inc(v_r, 1)
            v.wait_ge(c_r, 1)
            v.tensor_reduce(out=rsum[:, :], in_=prob[:, :, 0:E0], op=ALU.add, axis=AX.X).then_inc(v_r, 1)
            v.wait_ge(v_r, 4)
            v.reciprocal(rsum[:, :], rsum[:, :]).then_inc(v_r, 1)
            v.wait_ge(v_r, 5)
            v.tensor_tensor(out=prob[:, :, 0:E0], in0=prob[:, :, 0:E0],
                            in1=rsum[:, :].unsqueeze(2).to_broadcast([P, TILES, E0]), op=ALU.mult).then_inc(v_r, 1)
            v.wait_ge(v_r, 6)
            W = E0 + 8 - K0
            for t in range(TILES):
                v.max(out=top8[:, t, :], in_=prob[:, t, 0:W]).then_inc(v_r, 1)
            v.wait_ge(v_r, 14)
            v.memset(top8[:, :, K0:8], -1.0).then_inc(v_r, 1)
            v.wait_ge(v_r, 15)
            for t in range(TILES):
                v.match_replace(out=repl[:, t, 0:W], in_to_replace=top8[:, t, :], in_values=prob[:, t, 0:W],
                                imm_value=-2.0).then_inc(v_r, 1)
            v.tensor_reduce(out=rsum[:, :], in_=top8[:, :, 0:K0], op=ALU.add, axis=AX.X).then_inc(v_r, 1)
            v.wait_ge(v_r, 24)
            v.tensor_scalar(out=rsum[:, :], in0=rsum[:, :], scalar1=1e-9, scalar2=None, op0=ALU.max).then_inc(v_r, 1)
            v.tensor_tensor(out=repl[:, :, 0:E0], in0=repl[:, :, 0:E0], in1=prob[:, :, 0:E0], op=ALU.not_equal).then_inc(v_r, 1)
            v.wait_ge(v_r, 26)
            v.reciprocal(rsum[:, :], rsum[:, :]).then_inc(v_r, 1)
            v.tensor_tensor(out=prob[:, :, 0:E0], in0=prob[:, :, 0:E0], in1=repl[:, :, 0:E0], op=ALU.mult).then_inc(v_r, 1)
            v.wait_ge(c_r, 2)
            v.tensor_scalar(out=rsg[:, :], in0=rsg[:, :], scalar1=1.0, scalar2=None, op0=ALU.add).then_inc(v_r, 1)
            v.wait_ge(v_r, 29)
            v.tensor_tensor(out=gates[:, :, 0:E0], in0=prob[:, :, 0:E0],
                            in1=rsum[:, :].unsqueeze(2).to_broadcast([P, TILES, E0]), op=ALU.mult).then_inc(v_r, 1)
            v.reciprocal(gates[:, :, E0], rsg[:, :]).then_inc(v_r, 1)
            v.wait_ge(v_r, 31)
            v.tensor_copy(gsplit[:, :, 0, :], gates[:, :, :]).then_inc(v_r, 1)
            v.wait_ge(v_r, 32)
            v.tensor_tensor(out=gsplit[:, :, 1, :], in0=gates[:, :, :], in1=gsplit[:, :, 0, :].bitcast(F32),
                            op=ALU.subtract).then_inc(v_r, 1)

            def body(i, wkv):
                for n in range(4):
                    ch, hf = n // 2, n % 2
                    v.wait_ge(t_u, 4 * i + n + 1)
                    v.wait_ge(c_sil, 4 * i + n + 1)
                    v.tensor_tensor(out=up[:, :], in0=bank[5][:, :], in1=sil[:, hf, :], op=ALU.mult).then_inc(v_up, 1)
                    v.wait_ge(t_cb, 4 * i + n + 1)
                    v.wait_ge(v_up, 4 * i + n + 1)
                    v.tensor_tensor(out=hid[:, hf, :], in0=bank[6][:, :], in1=up[:, :], op=ALU.mult).then_inc(v_hid, 1)
                    if wkv:
                        l, p, k = wkv
                        if n == 0:
                            scans(v, l, p, 0, True)
                        elif n == 1:
                            scans(v, l, p, 0, False)
                        elif n == 2:
                            v.wait_ge(p_den, k + 1)
                            finish_den(v, 0, 0, k)
                        else:
                            finish_den(v, 0, 1, k)
                            v.wait_ge(v_den, 4 * (k + 1))
                            v.wait_ge(p_num, k + 1)
                            finish_mix(v, l, p, 0, k)
                    v.wait_ge(c_hhi, 4 * i + n + 1)
                    at_least(v, t_down, 4 * i + n - 1)
                    v.tensor_tensor(out=hid_lo[:, hf, :], in0=hid[:, hf, :], in1=hid_hi[:, hf, :].bitcast(F32),
                                    op=ALU.subtract).then_inc(v_hlo, 1)

            body(0, None)
            with v.Fori(1, LAYERS) as l:
                for p in range(PAIRS):
                    body(PAIRS * l + p + 1 - PAIRS, (l, p, PAIRS * l + p))
            for i in range(1 + PAIRS * (LAYERS - 1), HALF_IT):
                body(i, None)
            v.wait_ge(t_down, 4 * HALF_IT)
            for q in range(4):
                cut = slice(q * Q4, (q + 1) * Q4)
                v.tensor_tensor(out=x[:, cut], in0=bank[q][:, :], in1=x[:, cut], op=ALU.add).then_inc(v_x, 1)

            cond_dve(v, 1)
            v.wait_ge(t_rout, 2)
            lg = bank[4][:, :].rearrange("p (t e) -> p t e", t=TILES)[:, :, 0:HEADS]
            v.tensor_reduce(out=rmax[:, :], in_=lg, op=ALU.max, axis=AX.X).then_inc(v_r, 1)
            v.wait_ge(v_r, R0 + 1)
            v.tensor_tensor(out=prob[:, :, 0:HEADS], in0=lg, in1=rmax[:, :].unsqueeze(2).to_broadcast([P, TILES, HEADS]),
                            op=ALU.subtract).then_inc(v_r, 1)
            v.memset(prob[:, :, HEADS:HEADS + 8], -1.0).then_inc(v_r, 1)
            v.wait_ge(c_r, 3)
            v.tensor_reduce(out=rsum[:, :], in_=prob[:, :, 0:HEADS], op=ALU.add, axis=AX.X).then_inc(v_r, 1)
            v.wait_ge(v_r, R0 + 4)
            v.reciprocal(rsum[:, :], rsum[:, :]).then_inc(v_r, 1)
            v.wait_ge(v_r, R0 + 5)
            v.tensor_tensor(out=prob[:, :, 0:HEADS], in0=prob[:, :, 0:HEADS],
                            in1=rsum[:, :].unsqueeze(2).to_broadcast([P, TILES, HEADS]), op=ALU.mult).then_inc(v_r, 1)
            v.wait_ge(v_r, R0 + 6)
            v.tensor_reduce(out=rmax[:, :], in_=prob[:, :, 0:HEADS], op=ALU.max, axis=AX.X).then_inc(v_r, 1)
            v.memset(top8[:, :, 1:8], -1.0).then_inc(v_r, 1)
            v.wait_ge(v_r, R0 + 8)
            v.tensor_copy(top8[:, :, 0], rmax[:, :]).then_inc(v_r, 1)
            v.wait_ge(v_r, R0 + 9)
            for t in range(TILES):
                v.match_replace(out=repl[:, t, 0:HEADS + 7], in_to_replace=top8[:, t, :],
                                in_values=prob[:, t, 0:HEADS + 7], imm_value=-2.0).then_inc(v_k1, 1)
            v.wait_ge(v_k1, TILES)
            v.tensor_tensor(out=repl[:, :, 0:HEADS], in0=repl[:, :, 0:HEADS], in1=prob[:, :, 0:HEADS],
                            op=ALU.not_equal).then_inc(v_k1, 1)
            v.wait_ge(v_k1, TILES + 1)
            v.wait_ge(p_const, 4)
            for n in range(4):
                cut = slice((n // 2) * Q4, (n // 2 + 1) * Q4)
                v.wait_ge(c_qc, n + 1)
                v.tensor_tensor(out=qc_lo[:, n % 2, cut], in0=bank[5 + n % 2][:, :], in1=qc_hi[:, n % 2, cut].bitcast(F32),
                                op=ALU.subtract).then_inc(v_qc, 1)
            for t in range(TILES):
                u = t % 2
                v.wait_ge(t_qs, 2 * t + 2)
                v.tensor_copy(qs[:, t % 4 * 2 + 1, (t // 4) * Q4:(t // 4 + 1) * Q4], bank[3][:, :]).then_inc(v_qs, 1)
                v.wait_ge(p_kv, t + 1)
                v.tensor_reduce(out=kv1[:, u, :, :], in_=kvs[:, u, :].rearrange("p (a h d) -> p a d h", a=2, h=HEADS),
                                op=ALU.add, axis=AX.X).then_inc(v_red, 1)
                v.wait_ge(v_red, t + 1)
                at_least(v, t_kt, t - 1)
                v.tensor_copy(kst[:, u, :, 0:REP:2, :],
                              kv1[:, u, 0, :].unsqueeze(1).unsqueeze(1).to_broadcast([P, 2, 2, HD])).then_inc(v_kst, 1)
                v.tensor_scalar(out=vals[:, t, VGAP:VGAP + HD], in0=kv1[:, u, 1, :], scalar1=rmax[:, t:t + 1], scalar2=None,
                                op0=ALU.mult).then_inc(v_val, 1)
                v.wait_ge(v_kst, 2 * t + 1)
                v.tensor_tensor(out=kst[:, u, :, 1, :], in0=kv1[:, u, 0, :].unsqueeze(1).to_broadcast([P, 2, HD]),
                                in1=kst[:, u, :, 0, :].bitcast(F32), op=ALU.subtract).then_inc(v_kst, 1)
            def maxima_of(t, gi):
                r, m, nm = ALIST[t % 2][gi]
                v.wait_ge(t_a, a_before(t) + gi + 1)
                v.tensor_reduce(out=nmax[:, t % 2, r, m:m + nm], in_=bank[4 + r][:, :].rearrange("p (m k) -> p m k", m=nm),
                                op=ALU.max, axis=AX.X, negate=True).then_inc(v_nmax, 1)

            def maxima_parts(t):
                v.wait_ge(v_nmax, a_before(t + 1))
                at_least(v, t_nmx, t - 1)
                v.tensor_copy(nmx[:, t % 2, :, 0, :], nmax[:, t % 2, :, :]).then_inc(v_nmx, 1)
                v.wait_ge(v_nmx, 2 * t + 1)
                v.tensor_tensor(out=nmx[:, t % 2, :, 1, :], in0=nmax[:, t % 2, :, :], in1=nmx[:, t % 2, :, 0, :].bitcast(F32),
                                op=ALU.subtract).then_inc(v_nmx, 1)

            def block_end(k):
                acc = bank[k % 2]
                v.wait_ge(t_pv, k + 1)
                v.reciprocal(rden[:, :], acc[P // 2:P, :]).then_inc(v_rden, 1)
                v.wait_ge(v_rden, k + 1)
                for j in range(2):
                    v.tensor_tensor(out=yt[j * P // 2:(j + 1) * P // 2, k % 2, :], in0=acc[0:P // 2, j * T:(j + 1) * T],
                                    in1=rden[:, j * T:(j + 1) * T], op=ALU.mult).then_inc(v_y, 1)
                cut = slice((k % 2) * N + (k // 2) * T, (k % 2) * N + (k // 2 + 1) * T)
                v.wait_ge(v_y, 2 * k + 2)
                v.tensor_tensor(out=x[:, cut], in0=yt[:, k % 2, :], in1=x[:, cut], op=ALU.add).then_inc(v_x, 1)

            for t in range(AHEAD):
                for gi in range(len(ALIST[t % 2])):
                    maxima_of(t, gi)
                maxima_parts(t)
            for k in range(BLOCKS + 2):
                for gi in range(GROUPS):
                    if k + AHEAD < TILES:
                        for ai in ASTEPS[(k + AHEAD) % 2][gi]:
                            maxima_of(k + AHEAD, ai)
                    if gi == 1 and k >= 2:
                        block_end(k - 2)
                if k + AHEAD < TILES:
                    maxima_parts(k + AHEAD)

            v.wait_ge(d_w23, 48)
            for k in range(CH):
                v.tensor_reduce(out=peak[:, 4 + k:5 + k], in_=w2in[:, k, :], op=ALU.max, axis=AX.X,
                                apply_absolute_value=True).then_inc(v_peak, 1)
            v.tensor_copy(b2[:, :], b2in[:, :]).then_inc(v_wq2, 1)
            cond_dve(v, 2)
            v.wait_ge(v_peak, 6)
            v.tensor_reduce(out=peak2[:, 0:1], in_=peak[:, 0:4], op=ALU.max, axis=AX.X).then_inc(v_peak, 1)
            v.tensor_reduce(out=peak2[:, 1:2], in_=peak[:, 4:6], op=ALU.max, axis=AX.X).then_inc(v_peak, 1)
            v.wait_ge(p_peak, 1)
            v.tensor_scalar(out=peakall[:, :], in0=peakall[:, :], scalar1=1e-6, scalar2=None, op0=ALU.max).then_inc(v_peak, 1)
            v.wait_ge(v_peak, 9)
            v.reciprocal(peakinv[:, :], peakall[:, :]).then_inc(v_peak, 1)
            v.tensor_tensor(out=scale2[:, :], in0=peakall[:, 0:1], in1=peakall[:, 1:2], op=ALU.mult).then_inc(v_peak, 1)
            v.wait_ge(v_peak, 11)
            v.tensor_scalar(out=w2q[:, :, :], in0=w2in[:, :, :], scalar1=peakinv[:, 1:2], scalar2=None,
                            op0=ALU.mult, saturate=False).then_inc(v_wq2, 1)
            for q in range(4):
                cut = slice(q * Q4, (q + 1) * Q4)
                v.tensor_scalar(out=xq[:, cut], in0=s[:, cut], scalar1=peakinv[:, 0:1], scalar2=None,
                                op0=ALU.mult, saturate=False).then_inc(v_xq, 1)
            for q in range(4):
                cut = slice(q * Q4, (q + 1) * Q4)
                v.wait_ge(c_y2b, q + 1)
                v.tensor_tensor(out=x[:, cut], in0=x[:, cut], in1=y2b[:, q % 2, :], op=ALU.add).then_inc(v_x, 1)

            cond_dve(v, 3)
            v.memset(prob[:, :, E3:E3 + 4], LOW).then_inc(v_r, 1)
            v.wait_ge(t_rout, 3)
            lg = bank[7][:, :].rearrange("p (t e) -> p t e", t=TILES)[:, :, 0:E3]
            v.tensor_copy(prob[:, :, 0:E3], lg).then_inc(v_r, 1)
            v.wait_ge(v_r, R3 + 2)
            for t in range(TILES):
                v.max(out=top8[:, t, :], in_=prob[:, t, 0:E3 + 4]).then_inc(v_k1, 1)
            v.wait_ge(v_k1, 2 * TILES + 1)
            v.tensor_copy(rmax[:, :], top8[:, :, 0]).then_inc(v_k1, 1)
            v.memset(top8[:, :, K3:8], LOW).then_inc(v_k1, 1)
            v.wait_ge(v_k1, 2 * TILES + 3)
            for t in range(TILES):
                v.match_replace(out=repl[:, t, 0:E3 + 4], in_to_replace=top8[:, t, :],
                                in_values=prob[:, t, 0:E3 + 4], imm_value=1.1 * LOW).then_inc(v_k1, 1)
            v.wait_ge(v_k1, 3 * TILES + 3)
            v.tensor_tensor(out=repl[:, :, 0:E3], in0=repl[:, :, 0:E3], in1=prob[:, :, 0:E3], op=ALU.not_equal).then_inc(v_k1, 1)
            v.wait_ge(v_k1, 3 * TILES + 4)
            v.tensor_tensor(out=prob[:, :, 0:E3], in0=prob[:, :, 0:E3],
                            in1=rmax[:, :].unsqueeze(2).to_broadcast([P, TILES, E3]), op=ALU.subtract).then_inc(v_r, 1)
            v.wait_ge(c_r, 4)
            v.tensor_tensor(out=prob[:, :, 0:E3], in0=prob[:, :, 0:E3], in1=repl[:, :, 0:E3], op=ALU.mult).then_inc(v_r, 1)
            v.wait_ge(v_r, R3 + 4)
            v.tensor_reduce(out=rsum[:, :], in_=prob[:, :, 0:E3], op=ALU.add, axis=AX.X).then_inc(v_r, 1)
            v.wait_ge(v_r, R3 + 5)
            v.reciprocal(rsum[:, :], rsum[:, :]).then_inc(v_r, 1)
            v.wait_ge(v_r, R3 + 6)
            v.tensor_tensor(out=prob[:, :, 0:E3], in0=prob[:, :, 0:E3],
                            in1=rsum[:, :].unsqueeze(2).to_broadcast([P, TILES, E3]), op=ALU.mult).then_inc(v_r, 1)
            v.wait_ge(v_r, R3 + 7)
            v.tensor_scalar(out=gates[:, :, 0:E3], in0=prob[:, :, 0:E3], scalar1=1.0, scalar2=None, op0=ALU.add).then_inc(v_r, 1)
            v.wait_ge(v_r, R3 + 8)
            v.tensor_tensor(out=gates[:, :, 0:E3], in0=gates[:, :, 0:E3], in1=prob[:, :, 0:E3], op=ALU.subtract).then_inc(v_r, 1)
            v.wait_ge(v_r, R3 + 9)
            v.tensor_tensor(out=gates[:, :, 0:E3], in0=gates[:, :, 0:E3], in1=repl[:, :, 0:E3], op=ALU.mult).then_inc(v_r, 1)
            v.wait_ge(v_r, R3 + 10)
            v.tensor_copy(gsplit3[:, :, 0, :], gates[:, :, 0:E3]).then_inc(v_r, 1)
            v.wait_ge(v_r, R3 + 11)
            v.tensor_tensor(out=gsplit3[:, :, 1, :], in0=gates[:, :, 0:E3], in1=gsplit3[:, :, 0, :].bitcast(F32),
                            op=ALU.subtract).then_inc(v_r, 1)
            for n in range(2 * E3):
                v.wait_ge(c_act3, n + 1)
                v.wait_ge(t_cb3, n + 1)
                v.tensor_tensor(out=hid3[:, n % 2, :], in0=bank[6 + n % 2][:, :], in1=act3[:, n % 2, :], op=ALU.mult).then_inc(v_h3, 1)
                v.wait_ge(c_h3, n + 1)
                at_least(v, t_d3, n - 1)
                v.tensor_tensor(out=hid3_lo[:, n % 2, :], in0=hid3[:, n % 2, :], in1=hid3_hi[:, n % 2, :].bitcast(F32),
                                op=ALU.subtract).then_inc(v_h3lo, 1)
            v.wait_ge(t_d3, 2 * E3)
            for q in range(4):
                cut = slice(q * Q4, (q + 1) * Q4)
                v.tensor_tensor(out=x[:, cut], in0=bank[q][:, :], in1=x[:, cut], op=ALU.add).then_inc(v_x, 1)

        @block.gpsimd
        def _(g):
            g.memset(ident[:, :], 0.0).then_inc(p_id, 1)
            g.dma_start(spread[:, :, :, :], a["spread"]).then_inc(d_spread, 16)
            g.wait_ge(p_id, 1)
            g.affine_select(out=ident[:, :], in_=ident[:, :], compare_op=ALU.not_equal, fill=1.0, base=0,
                            pattern=[[-1, P]], channel_multiplier=1).then_inc(p_id, 1)
            g.wait_ge(c_ek, 1)
            g.tensor_tensor(out=ekv[:, 0:N], in0=ek[:, 0:N], in1=f[:, 0:N], op=ALU.mult).then_inc(p_ekv, 1)
            for k in range(PAIRS):
                if k == 2:
                    g.wait_ge(c_ek, 2)
                    g.tensor_tensor(out=ekv[:, N:2 * N], in0=ek[:, N:2 * N], in1=f[:, N:2 * N], op=ALU.mult).then_inc(p_ekv, 1)
                g.wait_ge(c_euk, k // 2 + 1)
                if k >= 2:
                    g.wait_ge(v_mix, 2 * (k - 1))
                pool_dk(g, 0, k, k % 2)
                pool_dkv(g, k, k % 2, k)
                pool_den(g, k % 2, k)
                pool_num(g, k % 2, k)
            for l in range(1, LAYERS):
                for h in range(CH):
                    cut = slice(h * N, (h + 1) * N)
                    g.tensor_scalar(out=mixed(l, h * N, N), in0=f[:, cut], scalar1=ucol[:, l, h:h + 1], scalar2=CAP,
                                    op0=ALU.add, op1=ALU.min).then_inc(p_cap, 1)

            def split(c, slot, done, loads):
                g.wait_ge(d_raw[slot], 16 * loads)
                g.wait_ge(c_whi, c + 1)
                at_least(g, t_down, done)
                g.tensor_tensor(out=wlo[slot][:, :], in0=raw[:, slot, 0:WCOLS], in1=whi[slot][:, 0:WCOLS].bitcast(F32),
                                op=ALU.subtract).then_inc(p_wlo, 1)

            split(0, 0, 0, 1)

            def body(i, wkv, last=False):
                if wkv:
                    l, p, k = wkv
                    g.wait_ge(v_mix, 2 * k)
                    pool_dk(g, l, p, 0)
                    pool_dkv(g, p, 0, k)
                split(2 * i + 1, 1, 4 * i, i + 1)
                if last:
                    g.wait_ge(c_w1, 1)
                    g.tensor_tensor(out=wq_lo[:, :, :], in0=w1raw[:, :, 0:C], in1=wq_hi[:, :, :].bitcast(F32),
                                    op=ALU.subtract).then_inc(p_w1, 1)
                    g.wait_ge(c_w1, 2)
                    g.tensor_tensor(out=wkv_lo[:, :, :], in0=w1raw[:, :, C:3 * C], in1=wkv_hi[:, :, :].bitcast(F32),
                                    op=ALU.subtract).then_inc(p_w1, 1)
                if wkv:
                    pool_den(g, 0, k)
                    pool_num(g, 0, k)
                if not last:
                    split(2 * i + 2, 0, 4 * i + 2, i + 2)

            body(0, None)
            with g.Fori(1, LAYERS) as l:
                g.wait_ge(c_euk, l + 2)
                for p in range(PAIRS):
                    body(PAIRS * l + p + 1 - PAIRS, (l, p, PAIRS * l + p))
            for i in range(1 + PAIRS * (LAYERS - 1), HALF_IT):
                body(i, None, i == HALF_IT - 1)
            g.wait_ge(v_x, 4)
            g.tensor_copy(identb[:, :], ident[:, :]).then_inc(p_const, 1)
            g.memset(negmask[:, :], 0.0).then_inc(p_id, 1)
            g.wait_ge(p_id, 3)
            g.affine_select(out=negmask[:, :], in_=negmask[:, :], compare_op=ALU.is_ge, fill=-1e30, base=0,
                            pattern=[[-1, P]], channel_multiplier=1).then_inc(p_const, 1)
            g.memset(kst[:, :, :, REP - 1, :].bitcast(F32), 0.0).then_inc(p_id, 1)
            g.wait_ge(p_id, 4)
            g.memset(kst[:, :, :, REP - 1, 0:2].bitcast(F32), 1.0).then_inc(p_const, 1)
            g.memset(vals[:, :, :], 0.0).then_inc(p_id, 1)
            g.wait_ge(p_id, 5)
            g.memset(vals[:, :, 2 * VGAP + HD:2 * VGAP + 2 * HD], 1.0).then_inc(p_const, 1)
            for t in range(TILES):
                g.wait_ge(c_kv, t + 1)
                if t == 0:
                    g.wait_ge(v_k1, TILES + 1)
                kv4 = kvs[:, t % 2, :].rearrange("p (a h d) -> p a h d", a=2, h=HEADS)
                g.tensor_tensor(out=kv4, in0=kv4,
                                in1=repl[:, t, 0:HEADS].unsqueeze(1).unsqueeze(3).to_broadcast([P, 2, HEADS, HD]),
                                op=ALU.mult).then_inc(p_kv, 1)
            for i in range(BLOCKS * GROUPS):
                kc, r, m, nm = BLIST[i % GROUPS]
                g.wait_ge(c_p, i + 1)
                d = p_at(pexp, i // GROUPS, kc, r, m, nm).rearrange("p (m q) -> p m q", m=nm)[:, :, 0:P]
                g.affine_select(out=d, in_=d, compare_op=ALU.is_ge, fill=0.0, base=0,
                                pattern=[[0, 2 if kc == 0 else 4], [1, P]], channel_multiplier=-1).then_inc(p_sel, 1)
            g.wait_ge(v_peak, 8)
            g.partition_all_reduce(peakall[:, :], peak2[:, :], channels=P, reduce_op=bass.bass_isa.ReduceOp.max).then_inc(p_peak, 1)
            g.dma_start(sel3[:, :, :], a["sel3"]).then_inc(d_sel3, 16)
            g.wait_ge(c_w3, 1)
            g.tensor_tensor(out=w3a_lo[:, :, :], in0=w3a_raw, in1=w3a_hi[:, :, :].bitcast(F32), op=ALU.subtract).then_inc(p_w3, 1)
            g.wait_ge(c_w3, 2)
            g.tensor_tensor(out=w3b_lo[:, :, :], in0=w3b_raw, in1=w3b_hi[:, :, :].bitcast(F32), op=ALU.subtract).then_inc(p_w3, 1)

        @block.tensor
        def _(t):
            mm = nc.tensor.matmul
            t.wait_ge(v_s, 4)
            rv = bank[7][:, :].rearrange("p (t e) -> p t e", t=TILES)
            for i in range(TILES):
                for k in range(CH):
                    last = mm(rv[:, i, 0:GATES], s[:, k * N + i * P:k * N + (i + 1) * P], rw[:, k, :],
                              start=(k == 0), stop=(k == CH - 1))
            last.then_inc(t_rout, 1)
            t.wait_ge(p_id, 2)
            t.wait_ge(v_r, 33)
            for j in range(2):
                for i in range(4):
                    last = nc.tensor.transpose(bank[4 + j][0:2 * GATES, i * P:(i + 1) * P],
                                               gsplit[:, 4 * j + i, :, :].rearrange("p a e -> p (a e)").bitcast(F32), ident[:, :])
                last.then_inc(t_rtr, 1)
            t.wait_ge(v_slo, 4)
            t.wait_ge(c_gate, 2)

            def down(slot, hf, n_done, first, last):
                t.wait_ge(c_hhi, n_done)
                t.wait_ge(v_hlo, n_done)
                for ch in range(CH):
                    cols = slice(2 * CH * P + ch * P, 2 * CH * P + (ch + 1) * P)
                    o = bank[2 * ch + hf][:, :]
                    mm(o, whi[slot][:, cols], hid_hi[:, hf, :], start=first, stop=False)
                    mm(o, whi[slot][:, cols], hid_lo[:, hf, :], start=False, stop=False)
                    m = mm(o, wlo[slot][:, cols], hid_hi[:, hf, :], start=False, stop=last)
                m.then_inc(t_down, 1)

            def body(i, first, final=False):
                for n in range(4):
                    ch, hf = n // 2, n % 2
                    if hf == 0:
                        t.wait_ge(c_whi, 2 * i + ch + 1)
                        t.wait_ge(p_wlo, 2 * i + ch + 1)
                    for part, (bk, free, done) in enumerate(((4, c_sil, t_g), (5, v_up, t_u))):
                        at_least(t, free, 4 * i + n)
                        for k in range(CH):
                            w = slice((k * 2 + part) * P, (k * 2 + part + 1) * P)
                            r = slice(k * N + hf * Q4, k * N + (hf + 1) * Q4)
                            mm(bank[bk][:, :], whi[ch][:, w], s_hi[:, r], start=(k == 0), stop=False)
                            mm(bank[bk][:, :], whi[ch][:, w], s_lo[:, r], start=False, stop=False)
                            m = mm(bank[bk][:, :], wlo[ch][:, w], s_hi[:, r], start=False, stop=(k == CH - 1))
                        m.then_inc(done, 1)
                    at_least(t, v_hid, 4 * i + n)
                    mm(bank[6][:, :], whi[ch][0:2 * GATES, WCOLS:RAWCOLS], gate_t[:, hf * Q4:(hf + 1) * Q4],
                       start=True, stop=True).then_inc(t_cb, 1)
                    if not (first and n == 0):
                        down((ch - 1 + hf) % 2, 1 - hf, 4 * i + n, first and n in (1, 2), final and n == 3)

            body(0, True)
            with t.Fori(1, HALF_IT - 1) as i:
                body(i, False)
            body(HALF_IT - 1, False, True)
            down(1, 1, 4 * HALF_IT, False, True)

            def router(bk, w, width, n_s):
                t.wait_ge(v_s, n_s)
                r = bank[bk][:, :].rearrange("p (t e) -> p t e", t=TILES)
                for i in range(TILES):
                    for k in range(CH):
                        m = mm(r[:, i, 0:width], s[:, k * N + i * P:k * N + (i + 1) * P], w[:, k, :],
                               start=(k == 0), stop=(k == CH - 1))
                m.then_inc(t_rout, 1)

            def key_rows(i):
                t.wait_ge(v_kst, 2 * i + 2)
                at_least(t, c_kt, i - 1)
                nc.tensor.transpose(bank[6 + i % 2][:, 0:P], kst[:, i % 2, :, :, :].rearrange("p r a d -> p (r a d)").bitcast(F32),
                                    ident[:, :]).then_inc(t_kt, 1)

            t.wait_ge(d_w1, 32)
            router(4, wg1, HEADS, 8)
            t.wait_ge(c_w1, 2)
            t.wait_ge(p_w1, 2)
            t.wait_ge(v_slo, 8)
            for n in range(4):
                at_least(t, v_qc, n - 1)
                w = slice((n % 2) * P, (n % 2 + 1) * P)
                for k in range(CH):
                    r = slice(k * N + (n // 2) * Q4, k * N + (n // 2 + 1) * Q4)
                    mm(bank[5 + n % 2][:, :], wq_hi[:, k, w], s_hi[:, r], start=(k == 0), stop=False)
                    mm(bank[5 + n % 2][:, :], wq_hi[:, k, w], s_lo[:, r], start=False, stop=False)
                    last = mm(bank[5 + n % 2][:, :], wq_lo[:, k, w], s_hi[:, r], start=False, stop=(k == CH - 1))
                last.then_inc(t_qc, 1)
            t.wait_ge(d_spread, 16)
            for i in range(TILES):
                at_least(t, c_kv, i - 1)
                for k in range(CH):
                    r = slice(k * N + i * P, k * N + (i + 1) * P)
                    mm(bank[i % 2][:, :], s_hi[:, r], wkv_hi[:, k, :], start=(k == 0), stop=False)
                    mm(bank[i % 2][:, :], s_lo[:, r], wkv_hi[:, k, :], start=False, stop=False)
                    last = mm(bank[i % 2][:, :], s_hi[:, r], wkv_lo[:, k, :], start=False, stop=(k == CH - 1))
                last.then_inc(t_kv, 1)
                if i == 0:
                    t.wait_ge(v_qc, 4)
                for j in range(2):
                    m = i % 4 * 2 + j
                    cols = slice((i // 4) * Q4, (i // 4 + 1) * Q4)
                    at_least(t, (c_qs, v_qs)[j], i)
                    mm(bank[2 + j][:, :], spread[:, 0, m % 4, :], qc_hi[:, m // 4, cols], start=True, stop=False)
                    mm(bank[2 + j][:, :], spread[:, 1, m % 4, :], qc_lo[:, m // 4, cols], start=False, stop=True).then_inc(t_qs, 1)
                if i >= 1:
                    key_rows(i - 1)
            key_rows(TILES - 1)
            t.wait_ge(c_kt, TILES)
            t.wait_ge(c_qs, TILES)
            t.wait_ge(v_qs, TILES)
            t.wait_ge(p_const, 2)

            def scores_for_maxima(i, gi):
                r, m0, nm = ALIST[i % 2][gi]
                kw = P * (i % 2 + 1)
                bk = bank[4 + r][:, :].rearrange("p (m k) -> p m k", m=nm)
                at_least(t, v_nmax, a_before(i) + gi - 1)
                mm(bk[:, :, kw - P:kw], identb[:, :], negmask[:, :].unsqueeze(1).to_broadcast([P, nm, P]),
                   start=True, stop=False, skip_group_check=True)
                rows = slice(r * HROWS, (r + 1) * HROWS)
                for m in range(m0, m0 + nm):
                    last = mm(bk[:, m - m0, :], qs[rows, m, i * P:(i + 1) * P], keys_t[rows, (i // 2) * T:(i // 2) * T + kw],
                              start=False, stop=(m == m0 + nm - 1), skip_group_check=True)
                last.then_inc(t_a, 1)

            def maxima_rows(i):
                t.wait_ge(v_nmx, 2 * i + 2)
                at_least(t, c_nmx, i)
                nc.tensor.transpose(bank[6][0:2 * HEADS, 0:P], nmx[:, i % 2, :, :, :].rearrange("p r a m -> p (r a m)").bitcast(F32),
                                    ident[:, :]).then_inc(t_nmx, 1)

            def scores(g):
                k = g // GROUPS
                kc, r, m, nm = BLIST[g % GROUPS]
                m0 = (k % 2) * 4 + m
                at = (k // 2) * T
                rows = slice(r * HROWS, (r + 1) * HROWS)
                at_least(t, c_p, g - 1)
                mm(bank[2 + g % 2][:, :].rearrange("p (m q) -> p m q", m=nm), keys_t[rows, at + kc * P:at + (kc + 1) * P],
                   qs[rows, m0:m0 + nm, at + kc * P:at + T], start=True, stop=True).then_inc(t_b, 1)

            def times_values(k, part):
                jobs = [(0, 0), (1, 0), (1, 1), (1, 2), (1, 3), (0, 1), (0, 2), (0, 3)]
                if part == 0:
                    t.wait_ge(p_sel, GROUPS * (k + 1))
                    t.wait_ge(v_val, 2 * (k // 2) + 2)
                    t.wait_ge(p_const, 4)
                    at_least(t, v_y, 2 * (k - 1))
                for n in range(part * len(jobs) // 5, (part + 1) * len(jobs) // 5):
                    kc, j = jobs[n]
                    w = T - kc * P
                    weights = p_at(pexp, k, kc, j % 2, 0, 4).rearrange("p (g m q) -> p g m q", g=2, m=2)[:, :, j // 2, :]
                    values = vals[:, 2 * (k // 2) + kc, VGAP - j * HD:VGAP - j * HD + P]
                    last = mm(bank[k % 2][:, :].rearrange("p (g q) -> p g q", g=2)[:, :, T - w:T], values, weights,
                              start=(n == 0), stop=(n == len(jobs) - 1), skip_group_check=True)
                if part == 4:
                    last.then_inc(t_pv, 1)

            for i in range(AHEAD):
                for gi in range(len(ALIST[i % 2])):
                    scores_for_maxima(i, gi)
                if i >= 1:
                    maxima_rows(i - 1)
            maxima_rows(AHEAD - 1)
            for k in range(BLOCKS + 1):
                if k % 2 == 0 and k < BLOCKS:
                    t.wait_ge(d_nmx[0], 32 * (k // 2 + 1))
                    t.wait_ge(d_nmx[1], 32 * (k // 2 + 1))
                for gi in range(GROUPS):
                    if k < BLOCKS:
                        scores(k * GROUPS + gi)
                    if k + AHEAD < TILES:
                        for ai in ASTEPS[(k + AHEAD) % 2][gi]:
                            scores_for_maxima(k + AHEAD, ai)
                    if gi == 1 and k >= 1 and k + AHEAD - 1 < TILES:
                        maxima_rows(k + AHEAD - 1)
                    if gi >= 1 and 1 <= k <= BLOCKS:
                        times_values(k - 1, gi - 1)

            t.wait_ge(v_wq2, 2)
            for q in range(4):
                t.wait_ge(v_xq, 4)
                for k in range(CH):
                    last = mm(bank[q][:, :], w2q[:, k, (q // 2) * P:(q // 2 + 1) * P],
                              xq[:, k * N + (q % 2) * Q4:k * N + (q % 2 + 1) * Q4], start=(k == 0), stop=(k == CH - 1))
                last.then_inc(t_l2, 1)

            router(7, wg3, E3, 16)
            t.wait_ge(v_r, R3 + 12)
            for j in range(2):
                for i in range(4):
                    last = nc.tensor.transpose(bank[4 + j][0:2 * E3, i * P:(i + 1) * P],
                                               gsplit3[:, 4 * j + i, :, :].rearrange("p a e -> p (a e)").bitcast(F32), ident[:, :])
                last.then_inc(t_rtr, 1)
            t.wait_ge(c_w3, 2)
            t.wait_ge(d_sel3, 16)
            t.wait_ge(p_w3, 2)
            t.wait_ge(v_slo, 12)
            t.wait_ge(c_gate, 4)

            def down3(n):
                t.wait_ge(c_h3, n + 1)
                t.wait_ge(v_h3lo, n + 1)
                e, hf = n // 2, n % 2
                for ch in range(CH):
                    cols = slice(ch * P, (ch + 1) * P)
                    o = bank[2 * ch + hf][:, :]
                    mm(o, w3b_hi[:, e, cols], hid3_hi[:, hf, :], start=(e == 0), stop=False)
                    mm(o, w3b_hi[:, e, cols], hid3_lo[:, hf, :], start=False, stop=False)
                    m = mm(o, w3b_lo[:, e, cols], hid3_hi[:, hf, :], start=False, stop=(e == E3 - 1))
                m.then_inc(t_d3, 1)

            for n in range(2 * E3):
                e, hf = n // 2, n % 2
                at_least(t, c_act3, n - 1)
                for k in range(CH):
                    w = slice(e * H3, (e + 1) * H3)
                    r = slice(k * N + hf * Q4, k * N + (hf + 1) * Q4)
                    mm(bank[4 + hf][:, :], w3a_hi[:, k, w], s_hi[:, r], start=(k == 0), stop=False)
                    mm(bank[4 + hf][:, :], w3a_hi[:, k, w], s_lo[:, r], start=False, stop=False)
                    m = mm(bank[4 + hf][:, :], w3a_lo[:, k, w], s_hi[:, r], start=False, stop=(k == CH - 1))
                m.then_inc(t_h3, 1)
                at_least(t, v_h3, n - 1)
                mm(bank[6 + hf][:, :], sel3[:, e, :], gate3_t[:, hf * Q4:(hf + 1) * Q4], start=True, stop=True).then_inc(t_cb3, 1)
                if n >= 1:
                    down3(n - 1)
            down3(2 * E3 - 1)


OUT_SHAPE = (B, T, C)


def lay_out(np_, inputs):
    cm = lambda v: np_.ascontiguousarray(np_.asarray(v).reshape(N, C).T)
    g = {k: np_.asarray(v) for k, v in inputs.items()}
    a = {"xT": cm(g["x"]), "fT": cm(g["fside_BxSxS_0"]), "temb": g["cond_512"]}
    for n in ("w", "u"):
        a[n] = np_.ascontiguousarray(np_.stack([g[f"L{l}_cond_{n}"].reshape(CH, P) for l in range(LAYERS)]).transpose(2, 0, 1))
    a["router"] = np_.ascontiguousarray(np_.concatenate([g["L0_ffn_router_w"].T, g["L0_ffn_sh_gate_w"]], axis=1))

    def rows(e, sh):
        w = np_.zeros((C, CHUNKS * P), np_.float32)
        w[:, :E0 * I_MOE] = e.transpose(1, 0, 2).reshape(C, E0 * I_MOE)
        w[:, E0 * I_MOE:ROWS0] = sh
        return w.reshape(CH, P, CHUNKS, P)

    w0 = np_.zeros((CHUNKS, P, RAWCOLS), np_.float32)
    for k in range(CH):
        for j, (e, sh) in enumerate((("w_gate", "sh_gate"), ("w_up", "sh_up"))):
            w0[:, :, (k * 2 + j) * P:(k * 2 + j + 1) * P] = rows(g["L0_ffn_" + e], g["L0_ffn_" + sh])[k].transpose(1, 0, 2)
    down = np_.zeros((CHUNKS * P, C), np_.float32)
    down[:E0 * I_MOE] = g["L0_ffn_w_down"].reshape(E0 * I_MOE, C)
    down[E0 * I_MOE:ROWS0] = g["L0_ffn_sh_down"]
    w0[:, :, 2 * CH * P:WCOLS] = down.reshape(CHUNKS, P, C)
    for r in range(ROWS0):
        e = min(r // I_MOE, E0)
        w0[r // P, e, WCOLS + r % P] = 1.0
        w0[r // P, GATES + e, WCOLS + r % P] = 1.0
    a["w0"] = w0
    a["w1"] = np_.ascontiguousarray(g["L1_ffn_W_qkv"].T)
    sel = np_.zeros((P, 2, 4, P), np_.float32)
    for m in range(4):
        for r in range(2):
            for d in range(HD):
                row, at = (2 * m + r) * HD + d, r * HROWS + d
                sel[row, 0, m, [at, at + HD]] = 1.0
                sel[row, 1, m, at + 2 * HD] = 1.0
    a["spread"] = sel
    a["wg1"] = np_.ascontiguousarray(g["L1_ffn_W_gate"].T)
    a["w2"] = np_.ascontiguousarray(g["L2_ffn_weight"].T)
    a["b2"] = np_.ascontiguousarray(g["L2_ffn_bias"].reshape(CH, P).T)
    a["wg3"] = g["L3_ffn_wg"]
    a["w3a"] = np_.ascontiguousarray(g["L3_ffn_w1"].transpose(2, 0, 1).reshape(C, E3 * H3))
    a["w3b"] = np_.ascontiguousarray(g["L3_ffn_w2"].transpose(0, 2, 1))
    a["sel3"] = np_.ascontiguousarray(np_.tile(np_.repeat(np_.eye(E3, dtype=np_.float32)[:, :, None], P, axis=2), (2, 1, 1)))
    return a


def kernel(**inputs):
    import numpy as _np
    import concourse.bacc as _bacc
    from concourse.bass_utils import run_bass_kernel_spmd as _run

    nc = _bacc.Bacc("TRN2", target_bir_lowering=False, num_devices=1)
    arrays = lay_out(_np, inputs)
    aps = {k: nc.dram_tensor("in_" + k, v.shape, mybir.dt.from_np(v.dtype), kind="ExternalInput").ap() for k, v in arrays.items()}
    res = nc.dram_tensor("res", (C, N), F32, kind="ExternalOutput").ap()
    build(nc, aps, res)
    r = _run(nc, [{"in_" + k: v for k, v in arrays.items()}], core_ids=[0])
    return _np.ascontiguousarray(r.results[0]["res"].T).reshape(OUT_SHAPE)
```

```python
from contextlib import ExitStack

import numpy as np
import concourse.bass as bass
from concourse import mybir
from concourse.alu_op_type import AluOpType as ALU

F32 = mybir.dt.float32
F32R = mybir.dt.float32r
BF16 = mybir.dt.bfloat16
FP8 = mybir.dt.float8e4
ACT = mybir.ActivationFunctionType
AX = mybir.AxisListType

P = 128
LAYERS = 4
B, T, C, TE = 4, 256, 256, 64
N = B * T
CH = C // P
COLS = CH * N
HB = CH * B
PAIR = 2 * T
PAIRS = HB // 2
PAIR_ORDER = (0, 2, 1, 3)
Q4 = 512
TILES = N // P
E0, I_MOE, I_SH, K0 = 16, 176, 704, 4
GATES = E0 + 1
ROWS0 = E0 * I_MOE + I_SH
CHUNKS = -(-ROWS0 // (2 * P)) * 2
WCOLS = 2 * CH * P + C
RAWCOLS = WCOLS + P
HEADS, HD = 16, 16
E3, H3, K3 = 8, 128, 4
LEAD3 = 4
HID3 = 3
ACT3 = LEAD3 + 2
REP = 4
HROWS = REP * HD
VGAP = 3 * HD
VW = 3 * VGAP + 2 * HD
GROUPS = 6
PCOLS = GROUPS * Q4
BLOCKS = 2 * B
CAP = 30.0
LOW = -3.0e38


def at_least(eng, sem, value):
    if isinstance(value, int) and value <= 0:
        return
    eng.wait_ge(sem, value)


def build(nc, a, out):
    ctx = ExitStack()
    with ctx:
        def sb(name, shape, dt=F32):
            return ctx.enter_context(nc.sbuf_tensor(name, shape, dt))

        def sem(name):
            return ctx.enter_context(nc.semaphore(name))

        bank = [ctx.enter_context(nc.psum_tensor(f"bank{i}", [P, Q4], F32)) for i in range(8)]

        x = sb("x", [P, COLS])
        f = sb("f", [P, COLS])
        mix = sb("mix", [P, LAYERS * COLS])
        sig = sb("sig", [P, 2, Q4])
        s = sb("s", [P, COLS])
        s_parts = sb("s_parts", [P, 2 * COLS], F32R)
        s_hi = s_parts[:, 0:COLS]
        s_lo = s_parts[:, COLS:2 * COLS]
        temb = sb("temb", [P, B, TE])
        tsum = sb("tsum", [P, B])
        tf = sb("tf", [P, B])
        tdecay = sb("tdecay", [P, B])
        wcol = sb("wcol", [P, LAYERS, CH])
        ucol = sb("ucol", [P, LAYERS, CH])
        wexp = sb("wexp", [P, LAYERS, CH])
        wdec = sb("wdec", [P, LAYERS, CH])
        decay = sb("decay", [P, LAYERS, CH, B])
        tmul = sb("tmul", [P, CH, B])
        decay_c = decay[:, :, :, :].rearrange("p l h b -> p (l h b)")
        tmul_c = tmul[:, :, :].rearrange("p h b -> p (h b)")
        EP = E0 + 8
        prob = sb("prob", [P, TILES, EP])
        repl = sb("repl", [P, TILES, EP])
        top8 = sb("top8", [P, TILES, 8])
        rmax = sb("rmax", [P, TILES])
        rsum = sb("rsum", [P, TILES])
        rsg = sb("rsg", [P, TILES])
        gates = sb("gates", [P, TILES, GATES])
        gsplit = sb("gsplit", [P, TILES, 2, GATES], F32R)
        gsplit3 = sb("gsplit3", [P, TILES, 2, E3], F32R)
        ident = sb("ident", [P, P])
        identb = sb("identb", [P, P], BF16)

        rw = sb("rw", [P, CH, GATES])
        w1raw = sb("w1raw", [P, CH, 3 * C])
        wq_hi = sb("wq_hi", [P, CH, C], F32R)
        wq_lo = sb("wq_lo", [P, CH, C], F32R)
        wkv_hi = sb("wkv_hi", [P, CH, 2 * C], F32R)
        wkv_lo = sb("wkv_lo", [P, CH, 2 * C], F32R)
        spread = sb("spread", [P, 2, 4, P], F32R)
        wg1 = sb("wg1", [P, CH, HEADS])
        w2in = sb("w2in", [P, CH, C], BF16)
        w2q = sb("w2q", [P, CH, C], FP8)
        b2in = sb("b2in", [P, CH], BF16)
        b2 = sb("b2", [P, CH])
        wg3 = sb("wg3", [P, CH, E3])
        peak = sb("peak", [P, CH * B + CH])
        peak2 = sb("peak2", [P, 2])
        peakall = sb("peakall", [P, 2])
        peakinv = sb("peakinv", [P, 2])
        scale2 = sb("scale2", [P, 1])
        own0 = ExitStack()

        def sb0(name, shape, dt=F32):
            return own0.enter_context(nc.sbuf_tensor(name, shape, dt))

        ek = sb0("ek", [P, COLS])
        ekv = sb0("ekv", [P, COLS])
        dkv = sb0("dkv", [P, 2, PAIR])
        nf = sb0("nf", [P, 2, PAIR])
        nb = sb0("nb", [P, 2, PAIR])
        df = sb0("df", [P, 2, PAIR])
        db = sb0("db", [P, 2, PAIR])
        raw = sb0("raw", [P, 2, RAWCOLS])
        whi = [sb0(f"whi{i}", [P, RAWCOLS], F32R) for i in range(2)]
        wlo = [sb0(f"wlo{i}", [P, WCOLS], F32R) for i in range(2)]
        sil = sb0("sil", [P, 2, Q4])
        up = sb0("up", [P, Q4])
        hid = sb0("hid", [P, 2, Q4])
        hid_hi = sb0("hid_hi", [P, 2, Q4], F32R)
        hid_lo = sb0("hid_lo", [P, 2, Q4], F32R)
        gate_t = sb0("gate_t", [2 * GATES, N], F32R)
        own0.close()
        own1 = ExitStack()

        def sb1(name, shape, dt=F32):
            return own1.enter_context(nc.sbuf_tensor(name, shape, dt))

        qc_hi = sb1("qc_hi", [P, CH, N], F32R)
        qc_lo = sb1("qc_lo", [P, CH, N], F32R)
        qs = sb1("qs", [P, HEADS // 2, N], F32R)
        negmask = sb1("negmask", [P, P], BF16)
        kvs = sb1("kvs", [P, 2, 2 * C])
        kv1 = sb1("kv1", [P, 2, 2, HD])
        kst = sb1("kst", [P, 2, 2, REP, HD], F32R)
        vals = sb1("vals", [P, TILES, VW])
        keys_t = sb1("keys_t", [P, N], F32R)
        nmax = sb1("nmax", [P, 2, 2, HEADS // 2])
        nmx = sb1("nmx", [P, 2, 2, 2, HEADS // 2], F32R)
        nmx_t = sb1("nmx_t", [2 * HEADS, 2, P])
        pexp = [sb1(f"pexp{i}", [P, PCOLS]) for i in range(2)]
        rden = sb1("rden", [P // 2, Q4])
        yt = sb1("yt", [P, 2, T])
        own1.close()
        own2 = ExitStack()

        def sb2(name, shape, dt=F32):
            return own2.enter_context(nc.sbuf_tensor(name, shape, dt))

        xq = sb2("xq", [P, COLS], FP8)
        y2a = sb2("y2a", [P, 2, Q4], BF16)
        y2b = sb2("y2b", [P, 2, Q4], BF16)
        w3a_hi = sb2("w3a_hi", [P, CH, E3 * H3], F32R)
        w3a_lo = sb2("w3a_lo", [P, CH, E3 * H3], F32R)
        w3b_hi = sb2("w3b_hi", [P, E3, C], F32R)
        w3b_lo = sb2("w3b_lo", [P, E3, C], F32R)
        sel3 = sb2("sel3", [2 * E3, E3, P], F32R)
        act3 = sb2("act3", [P, ACT3, Q4])
        hid3 = sb2("hid3", [P, HID3, Q4])
        hid3_hi = sb2("hid3_hi", [P, HID3, Q4], F32R)
        hid3_lo = sb2("hid3_lo", [P, HID3, Q4], F32R)
        gate3_t = sb2("gate3_t", [2 * E3, N], F32R)
        own2.close()
        w3a_raw = f[:, :].rearrange("p (k n) -> p k n", k=CH)
        w3b_raw = mix[:, 0:COLS].rearrange("p (e n) -> p e n", e=E3)

        ctx.enter_context(nc.allow_low_precision(reason="exact splits into float32r parts"))

        d_f = [sem("d_f0"), sem("d_f1")]
        d_in = sem("d_in")
        t_num = sem("t_num")
        d_small = sem("d_small")
        d_raw = [sem("d_raw0"), sem("d_raw1")]
        d_out = sem("d_out")
        c_tf = sem("c_tf")
        v_tf = sem("v_tf")
        p_id = sem("p_id")
        v_cap = sem("v_cap")
        v_zero = sem("v_zero")
        c_ek = sem("c_ek")
        c_euk = sem("c_euk")
        p_ekv = sem("p_ekv")
        p_dkv = sem("p_dkv")
        p_den = sem("p_den")
        p_num = sem("p_num")
        p_dsum = sem("p_dsum")
        p_nsum = sem("p_nsum")
        v_dscan = sem("v_dscan")
        v_nscan = sem("v_nscan")
        v_guard = sem("v_guard")
        v_den = sem("v_den")
        v_mix = sem("v_mix")
        c_sig = sem("c_sig")
        s_ready = sem("s_ready")
        c_shi = sem("c_shi")
        v_slo = sem("v_slo")
        p_slo = sem("p_slo")
        t_rout = sem("t_rout")
        v_r = sem("v_r")
        c_r = sem("c_r")
        t_rtr = sem("t_rtr")
        c_gate = sem("c_gate")
        c_whi = sem("c_whi")
        p_wlo = sem("p_wlo")
        t_g = sem("t_g")
        t_u = sem("t_u")
        t_cb = sem("t_cb")
        t_down = sem("t_down")
        c_sil = sem("c_sil")
        v_up = sem("v_up")
        v_hid = sem("v_hid")
        c_hhi = sem("c_hhi")
        v_hlo = sem("v_hlo")
        v_x = sem("v_x")
        d_w1 = sem("d_w1")
        d_w23 = sem("d_w23")
        d_w3 = sem("d_w3")
        c_w1 = sem("c_w1")
        p_w1 = sem("p_w1")
        p_const = sem("p_const")
        d_spread = sem("d_spread")
        d_sel3 = sem("d_sel3")
        t_qc = sem("t_qc")
        c_qc = sem("c_qc")
        v_qc = sem("v_qc")
        t_qs = sem("t_qs")
        c_qs = sem("c_qs")
        t_kv = sem("t_kv")
        c_kv = sem("c_kv")
        p_kv = sem("p_kv")
        v_red = sem("v_red")
        v_k1 = sem("v_k1")
        v_kst = sem("v_kst")
        v_val = sem("v_val")
        t_kt = sem("t_kt")
        c_kt = sem("c_kt")
        t_a = sem("t_a")
        v_nmax = sem("v_nmax")
        v_nmx = sem("v_nmx")
        t_nmx = sem("t_nmx")
        c_nmx = sem("c_nmx")
        d_nmx = [sem("d_nmx0"), sem("d_nmx1")]
        t_b = sem("t_b")
        c_p = sem("c_p")
        p_sel = sem("p_sel")
        t_pv = sem("t_pv")
        v_rden = sem("v_rden")
        v_y = sem("v_y")
        v_peak = sem("v_peak")
        v_wpeak = sem("v_wpeak")
        p_peak = sem("p_peak")
        v_xq = sem("v_xq")
        v_wq2 = sem("v_wq2")
        t_l2 = sem("t_l2")
        c_y2 = sem("c_y2")
        v_y2b = sem("v_y2b")
        c_w3 = sem("c_w3")
        p_w3 = sem("p_w3")
        t_h3 = sem("t_h3")
        t_cb3 = sem("t_cb3")
        c_act3 = sem("c_act3")
        v_h3 = sem("v_h3")
        c_h3 = sem("c_h3")
        v_h3lo = sem("v_h3lo")
        t_d3 = sem("t_d3")

        block = ctx.enter_context(nc.Block())
        HALF_IT = CHUNKS // 2


        def mixed(l, col, n):
            return mix[:, bass.ds(l * COLS + col, n)]

        def forward(v, l, p, st, den, j):
            src, fw, done = (ek, df, v_dscan) if den else (ekv, nf, v_nscan)
            d = decay_c[:, bass.ds(l * HB + p * 2 + j, 1)].to_broadcast([P, T])
            v.tensor_tensor_scan(out=fw[:, st, j * T:(j + 1) * T], data0=d, data1=src[:, p * PAIR + j * T:p * PAIR + (j + 1) * T],
                                 initial=0.0, op0=ALU.mult, op1=ALU.add).then_inc(done, 1)

        def backward(v, l, p, st, den, j):
            src, bw, done = (ek, db, v_dscan) if den else (ekv, nb, v_nscan)
            d = decay_c[:, bass.ds(l * HB + p * 2 + j, 1)].to_broadcast([P, T - 1])
            data = src[:, p * PAIR + j * T:p * PAIR + (j + 1) * T]
            rev = slice((j + 1) * T - 2, j * T - 1 if j else None, -1)
            v.tensor_tensor_scan(out=bw[:, st, rev], data0=data[:, T - 1:0:-1], data1=d,
                                 initial=0.0, op0=ALU.add, op1=ALU.mult).then_inc(done, 1)

        def scans(v, l, p, st, den):
            for j in range(2):
                forward(v, l, p, st, den, j)
                backward(v, l, p, st, den, j)

        def guard_den(v, st, part):
            cut = slice(part * T, (part + 1) * T)
            v.tensor_scalar(out=df[:, st, cut], in0=df[:, st, cut], scalar1=1e-8, scalar2=None,
                            op0=ALU.max).then_inc(v_guard, 1)

        def invert_den(v, st, part, quarter, k):
            cut = slice(part * T + quarter * P, part * T + (quarter + 1) * P)
            v.wait_ge(v_guard, 2 * k + part + 1)
            v.reciprocal(df[:, st, cut], df[:, st, cut]).then_inc(v_den, 1)

        def finish_mix(v, l, p, st, num):
            for j in range(2):
                cut = slice(j * T, (j + 1) * T)
                v.scalar_tensor_tensor(out=mixed(l, p * PAIR + j * T, T), in0=num[:, cut],
                                       scalar=tmul_c[:, p * 2 + j:p * 2 + j + 1], in1=df[:, st, cut],
                                       op0=ALU.mult, op1=ALU.mult).then_inc(v_mix, 1)

        def pool_dkv(g, l, p, st):
            g.tensor_tensor(out=dkv[:, st, :], in0=mixed(l, p * PAIR, PAIR), in1=f[:, p * PAIR:(p + 1) * PAIR],
                            op=ALU.mult).then_inc(p_dkv, 1)

        def pool_sums(g, l, p, st, k):
            g.wait_ge(v_dscan, 4 * (k + 1))
            g.tensor_tensor(out=df[:, st, :], in0=df[:, st, :], in1=db[:, st, :], op=ALU.add).then_inc(p_dsum, 1)
            g.wait_ge(c_ek, 2)
            g.wait_ge(p_dsum, k + 1)
            g.tensor_tensor(out=df[:, st, :], in0=df[:, st, :], in1=mixed(l, p * PAIR, PAIR), op=ALU.add).then_inc(p_den, 1)
            g.wait_ge(v_nscan, 4 * (k + 1))
            g.tensor_tensor(out=nf[:, st, :], in0=nf[:, st, :], in1=nb[:, st, :], op=ALU.add).then_inc(p_nsum, 1)
            g.wait_ge(p_nsum, k - PAIRS + 1)
            g.tensor_tensor(out=nf[:, st, :], in0=nf[:, st, :], in1=dkv[:, st, :], op=ALU.add).then_inc(p_num, 1)

        def chunk(i):
            return slice(PAIR_ORDER[i] * Q4, (PAIR_ORDER[i] + 1) * Q4)

        def of_batch(buf, b, layer=0):
            return buf[:, layer * COLS:(layer + 1) * COLS].rearrange("p (h n) -> p h n", h=CH)[:, :, b * T:(b + 1) * T]

        def halves(buf):
            return buf.rearrange("p (h n) -> p h n", h=CH)

        def sigmoid_of(c, l, i):
            c.wait_ge(v_x, (i + 1) if l == 1 else 4 + TILES + i + 1)
            c.wait_ge(s_ready, 4 * l + i - 1)
            c.activation(sig[:, i % 2, :], x[:, chunk(i)], ACT.Sigmoid).then_inc(c_sig, 1)

        def high_of(c, l, i):
            c.wait_ge(s_ready, 4 * l + i + 1)
            c.activation(s_hi[:, chunk(i)], s[:, chunk(i)], ACT.Copy).then_inc(c_shi, 1)

        R0 = 33
        R3 = R0 + 9
        ALIST = [[(r, m, nm) for m in range(0, 8, nm) for r in range(2)] for nm in (4, 2)]
        BLIST = [(kc, r, m, nm) for kc, nm in ((0, 2), (1, 4)) for m in range(0, 4, nm) for r in range(2)]
        AHEAD = 3
        ASTEPS = [[[0], [1], [2], [3], [], []], [[0, 1], [2, 3], [4], [5], [6], [7]]]

        EARLY = {5: [(0, gi) for gi in range(4)], 6: [(1, gi) for gi in range(4)], 7: [(1, gi) for gi in range(4, 8)],
                 8: [(2, gi) for gi in range(2)]}

        def a_before(t):
            return sum(len(ALIST[i % 2]) for i in range(t))

        def p_at(buf, k, kc, r, m, nm):
            w = T if kc == 0 else P
            at = (0 if kc == 0 else 8 * T) + (r * 4 + m) * w
            return buf[k % 2][:, at:at + nm * w]

        COND_STEPS = {1: (("add", 0), ("add", 1), ("product", 0), ("product", 1), ("add", 2), ("low", 0),
                          ("add", 3), ("low", 1), ("product", 2), ("product", 3), ("low", 2), ("low", 3)),
                      3: (("add", 0), ("add", 1), ("product", 0), ("product", 1), ("add", 2), ("add", 3),
                          ("product", 2), ("product", 3), ("low", 0), ("low", 1), ("low", 2), ("low", 3))}

        def cond_dve(v, l, add):
            for step, i in COND_STEPS[l]:
                if step == "add":
                    add(i)
                elif step == "product":
                    v.wait_ge(c_sig, 4 * l + i + 1)
                    v.wait_ge(v_mix, 8 * l + 8)
                    if l == 3:
                        v.wait_ge(v_xq, 4)
                    v.tensor_tensor(out=s[:, chunk(i)], in0=sig[:, i % 2, :],
                                    in1=mix[:, l * COLS + chunk(i).start:l * COLS + chunk(i).stop], op=ALU.mult).then_inc(s_ready, 1)
                else:
                    v.wait_ge(c_shi, (4 if l == 1 else 8) + i + 1)
                    v.tensor_tensor(out=s_lo[:, chunk(i)], in0=s[:, chunk(i)], in1=s_hi[:, chunk(i)].bitcast(F32),
                                    op=ALU.subtract).then_inc(v_slo, 1)

        @block.sync
        def _(sp):
            sp.dma_start(temb[:, :, :], a["temb"].rearrange("(o b) t -> o b t", o=1).to_broadcast([P, B, TE])).then_inc(d_small, 16)
            sp.dma_start(wcol[:, :, :], a["w"]).then_inc(d_small, 16)
            sp.dma_start(ucol[:, :, :], a["u"]).then_inc(d_small, 16)
            for h in range(CH):
                sp.dma_start(f[:, h * N:(h + 1) * N], a["fT"][h * P:(h + 1) * P, :]).then_inc(d_f[h], 16)
            sp.dma_start(x[:, :], a["xT"].rearrange("(h p) t -> p h t", p=P)).then_inc(d_in, 16)
            sp.dma_start(rw[:, :, :], a["router"].rearrange("(k p) e -> p k e", p=P)).then_inc(d_in, 16)
            for c in range(2):
                sp.dma_start(raw[:, c, :], a["w0"][c, :, :]).then_inc(d_raw[c], 16)
            sp.dma_start(w1raw[:, :, :], a["w1"].rearrange("(k p) n -> p k n", p=P)).then_inc(d_w1, 16)
            sp.dma_start(wg1[:, :, :], a["wg1"].rearrange("(k p) n -> p k n", p=P)).then_inc(d_w1, 16)
            sp.dma_start(w2in[:, :, :], a["w2"].rearrange("(k p) n -> p k n", p=P)).then_inc(d_w23, 16)
            sp.dma_start(b2in[:, :], a["b2"]).then_inc(d_w23, 16)
            sp.dma_start(wg3[:, :, :], a["wg3"].rearrange("(k p) n -> p k n", p=P)).then_inc(d_w23, 16)
            with sp.Fori(0, HALF_IT - 1) as i:
                for c in range(2):
                    sp.wait_ge(c_whi, 2 * i + c + 1)
                    sp.wait_ge(p_wlo, 2 * i + c + 1)
                    sp.dma_start(raw[:, c, :], a["w0"][bass.ds(2 * i + 2 + c, 1), :, :].rearrange("o p n -> (o p) n")).then_inc(d_raw[c], 16)
            sp.wait_ge(v_x, 4)
            sp.dma_start(w3a_raw, a["w3a"].rearrange("(k p) n -> p k n", p=P)).then_inc(d_w3, 16)
            sp.dma_start(w3b_raw, a["w3b"].rearrange("e p n -> p e n")).then_inc(d_w3, 16)
            for t in range(TILES):
                sp.wait_ge(c_nmx, t + 1)
                for r in range(2):
                    at = r * HROWS + (REP - 1) * HD
                    sp.dma_start(qs[at:at + 2, :, t * P:(t + 1) * P].bitcast(F32),
                                 nmx_t[r * HEADS:(r + 1) * HEADS, t % 2, :]).then_inc(d_nmx[t % 2], 16)
            for i, q in enumerate(PAIR_ORDER):
                sp.wait_ge(v_x, 4 + TILES + 4 + i + 1)
                h, th = q // 2, q % 2
                sp.dma_start(out[h * P:(h + 1) * P, th * Q4:(th + 1) * Q4], x[:, q * Q4:(q + 1) * Q4]).then_inc(d_out, 16)
            sp.wait_ge(d_out, 64)

        @block.scalar
        def _(c):
            c.wait_ge(v_tf, 1)
            c.activation(tf[:, :], tsum[:, :], ACT.Sigmoid).then_inc(c_tf, 1)
            c.activation(wexp[:, :, :], wcol[:, :, :], ACT.Exp).then_inc(c_tf, 1)
            c.wait_ge(c_tf, 2)
            c.activation(wdec[:, :, :], wexp[:, :, :], ACT.Exp, scale=-1.0).then_inc(c_tf, 1)
            for h in range(CH):
                cut = slice(h * N, (h + 1) * N)
                c.wait_ge(v_cap, 2 * h + 1)
                c.activation(ek[:, cut], ek[:, cut], ACT.Exp).then_inc(c_ek, 1)
                c.wait_ge(v_cap, 2 * h + 2)
                c.activation(mix[:, cut], mix[:, cut], ACT.Exp).then_inc(c_euk, 1)
            c.wait_ge(d_in, 32)
            for p in PAIR_ORDER:
                cut = slice(p * PAIR, (p + 1) * PAIR)
                c.activation(s[:, cut], x[:, cut], ACT.Sigmoid).then_inc(c_sig, 1)
            for k, p in enumerate(PAIR_ORDER):
                cut = slice(p * PAIR, (p + 1) * PAIR)
                c.wait_ge(s_ready, k + 1)
                c.activation(s_hi[:, cut], s[:, cut], ACT.Copy).then_inc(c_shi, 1)
            c.wait_ge(d_raw[0], 16)
            c.activation(whi[0][:, :], raw[:, 0, :], ACT.Copy).then_inc(c_whi, 1)

            def exp_euk(l):
                c.wait_ge(v_cap, 2 * CH + 2 * l)
                c.activation(mixed(l, 0, COLS), mixed(l, 0, COLS), ACT.Exp).then_inc(c_euk, 1)

            exp_euk(1)
            c.wait_ge(v_r, 2)
            c.activation(prob[:, :, 0:E0], prob[:, :, 0:E0], ACT.Exp).then_inc(c_r, 1)
            c.wait_ge(t_rout, 1)
            c.activation(rsg[:, :], bank[7][:, :].rearrange("p (t e) -> p t e", t=TILES)[:, :, E0], ACT.Exp, scale=-1.0).then_inc(c_r, 1)
            exp_euk(2)
            exp_euk(3)

            def body(i, first, last):
                for n in range(4):
                    ch, hf = n // 2, n % 2
                    if last and n == 1:
                        c.wait_ge(d_w1, 32)
                        c.activation(wq_hi[:, :, :], w1raw[:, :, 0:C], ACT.Copy).then_inc(c_w1, 1)
                        c.activation(wkv_hi[:, :, :], w1raw[:, :, C:3 * C], ACT.Copy).then_inc(c_w1, 1)
                    c.wait_ge(t_g, 4 * i + n + 1)
                    at_least(c, v_up, 4 * i + n - 1)
                    c.activation(sil[:, hf, :], bank[4][:, :], ACT.Silu).then_inc(c_sil, 1)
                    if first and n == 0:
                        for j in range(2):
                            c.wait_ge(t_rtr, j + 1)
                            c.activation(gate_t[:, j * Q4:(j + 1) * Q4], bank[7 - j][0:2 * GATES, :], ACT.Copy).then_inc(c_gate, 1)
                    if hf == 0 and not (last and ch == 1):
                        at_least(c, t_down, 4 * i + 2 * ch)
                        c.wait_ge(d_raw[1 - ch], 16 * (i + 1 + ch))
                        c.activation(whi[1 - ch][:, :], raw[:, 1 - ch, :], ACT.Copy).then_inc(c_whi, 1)
                    c.wait_ge(v_hid, 4 * i + n + 1)
                    at_least(c, t_down, 4 * i + n - 1)
                    c.activation(hid_hi[:, hf, :], hid[:, hf, :], ACT.Copy).then_inc(c_hhi, 1)

            body(0, True, False)
            with c.Fori(1, HALF_IT - 1) as i:
                body(i, False, False)
            body(HALF_IT - 1, False, True)

            for i in range(5):
                if i < 4:
                    sigmoid_of(c, 1, i)
                if i >= 1:
                    high_of(c, 1, i - 1)
            for n in range(4):
                if n == 2:
                    c.wait_ge(v_r, R0 + 2)
                    c.activation(prob[:, :, 0:HEADS], prob[:, :, 0:HEADS], ACT.Exp).then_inc(c_r, 1)
                c.wait_ge(t_qc, n + 1)
                c.activation(qc_hi[:, n % 2, (n // 2) * Q4:(n // 2 + 1) * Q4], bank[5 + n % 2][:, :], ACT.Copy).then_inc(c_qc, 1)

            def key_copy(t):
                c.wait_ge(t_kt, t + 1)
                c.activation(keys_t[:, t * P:(t + 1) * P], bank[6 + t % 2][:, 0:P], ACT.Copy).then_inc(c_kt, 1)

            def maxima(t):
                c.wait_ge(t_nmx, t + 1)
                at_least(c, d_nmx[t % 2], 32 * (t // 2))
                c.activation(nmx_t[:, t % 2, :], bank[0 if t < 2 else 6][0:2 * HEADS, 0:P], ACT.Copy).then_inc(c_nmx, 1)

            for t in range(TILES + 3):
                if t < TILES:
                    c.wait_ge(t_kv, t + 1)
                    at_least(c, v_red, t - 1)
                    c.activation(kvs[:, t % 2, :], bank[t % 2][:, :], ACT.Copy).then_inc(c_kv, 1)
                if 1 <= t <= TILES:
                    u = t - 1
                    for j in range(2):
                        c.wait_ge(t_qs, 2 * u + j + 1)
                        c.activation(qs[:, u % 4 * 2 + j, (u // 4) * Q4:(u // 4 + 1) * Q4], bank[2 + j][:, :], ACT.Copy).then_inc(c_qs, 1)
                if t >= 3:
                    key_copy(t - 3)
                if t in (8, 9):
                    maxima(t - 8)

            for k in range(BLOCKS):
                for gi in range(GROUPS):
                    g = k * GROUPS + gi
                    c.wait_ge(t_b, g + 1)
                    kc, r, m, nm = BLIST[gi]
                    at_least(c, t_pv, k - 1)
                    c.activation(p_at(pexp, k, kc, r, m, nm), bank[2 + g % 2][:, :], ACT.Exp, scale=HD ** -0.5).then_inc(c_p, 1)
                    if gi == 1 and k + AHEAD - 1 < TILES:
                        maxima(k + AHEAD - 1)

            for b in range(B):
                c.wait_ge(v_x, 4 + 2 * b + 2)
                c.wait_ge(s_ready, 8 + b - 1)
                c.activation(halves(sig[:, b % 2, :]), of_batch(x, b), ACT.Sigmoid).then_inc(c_sig, 1)
            c.wait_ge(d_w3, 32)
            c.activation(w3a_hi[:, :, :], w3a_raw, ACT.Copy).then_inc(c_w3, 1)
            c.activation(w3b_hi[:, :, :], w3b_raw, ACT.Copy).then_inc(c_w3, 1)

            def layer2_out(i):
                c.wait_ge(t_l2, i + 1)
                at_least(c, v_y2b, i - 1)
                c.activation(y2a[:, i % 2, :], bank[PAIR_ORDER[i]][:, :], ACT.Copy, scale=scale2[:, 0:1]).then_inc(c_y2, 1)

            layer2_out(0)
            layer2_out(1)
            for i in range(4):
                sigmoid_of(c, 3, i)
                if i < 2:
                    layer2_out(i + 2)
                else:
                    high_of(c, 3, i - 2)
            high_of(c, 3, 2)
            high_of(c, 3, 3)

            def hidden3(n):
                c.wait_ge(t_h3, n + 1)
                at_least(c, v_h3, n - ACT3 + 1)
                c.activation(act3[:, n % ACT3, :], bank[4 + n % 2][:, :], ACT.Relu).then_inc(c_act3, 1)

            c.wait_ge(v_r, R3 + 3)
            c.activation(prob[:, :, 0:E3], prob[:, :, 0:E3], ACT.Exp).then_inc(c_r, 1)
            for n in range(LEAD3 - 1):
                hidden3(n)
            for j in range(2):
                c.wait_ge(t_rtr, 2 + j + 1)
                c.activation(gate3_t[:, j * Q4:(j + 1) * Q4], bank[7 - j][0:2 * E3, :], ACT.Copy).then_inc(c_gate, 1)
            hidden3(LEAD3 - 1)
            for n in range(2 * E3):
                if n + LEAD3 < 2 * E3:
                    hidden3(n + LEAD3)
                c.wait_ge(v_h3, n + 1)
                at_least(c, t_d3, n - HID3 + 1)
                c.activation(hid3_hi[:, n % HID3, :], hid3[:, n % HID3, :], ACT.Copy).then_inc(c_h3, 1)

        @block.vector
        def _(v):
            v.wait_ge(d_small, 48)
            v.tensor_reduce(out=tsum[:, :], in_=temb[:, :, :], op=ALU.add, axis=AX.X).then_inc(v_tf, 1)
            v.memset(db[:, :, T - 1::T], 0.0).then_inc(v_zero, 1)
            v.memset(nb[:, :, T - 1::T], 0.0).then_inc(v_zero, 1)
            v.wait_ge(v_zero, 2)

            def cap(h):
                cut = slice(h * N, (h + 1) * N)
                v.wait_ge(d_f[h], 16)
                v.tensor_scalar(out=ek[:, cut], in0=f[:, cut], scalar1=CAP, scalar2=None, op0=ALU.min).then_inc(v_cap, 1)
                v.tensor_scalar(out=mix[:, cut], in0=f[:, cut], scalar1=ucol[:, 0, h:h + 1], scalar2=CAP,
                                op0=ALU.add, op1=ALU.min).then_inc(v_cap, 1)

            cap(0)
            v.wait_ge(c_tf, 1)
            v.tensor_scalar(out=tdecay[:, :], in0=tf[:, :], scalar1=0.5, scalar2=0.5, op0=ALU.mult, op1=ALU.add).then_inc(v_tf, 1)
            for h in range(CH):
                v.tensor_scalar(out=tmul[:, h, :], in0=tf[:, :], scalar1=0.2, scalar2=0.8, op0=ALU.mult, op1=ALU.add).then_inc(v_tf, 1)
            v.wait_ge(c_tf, 3)
            v.wait_ge(v_tf, 4)
            for b in range(B):
                v.tensor_scalar(out=decay[:, :, :, b], in0=wdec[:, :, :], scalar1=tdecay[:, b:b + 1], scalar2=None,
                                op0=ALU.mult).then_inc(v_tf, 1)
            v.wait_ge(v_tf, 8)
            def product(k):
                cut = chunk(k)
                v.wait_ge(v_mix, 2 * k + 2)
                v.wait_ge(c_sig, k + 1)
                v.tensor_tensor(out=s[:, cut], in0=s[:, cut], in1=mix[:, cut], op=ALU.mult).then_inc(s_ready, 1)

            for k in range(PAIRS + 1):
                st = (k - 1) % 2
                if k < PAIRS:
                    p = PAIR_ORDER[k]
                    v.wait_ge(c_ek, p // 2 + 1)
                    if k >= 2:
                        v.wait_ge(t_num, k - 1)
                        v.wait_ge(v_mix, 2 * (k - 1))
                    scans(v, 0, p, k % 2, True)
                    if k == 0:
                        cap(1)
                if k >= 1:
                    v.wait_ge(p_den, k)
                    v.tensor_scalar(out=df[:, st, :], in0=df[:, st, :], scalar1=1e-8, scalar2=None, op0=ALU.max).then_inc(v_guard, 2)
                if k < PAIRS:
                    v.wait_ge(p_ekv, k + 1)
                    scans(v, 0, p, k % 2, False)
                if k >= 1:
                    v.wait_ge(v_guard, 2 * k)
                    v.reciprocal(df[:, st, :], df[:, st, :]).then_inc(v_den, 4)
                if k >= 2:
                    product(k - 2)
                if k >= 1:
                    v.wait_ge(v_den, 4 * k)
                    v.wait_ge(t_num, k)
                    finish_mix(v, 0, PAIR_ORDER[k - 1], st, bank[st])
            product(PAIRS - 1)
            for l in range(1, LAYERS):
                for h in range(CH):
                    cut = slice(h * N, (h + 1) * N)
                    v.tensor_scalar(out=mix[:, l * COLS + h * N:l * COLS + (h + 1) * N], in0=f[:, cut],
                                    scalar1=ucol[:, l, h:h + 1], scalar2=CAP, op0=ALU.add, op1=ALU.min).then_inc(v_cap, 1)
            v.wait_ge(c_shi, PAIRS)
            v.tensor_tensor(out=s_lo[:, COLS - PAIR:COLS], in0=s[:, COLS - PAIR:COLS], in1=s_hi[:, COLS - PAIR:COLS].bitcast(F32),
                            op=ALU.subtract).then_inc(v_slo, 1)
            v.wait_ge(t_rout, 1)
            lg = bank[7][:, :].rearrange("p (t e) -> p t e", t=TILES)[:, :, 0:E0]
            v.tensor_reduce(out=rmax[:, :], in_=lg, op=ALU.max, axis=AX.X).then_inc(v_r, 1)
            v.wait_ge(v_r, 1)
            v.tensor_tensor(out=prob[:, :, 0:E0], in0=lg, in1=rmax[:, :].unsqueeze(2).to_broadcast([P, TILES, E0]),
                            op=ALU.subtract).then_inc(v_r, 1)
            v.memset(prob[:, :, E0:EP], -1.0).then_inc(v_r, 1)
            v.wait_ge(c_r, 1)
            v.tensor_reduce(out=rsum[:, :], in_=prob[:, :, 0:E0], op=ALU.add, axis=AX.X).then_inc(v_r, 1)
            v.wait_ge(v_r, 4)
            v.reciprocal(rsum[:, :], rsum[:, :]).then_inc(v_r, 1)
            v.wait_ge(v_r, 5)
            v.tensor_tensor(out=prob[:, :, 0:E0], in0=prob[:, :, 0:E0],
                            in1=rsum[:, :].unsqueeze(2).to_broadcast([P, TILES, E0]), op=ALU.mult).then_inc(v_r, 1)
            v.wait_ge(v_r, 6)
            W = E0 + 8 - K0
            for t in range(TILES):
                v.max(out=top8[:, t, :], in_=prob[:, t, 0:W]).then_inc(v_r, 1)
            v.wait_ge(v_r, 14)
            v.memset(top8[:, :, K0:8], -1.0).then_inc(v_r, 1)
            v.wait_ge(v_r, 15)
            for t in range(TILES):
                v.match_replace(out=repl[:, t, 0:W], in_to_replace=top8[:, t, :], in_values=prob[:, t, 0:W],
                                imm_value=-2.0).then_inc(v_r, 1)
            v.tensor_reduce(out=rsum[:, :], in_=top8[:, :, 0:K0], op=ALU.add, axis=AX.X).then_inc(v_r, 1)
            v.wait_ge(v_r, 24)
            v.tensor_scalar(out=rsum[:, :], in0=rsum[:, :], scalar1=1e-9, scalar2=None, op0=ALU.max).then_inc(v_r, 1)
            v.tensor_tensor(out=repl[:, :, 0:E0], in0=repl[:, :, 0:E0], in1=prob[:, :, 0:E0], op=ALU.not_equal).then_inc(v_r, 1)
            v.wait_ge(v_r, 26)
            v.reciprocal(rsum[:, :], rsum[:, :]).then_inc(v_r, 1)
            v.tensor_tensor(out=prob[:, :, 0:E0], in0=prob[:, :, 0:E0], in1=repl[:, :, 0:E0], op=ALU.mult).then_inc(v_r, 1)
            v.wait_ge(c_r, 2)
            v.tensor_scalar(out=rsg[:, :], in0=rsg[:, :], scalar1=1.0, scalar2=None, op0=ALU.add).then_inc(v_r, 1)
            v.wait_ge(v_r, 29)
            v.tensor_tensor(out=gates[:, :, 0:E0], in0=prob[:, :, 0:E0],
                            in1=rsum[:, :].unsqueeze(2).to_broadcast([P, TILES, E0]), op=ALU.mult).then_inc(v_r, 1)
            v.reciprocal(gates[:, :, E0], rsg[:, :]).then_inc(v_r, 1)
            v.wait_ge(v_r, 31)
            v.tensor_copy(gsplit[:, :, 0, :], gates[:, :, :]).then_inc(v_r, 1)
            v.wait_ge(v_r, 32)
            v.tensor_tensor(out=gsplit[:, :, 1, :], in0=gates[:, :, :], in1=gsplit[:, :, 0, :].bitcast(F32),
                            op=ALU.subtract).then_inc(v_r, 1)

            def body(i, wkv):
                l, p, k = wkv if wkv else (0, 0, 0)
                st = p % 2
                for n in range(4):
                    ch, hf = n // 2, n % 2
                    v.wait_ge(t_u, 4 * i + n + 1)
                    v.wait_ge(c_sil, 4 * i + n + 1)
                    v.tensor_tensor(out=up[:, :], in0=bank[5][:, :], in1=sil[:, hf, :], op=ALU.mult).then_inc(v_up, 1)
                    if wkv and n < 2:
                        forward(v, l, p, st, n == 0, 0)
                    elif wkv:
                        if n == 2:
                            v.wait_ge(p_den, k + 1)
                        guard_den(v, st, n - 2)
                    v.wait_ge(t_cb, 4 * i + n + 1)
                    v.wait_ge(v_up, 4 * i + n + 1)
                    v.tensor_tensor(out=hid[:, hf, :], in0=bank[6][:, :], in1=up[:, :], op=ALU.mult).then_inc(v_hid, 1)
                    if wkv and n < 2:
                        backward(v, l, p, st, n == 0, 0)
                    elif wkv:
                        invert_den(v, st, n - 2, 0, k)
                    v.wait_ge(c_hhi, 4 * i + n + 1)
                    at_least(v, t_down, 4 * i + n - 1)
                    v.tensor_tensor(out=hid_lo[:, hf, :], in0=hid[:, hf, :], in1=hid_hi[:, hf, :].bitcast(F32),
                                    op=ALU.subtract).then_inc(v_hlo, 1)
                    if wkv and n < 2:
                        forward(v, l, p, st, n == 0, 1)
                        backward(v, l, p, st, n == 0, 1)
                    elif wkv:
                        invert_den(v, st, n - 2, 1, k)
                    if wkv and n == 3:
                        v.wait_ge(v_den, 4 * (k + 1))
                        v.wait_ge(p_num, k - PAIRS + 1)
                        finish_mix(v, l, p, st, nf[:, st, :])

            body(0, None)
            with v.Fori(1, LAYERS) as l:
                for p in range(PAIRS):
                    body(PAIRS * l + p + 1 - PAIRS, (l, p, PAIRS * l + p))
            for i in range(1 + PAIRS * (LAYERS - 1), HALF_IT):
                body(i, None)
            def add_experts(i):
                v.wait_ge(t_down, 4 * HALF_IT - (1 if i < 2 else 0))
                v.tensor_tensor(out=x[:, chunk(i)], in0=bank[PAIR_ORDER[i]][:, :], in1=x[:, chunk(i)], op=ALU.add).then_inc(v_x, 1)

            cond_dve(v, 1, add_experts)

            def queries_low(n):
                cut = slice((n // 2) * Q4, (n // 2 + 1) * Q4)
                v.wait_ge(c_qc, n + 1)
                v.tensor_tensor(out=qc_lo[:, n % 2, cut], in0=bank[5 + n % 2][:, :], in1=qc_hi[:, n % 2, cut].bitcast(F32),
                                op=ALU.subtract).then_inc(v_qc, 1)

            queries_low(0)
            queries_low(1)
            v.wait_ge(t_rout, 2)
            lg = bank[4][:, :].rearrange("p (t e) -> p t e", t=TILES)[:, :, 0:HEADS]
            v.tensor_reduce(out=rmax[:, :], in_=lg, op=ALU.max, axis=AX.X).then_inc(v_r, 1)
            v.wait_ge(v_r, R0 + 1)
            v.tensor_tensor(out=prob[:, :, 0:HEADS], in0=lg, in1=rmax[:, :].unsqueeze(2).to_broadcast([P, TILES, HEADS]),
                            op=ALU.subtract).then_inc(v_r, 1)
            v.memset(prob[:, :, HEADS:HEADS + 8], -1.0).then_inc(v_r, 1)
            v.wait_ge(c_r, 3)
            v.tensor_reduce(out=rsum[:, :], in_=prob[:, :, 0:HEADS], op=ALU.add, axis=AX.X).then_inc(v_r, 1)
            v.wait_ge(v_r, R0 + 4)
            v.reciprocal(rsum[:, :], rsum[:, :]).then_inc(v_r, 1)
            v.wait_ge(v_r, R0 + 5)
            v.tensor_tensor(out=prob[:, :, 0:HEADS], in0=prob[:, :, 0:HEADS],
                            in1=rsum[:, :].unsqueeze(2).to_broadcast([P, TILES, HEADS]), op=ALU.mult).then_inc(v_r, 1)
            v.wait_ge(v_r, R0 + 6)
            v.tensor_reduce(out=rmax[:, :], in_=prob[:, :, 0:HEADS], op=ALU.max, axis=AX.X).then_inc(v_r, 1)
            v.memset(top8[:, :, 1:8], -1.0).then_inc(v_r, 1)
            v.wait_ge(v_r, R0 + 8)
            v.tensor_copy(top8[:, :, 0], rmax[:, :]).then_inc(v_r, 1)
            v.wait_ge(v_r, R0 + 9)
            for t in range(TILES):
                v.match_replace(out=repl[:, t, 0:HEADS + 7], in_to_replace=top8[:, t, :],
                                in_values=prob[:, t, 0:HEADS + 7], imm_value=-2.0).then_inc(v_k1, 1)
            v.wait_ge(v_k1, TILES)
            v.tensor_tensor(out=repl[:, :, 0:HEADS], in0=repl[:, :, 0:HEADS], in1=prob[:, :, 0:HEADS],
                            op=ALU.not_equal).then_inc(v_k1, 1)
            v.wait_ge(v_k1, TILES + 1)
            v.wait_ge(p_const, 4)
            queries_low(2)
            queries_low(3)
            def maxima_of(t, gi):
                r, m, nm = ALIST[t % 2][gi]
                v.wait_ge(t_a, a_before(t) + gi + 1)
                v.tensor_reduce(out=nmax[:, t % 2, r, m:m + nm], in_=bank[4 + r][:, :].rearrange("p (m k) -> p m k", m=nm),
                                op=ALU.max, axis=AX.X, negate=True).then_inc(v_nmax, 1)

            def maxima_parts(t):
                v.wait_ge(v_nmax, a_before(t + 1))
                at_least(v, t_nmx, t - 1)
                v.tensor_copy(nmx[:, t % 2, :, 0, :], nmax[:, t % 2, :, :]).then_inc(v_nmx, 1)
                v.wait_ge(v_nmx, 2 * t + 1)
                v.tensor_tensor(out=nmx[:, t % 2, :, 1, :], in0=nmax[:, t % 2, :, :], in1=nmx[:, t % 2, :, 0, :].bitcast(F32),
                                op=ALU.subtract).then_inc(v_nmx, 1)

            for t in range(TILES):
                u = t % 2
                for tile, gi in EARLY.get(t, ()):
                    maxima_of(tile, gi)
                    if gi == len(ALIST[tile % 2]) - 1:
                        maxima_parts(tile)
                v.wait_ge(p_kv, t + 1)
                v.tensor_reduce(out=kv1[:, u, :, :], in_=kvs[:, u, :].rearrange("p (a h d) -> p a d h", a=2, h=HEADS),
                                op=ALU.add, axis=AX.X).then_inc(v_red, 1)
                v.wait_ge(v_red, t + 1)
                at_least(v, t_kt, t - 1)
                v.tensor_copy(kst[:, u, :, 0:REP:2, :],
                              kv1[:, u, 0, :].unsqueeze(1).unsqueeze(1).to_broadcast([P, 2, 2, HD])).then_inc(v_kst, 1)
                v.tensor_scalar(out=vals[:, t, VGAP:VGAP + HD], in0=kv1[:, u, 1, :], scalar1=rmax[:, t:t + 1], scalar2=None,
                                op0=ALU.mult).then_inc(v_val, 1)
                v.wait_ge(v_kst, 2 * t + 1)
                v.tensor_tensor(out=kst[:, u, :, 1, :], in0=kv1[:, u, 0, :].unsqueeze(1).to_broadcast([P, 2, HD]),
                                in1=kst[:, u, :, 0, :].bitcast(F32), op=ALU.subtract).then_inc(v_kst, 1)

            def block_end(k, step):
                acc = bank[k % 2]
                if step == 0:
                    v.wait_ge(t_pv, k + 1)
                j = step // 2 if step < 3 else 1
                cols = slice(j * T, (j + 1) * T)
                if step % 2 == 0:
                    v.reciprocal(rden[:, cols], acc[P // 2:P, cols]).then_inc(v_rden, 1)
                else:
                    v.wait_ge(v_rden, 2 * k + j + 1)
                    v.tensor_tensor(out=yt[j * P // 2:(j + 1) * P // 2, k % 2, :], in0=acc[0:P // 2, cols],
                                    in1=rden[:, cols], op=ALU.mult).then_inc(v_y, 1)
                if step == 3:
                    cut = slice((k % 2) * N + (k // 2) * T, (k % 2) * N + (k // 2 + 1) * T)
                    v.wait_ge(v_y, 2 * k + 2)
                    v.tensor_tensor(out=x[:, cut], in0=yt[:, k % 2, :], in1=x[:, cut], op=ALU.add).then_inc(v_x, 1)

            def peak_of(b):
                v.wait_ge(c_sig, 8 + b + 1)
                v.wait_ge(v_mix, 24)
                if b == B - 1:
                    v.tensor_tensor(out=of_batch(s, b), in0=halves(sig[:, b % 2, :]), in1=of_batch(mix, b, 2), op=ALU.mult).then_inc(s_ready, 1)
                v.wait_ge(s_ready, 8 + b + 1)
                v.tensor_reduce(out=peak[:, CH * b:CH * (b + 1)], in_=of_batch(s, b), op=ALU.max, axis=AX.X,
                                apply_absolute_value=True).then_inc(v_peak, 1)

            v.wait_ge(d_w23, 48)
            for k in range(CH):
                v.tensor_reduce(out=peak[:, CH * B + k:CH * B + k + 1], in_=w2in[:, k, :], op=ALU.max, axis=AX.X,
                                apply_absolute_value=True).then_inc(v_wpeak, 1)
            v.wait_ge(v_wpeak, CH)
            v.tensor_reduce(out=peak2[:, 1:2], in_=peak[:, CH * B:CH * B + CH], op=ALU.max, axis=AX.X).then_inc(v_wpeak, 1)
            v.tensor_copy(b2[:, :], b2in[:, :]).then_inc(v_wq2, 1)
            for gi in range(len(ALIST[0])):
                maxima_of(AHEAD - 1, gi)
            maxima_parts(AHEAD - 1)
            v.wait_ge(p_peak, 1)
            v.tensor_scalar(out=peakall[:, 1:2], in0=peakall[:, 1:2], scalar1=1e-6, scalar2=None, op0=ALU.max).then_inc(v_wpeak, 1)
            v.wait_ge(v_wpeak, CH + 2)
            v.reciprocal(peakinv[:, 1:2], peakall[:, 1:2]).then_inc(v_wpeak, 1)
            v.wait_ge(v_wpeak, CH + 3)
            v.tensor_scalar(out=w2q[:, :, :], in0=w2in[:, :, :], scalar1=peakinv[:, 1:2], scalar2=None,
                            op0=ALU.mult, saturate=False).then_inc(v_wq2, 1)
            for k in range(BLOCKS + 2):
                for gi in range(GROUPS):
                    if k + AHEAD < TILES:
                        for ai in ASTEPS[(k + AHEAD) % 2][gi]:
                            maxima_of(k + AHEAD, ai)
                    if 1 <= gi <= 3 and k >= 2:
                        for step in ((0,), (1, 2), (3,))[gi - 1]:
                            block_end(k - 2, step)
                        if k == BLOCKS and gi == 3:
                            peak_of(0)
                if k + AHEAD < TILES:
                    maxima_parts(k + AHEAD)

            for b in range(1, B):
                peak_of(b)
            v.wait_ge(v_peak, 4)
            v.tensor_reduce(out=peak2[:, 0:1], in_=peak[:, 0:CH * B], op=ALU.max, axis=AX.X).then_inc(v_peak, 1)
            v.wait_ge(p_peak, 2)
            v.tensor_scalar(out=peakall[:, 0:1], in0=peakall[:, 0:1], scalar1=1e-6, scalar2=None, op0=ALU.max).then_inc(v_peak, 1)
            v.wait_ge(v_peak, 6)
            v.reciprocal(peakinv[:, 0:1], peakall[:, 0:1]).then_inc(v_peak, 1)
            v.tensor_tensor(out=scale2[:, :], in0=peakall[:, 0:1], in1=peakall[:, 1:2], op=ALU.mult).then_inc(v_peak, 1)
            v.wait_ge(v_peak, 8)
            for i in range(4):
                v.tensor_scalar(out=xq[:, chunk(i)], in0=s[:, chunk(i)], scalar1=peakinv[:, 0:1], scalar2=None,
                                op0=ALU.mult, saturate=False).then_inc(v_xq, 1)

            def add_layer2(i):
                v.wait_ge(c_y2, i + 1)
                v.tensor_scalar(out=y2b[:, i % 2, :], in0=y2a[:, i % 2, :], scalar1=b2[:, PAIR_ORDER[i] // 2:PAIR_ORDER[i] // 2 + 1],
                                scalar2=None, op0=ALU.add).then_inc(v_y2b, 1)
                v.wait_ge(v_y2b, i + 1)
                v.tensor_tensor(out=x[:, chunk(i)], in0=x[:, chunk(i)], in1=y2b[:, i % 2, :], op=ALU.add).then_inc(v_x, 1)

            cond_dve(v, 3, add_layer2)
            v.memset(prob[:, :, E3:E3 + 4], LOW).then_inc(v_r, 1)
            v.wait_ge(t_rout, 3)
            lg = bank[7][:, :].rearrange("p (t e) -> p t e", t=TILES)[:, :, 0:E3]
            v.tensor_copy(prob[:, :, 0:E3], lg).then_inc(v_r, 1)
            v.wait_ge(v_r, R3 + 2)
            for t in range(TILES):
                v.max(out=top8[:, t, :], in_=prob[:, t, 0:E3 + 4]).then_inc(v_k1, 1)
            v.wait_ge(v_k1, 2 * TILES + 1)
            v.tensor_copy(rmax[:, :], top8[:, :, 0]).then_inc(v_k1, 1)
            v.memset(top8[:, :, K3:8], LOW).then_inc(v_k1, 1)
            v.wait_ge(v_k1, 2 * TILES + 3)
            for t in range(TILES):
                v.match_replace(out=repl[:, t, 0:E3 + 4], in_to_replace=top8[:, t, :],
                                in_values=prob[:, t, 0:E3 + 4], imm_value=1.1 * LOW).then_inc(v_k1, 1)
            v.wait_ge(v_k1, 3 * TILES + 3)
            v.tensor_tensor(out=repl[:, :, 0:E3], in0=repl[:, :, 0:E3], in1=prob[:, :, 0:E3], op=ALU.not_equal).then_inc(v_k1, 1)
            v.wait_ge(v_k1, 3 * TILES + 4)
            v.tensor_tensor(out=prob[:, :, 0:E3], in0=prob[:, :, 0:E3],
                            in1=rmax[:, :].unsqueeze(2).to_broadcast([P, TILES, E3]), op=ALU.subtract).then_inc(v_r, 1)
            v.wait_ge(c_r, 4)
            v.tensor_tensor(out=prob[:, :, 0:E3], in0=prob[:, :, 0:E3], in1=repl[:, :, 0:E3], op=ALU.mult).then_inc(v_r, 1)
            v.wait_ge(v_r, R3 + 4)
            v.tensor_reduce(out=rsum[:, :], in_=prob[:, :, 0:E3], op=ALU.add, axis=AX.X).then_inc(v_r, 1)
            v.wait_ge(v_r, R3 + 5)
            v.reciprocal(rsum[:, :], rsum[:, :]).then_inc(v_r, 1)
            v.wait_ge(v_r, R3 + 6)
            v.tensor_tensor(out=prob[:, :, 0:E3], in0=prob[:, :, 0:E3],
                            in1=rsum[:, :].unsqueeze(2).to_broadcast([P, TILES, E3]), op=ALU.mult).then_inc(v_r, 1)
            v.wait_ge(v_r, R3 + 7)
            v.tensor_scalar(out=gates[:, :, 0:E3], in0=prob[:, :, 0:E3], scalar1=1.0, scalar2=None, op0=ALU.add).then_inc(v_r, 1)
            v.wait_ge(v_r, R3 + 8)
            v.tensor_tensor(out=gates[:, :, 0:E3], in0=gates[:, :, 0:E3], in1=prob[:, :, 0:E3], op=ALU.subtract).then_inc(v_r, 1)
            v.wait_ge(v_r, R3 + 9)
            v.tensor_tensor(out=gates[:, :, 0:E3], in0=gates[:, :, 0:E3], in1=repl[:, :, 0:E3], op=ALU.mult).then_inc(v_r, 1)
            v.wait_ge(v_r, R3 + 10)
            v.tensor_copy(gsplit3[:, :, 0, :], gates[:, :, 0:E3]).then_inc(v_r, 1)
            v.wait_ge(v_r, R3 + 11)
            v.tensor_tensor(out=gsplit3[:, :, 1, :], in0=gates[:, :, 0:E3], in1=gsplit3[:, :, 0, :].bitcast(F32),
                            op=ALU.subtract).then_inc(v_r, 1)
            for n in range(2 * E3 + 1):
                if n < 2 * E3:
                    v.wait_ge(c_act3, n + 1)
                    v.wait_ge(t_cb3, n + 1)
                    at_least(v, v_h3lo, n - HID3 + 1)
                    v.tensor_tensor(out=hid3[:, n % HID3, :], in0=bank[6 + n % 2][:, :], in1=act3[:, n % ACT3, :], op=ALU.mult).then_inc(v_h3, 1)
                if n >= 1:
                    m = (n - 1) % HID3
                    v.wait_ge(c_h3, n)
                    at_least(v, t_d3, n - HID3)
                    v.tensor_tensor(out=hid3_lo[:, m, :], in0=hid3[:, m, :], in1=hid3_hi[:, m, :].bitcast(F32),
                                    op=ALU.subtract).then_inc(v_h3lo, 1)
            for i in range(4):
                v.wait_ge(t_d3, 2 * E3 - (1 if i < 2 else 0))
                v.tensor_tensor(out=x[:, chunk(i)], in0=bank[PAIR_ORDER[i]][:, :], in1=x[:, chunk(i)], op=ALU.add).then_inc(v_x, 1)

        @block.gpsimd
        def _(g):
            g.memset(ident[:, :], 0.0).then_inc(p_id, 1)
            g.wait_ge(p_id, 1)
            g.affine_select(out=ident[:, :], in_=ident[:, :], compare_op=ALU.not_equal, fill=1.0, base=0,
                            pattern=[[-1, P]], channel_multiplier=1).then_inc(p_id, 1)
            for k, p in enumerate(PAIR_ORDER):
                cut = slice(p * PAIR, (p + 1) * PAIR)
                g.wait_ge(c_ek, p // 2 + 1)
                g.tensor_tensor(out=ekv[:, cut], in0=ek[:, cut], in1=f[:, cut], op=ALU.mult).then_inc(p_ekv, 1)
                g.wait_ge(c_euk, p // 2 + 1)
                at_least(g, t_num, k - 1)
                pool_dkv(g, 0, p, k % 2)
                g.wait_ge(v_dscan, 4 * (k + 1))
                g.tensor_tensor(out=df[:, k % 2, :], in0=df[:, k % 2, :], in1=db[:, k % 2, :], op=ALU.add).then_inc(p_dsum, 1)
                g.wait_ge(p_dsum, k + 1)
                g.tensor_tensor(out=df[:, k % 2, :], in0=df[:, k % 2, :], in1=mix[:, cut], op=ALU.add).then_inc(p_den, 1)

            for k, p in enumerate(PAIR_ORDER[:-1]):
                cut = slice(p * PAIR, (p + 1) * PAIR)
                g.wait_ge(c_shi, k + 1)
                g.tensor_tensor(out=s_lo[:, cut], in0=s[:, cut], in1=s_hi[:, cut].bitcast(F32), op=ALU.subtract).then_inc(p_slo, 1)
            g.dma_start(spread[:, :, :, :], a["spread"]).then_inc(d_spread, 16)

            def split(c, slot, done, loads):
                g.wait_ge(d_raw[slot], 16 * loads)
                g.wait_ge(c_whi, c + 1)
                at_least(g, t_down, done)
                g.tensor_tensor(out=wlo[slot][:, :], in0=raw[:, slot, 0:WCOLS], in1=whi[slot][:, 0:WCOLS].bitcast(F32),
                                op=ALU.subtract).then_inc(p_wlo, 1)

            split(0, 0, 0, 1)

            def body(i, wkv, last=False):
                if wkv:
                    l, p, k = wkv
                    g.wait_ge(v_mix, 2 * k - 2)
                    pool_dkv(g, l, p, p % 2)
                split(2 * i + 1, 1, 4 * i, i + 1)
                if last:
                    g.wait_ge(c_w1, 1)
                    g.tensor_tensor(out=wq_lo[:, :, :], in0=w1raw[:, :, 0:C], in1=wq_hi[:, :, :].bitcast(F32),
                                    op=ALU.subtract).then_inc(p_w1, 1)
                    g.wait_ge(c_w1, 2)
                    g.tensor_tensor(out=wkv_lo[:, :, :], in0=w1raw[:, :, C:3 * C], in1=wkv_hi[:, :, :].bitcast(F32),
                                    op=ALU.subtract).then_inc(p_w1, 1)
                if wkv:
                    pool_sums(g, l, p, p % 2, k)
                if not last:
                    split(2 * i + 2, 0, 4 * i + 2, i + 2)

            body(0, None)
            with g.Fori(1, LAYERS) as l:
                g.wait_ge(c_euk, l + 2)
                for p in range(PAIRS):
                    body(PAIRS * l + p + 1 - PAIRS, (l, p, PAIRS * l + p))
            for i in range(1 + PAIRS * (LAYERS - 1), HALF_IT):
                body(i, None, i == HALF_IT - 1)
            g.wait_ge(v_x, 4)
            g.tensor_copy(identb[:, :], ident[:, :]).then_inc(p_const, 1)
            g.memset(negmask[:, :], 0.0).then_inc(p_id, 1)
            g.wait_ge(p_id, 3)
            g.affine_select(out=negmask[:, :], in_=negmask[:, :], compare_op=ALU.is_ge, fill=-1e30, base=0,
                            pattern=[[-1, P]], channel_multiplier=1).then_inc(p_const, 1)
            g.memset(kst[:, :, :, REP - 1, :].bitcast(F32), 0.0).then_inc(p_id, 1)
            g.wait_ge(p_id, 4)
            g.memset(kst[:, :, :, REP - 1, 0:2].bitcast(F32), 1.0).then_inc(p_const, 1)
            g.memset(vals[:, :, :], 0.0).then_inc(p_id, 1)
            g.wait_ge(p_id, 5)
            g.memset(vals[:, :, 2 * VGAP + HD:2 * VGAP + 2 * HD], 1.0).then_inc(p_const, 1)
            for t in range(TILES):
                g.wait_ge(c_kv, t + 1)
                if t == 0:
                    g.wait_ge(v_k1, TILES + 1)
                kv4 = kvs[:, t % 2, :].rearrange("p (a h d) -> p a h d", a=2, h=HEADS)
                g.tensor_tensor(out=kv4, in0=kv4,
                                in1=repl[:, t, 0:HEADS].unsqueeze(1).unsqueeze(3).to_broadcast([P, 2, HEADS, HD]),
                                op=ALU.mult).then_inc(p_kv, 1)
            g.wait_ge(v_wpeak, CH + 1)
            g.partition_all_reduce(peakall[:, 1:2], peak2[:, 1:2], channels=P, reduce_op=bass.bass_isa.ReduceOp.max).then_inc(p_peak, 1)
            for i in range(BLOCKS * GROUPS):
                kc, r, m, nm = BLIST[i % GROUPS]
                g.wait_ge(c_p, i + 1)
                d = p_at(pexp, i // GROUPS, kc, r, m, nm).rearrange("p (m q) -> p m q", m=nm)[:, :, 0:P]
                g.affine_select(out=d, in_=d, compare_op=ALU.is_ge, fill=0.0, base=0,
                                pattern=[[0, 2 if kc == 0 else 4], [1, P]], channel_multiplier=-1).then_inc(p_sel, 1)
            for b in range(B - 1):
                g.wait_ge(c_sig, 8 + b + 1)
                g.wait_ge(v_mix, 24)
                g.tensor_tensor(out=of_batch(s, b), in0=halves(sig[:, b % 2, :]), in1=of_batch(mix, b, 2), op=ALU.mult).then_inc(s_ready, 1)
            g.wait_ge(v_peak, 5)
            g.partition_all_reduce(peakall[:, 0:1], peak2[:, 0:1], channels=P, reduce_op=bass.bass_isa.ReduceOp.max).then_inc(p_peak, 1)
            g.dma_start(sel3[:, :, :], a["sel3"]).then_inc(d_sel3, 16)
            g.wait_ge(c_w3, 1)
            g.tensor_tensor(out=w3a_lo[:, :, :], in0=w3a_raw, in1=w3a_hi[:, :, :].bitcast(F32), op=ALU.subtract).then_inc(p_w3, 1)
            g.wait_ge(c_w3, 2)
            g.tensor_tensor(out=w3b_lo[:, :, :], in0=w3b_raw, in1=w3b_hi[:, :, :].bitcast(F32), op=ALU.subtract).then_inc(p_w3, 1)

        @block.tensor
        def _(t):
            mm = nc.tensor.matmul
            t.wait_ge(p_id, 2)
            rv = bank[7][:, :].rearrange("p (t e) -> p t e", t=TILES)
            for k in range(PAIRS + 1):
                if k < PAIRS:
                    t.wait_ge(p_dkv, k + 1)
                    t.wait_ge(v_nscan, 4 * (k + 1))
                    at_least(t, v_mix, 2 * (k - 1))
                    mm(bank[k % 2][:, :], ident[:, :], dkv[:, k % 2, :], start=True, stop=False)
                    mm(bank[k % 2][:, :], ident[:, :], nf[:, k % 2, :], start=False, stop=False)
                    mm(bank[k % 2][:, :], ident[:, :], nb[:, k % 2, :], start=False, stop=True).then_inc(t_num, 1)
                if k in (PAIRS - 1, PAIRS):
                    t.wait_ge(s_ready, 2 if k < PAIRS else 4)
                    t.wait_ge(d_in, 32)
                    for i in range(4 * (k - PAIRS + 1), 4 * (k - PAIRS + 2)):
                        for h in range(CH):
                            last = mm(rv[:, i, 0:GATES], s[:, h * N + i * P:h * N + (i + 1) * P], rw[:, h, :],
                                      start=(h == 0), stop=(h == CH - 1))
            last.then_inc(t_rout, 1)
            t.wait_ge(p_slo, 3)
            t.wait_ge(v_slo, 1)

            def down(slot, hf, n_done, first, last):
                t.wait_ge(c_hhi, n_done)
                t.wait_ge(v_hlo, n_done)
                for ch in range(CH):
                    cols = slice(2 * CH * P + ch * P, 2 * CH * P + (ch + 1) * P)
                    o = bank[2 * ch + hf][:, :]
                    mm(o, whi[slot][:, cols], hid_hi[:, hf, :], start=first, stop=False)
                    mm(o, whi[slot][:, cols], hid_lo[:, hf, :], start=False, stop=False)
                    m = mm(o, wlo[slot][:, cols], hid_hi[:, hf, :], start=False, stop=last)
                m.then_inc(t_down, 1)

            def body(i, first, final=False):
                for n in range(4):
                    ch, hf = n // 2, n % 2
                    if hf == 0:
                        t.wait_ge(c_whi, 2 * i + ch + 1)
                        t.wait_ge(p_wlo, 2 * i + ch + 1)
                    for part, (bk, free, done) in enumerate(((4, c_sil, t_g), (5, v_up, t_u))):
                        at_least(t, free, 4 * i + n)
                        for k in range(CH):
                            w = slice((k * 2 + part) * P, (k * 2 + part + 1) * P)
                            r = slice(k * N + hf * Q4, k * N + (hf + 1) * Q4)
                            mm(bank[bk][:, :], whi[ch][:, w], s_hi[:, r], start=(k == 0), stop=False)
                            mm(bank[bk][:, :], whi[ch][:, w], s_lo[:, r], start=False, stop=False)
                            m = mm(bank[bk][:, :], wlo[ch][:, w], s_hi[:, r], start=False, stop=(k == CH - 1))
                        m.then_inc(done, 1)
                    if first and n == 0:
                        t.wait_ge(v_r, R0)
                        for j in range(2):
                            for q in range(4):
                                last = nc.tensor.transpose(bank[7 - j][0:2 * GATES, q * P:(q + 1) * P],
                                                           gsplit[:, 4 * j + q, :, :].rearrange("p a e -> p (a e)").bitcast(F32),
                                                           ident[:, :])
                            last.then_inc(t_rtr, 1)
                        t.wait_ge(c_gate, 2)
                    at_least(t, v_hid, 4 * i + n)
                    mm(bank[6][:, :], whi[ch][0:2 * GATES, WCOLS:RAWCOLS], gate_t[:, hf * Q4:(hf + 1) * Q4],
                       start=True, stop=True).then_inc(t_cb, 1)
                    if not (first and n == 0):
                        down((ch - 1 + hf) % 2, 1 - hf, 4 * i + n, first and n in (1, 2), final and n == 3)

            body(0, True)
            with t.Fori(1, HALF_IT - 1) as i:
                body(i, False)
            body(HALF_IT - 1, False, True)
            down(1, 1, 4 * HALF_IT, False, True)

            def keep_warm(bk, count):
                for _ in range(count):
                    mm(bank[bk][:, :], ident[:, :], w1raw[:, 0, 0:Q4], start=True, stop=True)

            def router(bk, w, width, n_s, j):
                t.wait_ge(s_ready, n_s - 2 * (1 - j))
                r = bank[bk][:, :].rearrange("p (t e) -> p t e", t=TILES)
                for i in range(4 * j, 4 * j + 4):
                    for k in range(CH):
                        m = mm(r[:, i, 0:width], s[:, k * N + i * P:k * N + (i + 1) * P], w[:, k, :],
                               start=(k == 0), stop=(k == CH - 1))
                if j == 1:
                    m.then_inc(t_rout, 1)

            def key_rows(i):
                t.wait_ge(v_kst, 2 * i + 2)
                at_least(t, c_kt, i - 1)
                nc.tensor.transpose(bank[6 + i % 2][:, 0:P], kst[:, i % 2, :, :, :].rearrange("p r a d -> p (r a d)").bitcast(F32),
                                    ident[:, :]).then_inc(t_kt, 1)

            t.wait_ge(d_w1, 32)
            keep_warm(7, 2)
            router(4, wg1, HEADS, 8, 0)
            t.wait_ge(c_w1, 2)
            t.wait_ge(p_w1, 2)
            for n in range(4):
                if n == 2:
                    router(4, wg1, HEADS, 8, 1)
                t.wait_ge(v_slo, 1 + 2 * (n // 2 + 1))
                at_least(t, v_qc, n - 1)
                w = slice((n % 2) * P, (n % 2 + 1) * P)
                for k in range(CH):
                    r = slice(k * N + (n // 2) * Q4, k * N + (n // 2 + 1) * Q4)
                    mm(bank[5 + n % 2][:, :], wq_hi[:, k, w], s_hi[:, r], start=(k == 0), stop=False)
                    mm(bank[5 + n % 2][:, :], wq_hi[:, k, w], s_lo[:, r], start=False, stop=False)
                    last = mm(bank[5 + n % 2][:, :], wq_lo[:, k, w], s_hi[:, r], start=False, stop=(k == CH - 1))
                last.then_inc(t_qc, 1)
            t.wait_ge(d_spread, 16)
            def scores_for_maxima(i, gi):
                r, m0, nm = ALIST[i % 2][gi]
                kw = P * (i % 2 + 1)
                bk = bank[4 + r][:, :].rearrange("p (m k) -> p m k", m=nm)
                at_least(t, v_nmax, a_before(i) + gi - 1)
                mm(bk[:, :, kw - P:kw], identb[:, :], negmask[:, :].unsqueeze(1).to_broadcast([P, nm, P]),
                   start=True, stop=False, skip_group_check=True)
                rows = slice(r * HROWS, (r + 1) * HROWS)
                for m in range(m0, m0 + nm):
                    last = mm(bk[:, m - m0, :], qs[rows, m, i * P:(i + 1) * P], keys_t[rows, (i // 2) * T:(i // 2) * T + kw],
                              start=False, stop=(m == m0 + nm - 1), skip_group_check=True)
                last.then_inc(t_a, 1)

            def maxima_rows(i):
                t.wait_ge(v_nmx, 2 * i + 2)
                at_least(t, c_nmx, i)
                if i == 0:
                    t.wait_ge(c_kv, TILES - 1)
                nc.tensor.transpose(bank[0 if i < 2 else 6][0:2 * HEADS, 0:P], nmx[:, i % 2, :, :, :].rearrange("p r a m -> p (r a m)").bitcast(F32),
                                    ident[:, :]).then_inc(t_nmx, 1)

            for i in range(TILES + 2):
                if i < TILES:
                    at_least(t, c_kv, i - 1)
                    for k in range(CH):
                        r = slice(k * N + i * P, k * N + (i + 1) * P)
                        mm(bank[i % 2][:, :], s_hi[:, r], wkv_hi[:, k, :], start=(k == 0), stop=False)
                        mm(bank[i % 2][:, :], s_lo[:, r], wkv_hi[:, k, :], start=False, stop=False)
                        last = mm(bank[i % 2][:, :], s_hi[:, r], wkv_lo[:, k, :], start=False, stop=(k == CH - 1))
                    last.then_inc(t_kv, 1)
                if i == 1:
                    t.wait_ge(v_qc, 4)
                if 1 <= i <= TILES:
                    for j in range(2):
                        m = (i - 1) % 4 * 2 + j
                        cols = slice(((i - 1) // 4) * Q4, ((i - 1) // 4 + 1) * Q4)
                        at_least(t, c_qs, 2 * (i - 2) + j + 1 if i >= 2 else 0)
                        mm(bank[2 + j][:, :], spread[:, 0, m % 4, :], qc_hi[:, m // 4, cols], start=True, stop=False)
                        mm(bank[2 + j][:, :], spread[:, 1, m % 4, :], qc_lo[:, m // 4, cols], start=False, stop=True).then_inc(t_qs, 1)
                if i >= TILES:
                    maxima_rows(i - TILES)
                if i >= 2:
                    key_rows(i - 2)
                if i in EARLY:
                    if i == min(EARLY):
                        t.wait_ge(c_qs, 8)
                        t.wait_ge(c_kt, 2)
                        t.wait_ge(p_const, 2)
                    for tile, gi in EARLY[i]:
                        scores_for_maxima(tile, gi)
            t.wait_ge(c_kt, TILES)
            t.wait_ge(c_qs, 2 * TILES)
            t.wait_ge(p_const, 2)

            def scores(g):
                k = g // GROUPS
                kc, r, m, nm = BLIST[g % GROUPS]
                m0 = (k % 2) * 4 + m
                at = (k // 2) * T
                rows = slice(r * HROWS, (r + 1) * HROWS)
                at_least(t, c_p, g - 1)
                mm(bank[2 + g % 2][:, :].rearrange("p (m q) -> p m q", m=nm), keys_t[rows, at + kc * P:at + (kc + 1) * P],
                   qs[rows, m0:m0 + nm, at + kc * P:at + T], start=True, stop=True).then_inc(t_b, 1)

            def times_values(k, part):
                jobs = [(0, 0), (1, 0), (1, 1), (1, 2), (1, 3), (0, 1), (0, 2), (0, 3)]
                if part == 0:
                    t.wait_ge(p_sel, GROUPS * (k + 1))
                    t.wait_ge(v_val, 2 * (k // 2) + 2)
                    t.wait_ge(p_const, 4)
                    at_least(t, v_y, 2 * (k - 1))
                for n in range(part * len(jobs) // 5, (part + 1) * len(jobs) // 5):
                    kc, j = jobs[n]
                    w = T - kc * P
                    weights = p_at(pexp, k, kc, j % 2, 0, 4).rearrange("p (g m q) -> p g m q", g=2, m=2)[:, :, j // 2, :]
                    values = vals[:, 2 * (k // 2) + kc, VGAP - j * HD:VGAP - j * HD + P]
                    last = mm(bank[k % 2][:, :].rearrange("p (g q) -> p g q", g=2)[:, :, T - w:T], values, weights,
                              start=(n == 0), stop=(n == len(jobs) - 1), skip_group_check=True)
                if part == 4:
                    last.then_inc(t_pv, 1)

            for gi in range(2, len(ALIST[0])):
                scores_for_maxima(AHEAD - 1, gi)
            for k in range(BLOCKS + 1):
                if k % 2 == 0 and k < BLOCKS:
                    t.wait_ge(d_nmx[0], 32 * (k // 2 + 1))
                    t.wait_ge(d_nmx[1], 32 * (k // 2 + 1))
                for gi in range(GROUPS):
                    if k < BLOCKS:
                        scores(k * GROUPS + gi)
                    if k + AHEAD < TILES:
                        for ai in ASTEPS[(k + AHEAD) % 2][gi]:
                            scores_for_maxima(k + AHEAD, ai)
                    if gi == 1 and k + AHEAD - 1 < TILES:
                        maxima_rows(k + AHEAD - 1)
                    if gi >= 1 and 1 <= k <= BLOCKS:
                        times_values(k - 1, gi - 1)

            t.wait_ge(v_wq2, 2)
            for i, q in enumerate(PAIR_ORDER):
                t.wait_ge(v_xq, 2 if i < 2 else 4)
                for k in range(CH):
                    last = mm(bank[q][:, :], w2q[:, k, (q // 2) * P:(q // 2 + 1) * P],
                              xq[:, k * N + (q % 2) * Q4:k * N + (q % 2 + 1) * Q4], start=(k == 0), stop=(k == CH - 1))
                last.then_inc(t_l2, 1)

            for j in range(2):
                router(7, wg3, E3, 16, j)

            def hidden3(n):
                e, hf = n // 2, n % 2
                at_least(t, c_act3, n - 1)
                for k in range(CH):
                    w = slice(e * H3, (e + 1) * H3)
                    r = slice(k * N + hf * Q4, k * N + (hf + 1) * Q4)
                    mm(bank[4 + hf][:, :], w3a_hi[:, k, w], s_hi[:, r], start=(k == 0), stop=False)
                    mm(bank[4 + hf][:, :], w3a_hi[:, k, w], s_lo[:, r], start=False, stop=False)
                    m = mm(bank[4 + hf][:, :], w3a_lo[:, k, w], s_hi[:, r], start=False, stop=(k == CH - 1))
                m.then_inc(t_h3, 1)

            t.wait_ge(c_w3, 2)
            t.wait_ge(d_sel3, 16)
            t.wait_ge(p_w3, 2)
            t.wait_ge(v_slo, 1 + 8)
            for n in range(LEAD3 - 1):
                hidden3(n)
            t.wait_ge(v_r, R3 + 12)
            for j in range(2):
                for i in range(4):
                    last = nc.tensor.transpose(bank[7 - j][0:2 * E3, i * P:(i + 1) * P],
                                               gsplit3[:, 4 * j + i, :, :].rearrange("p a e -> p (a e)").bitcast(F32), ident[:, :])
                last.then_inc(t_rtr, 1)
            hidden3(LEAD3 - 1)
            t.wait_ge(c_gate, 4)

            def down3(n):
                t.wait_ge(c_h3, n + 1)
                t.wait_ge(v_h3lo, n + 1)
                e, hf = n // 2, n % 2
                for ch in range(CH):
                    cols = slice(ch * P, (ch + 1) * P)
                    o = bank[2 * ch + hf][:, :]
                    mm(o, w3b_hi[:, e, cols], hid3_hi[:, n % HID3, :], start=(e == 0), stop=False)
                    mm(o, w3b_hi[:, e, cols], hid3_lo[:, n % HID3, :], start=False, stop=False)
                    m = mm(o, w3b_lo[:, e, cols], hid3_hi[:, n % HID3, :], start=False, stop=(e == E3 - 1))
                m.then_inc(t_d3, 1)

            for n in range(2 * E3):
                e, hf = n // 2, n % 2
                if n + LEAD3 < 2 * E3:
                    hidden3(n + LEAD3)
                at_least(t, v_h3, n - 1)
                mm(bank[6 + hf][:, :], sel3[:, e, :], gate3_t[:, hf * Q4:(hf + 1) * Q4], start=True, stop=True).then_inc(t_cb3, 1)
                if n >= 2:
                    down3(n - 2)
            down3(2 * E3 - 2)
            down3(2 * E3 - 1)


OUT_SHAPE = (B, T, C)


def lay_out(np_, inputs):
    cm = lambda v: np_.ascontiguousarray(np_.asarray(v).reshape(N, C).T)
    g = {k: np_.asarray(v) for k, v in inputs.items()}
    a = {"xT": cm(g["x"]), "fT": cm(g["fside_BxSxS_0"]), "temb": g["cond_512"]}
    for n in ("w", "u"):
        a[n] = np_.ascontiguousarray(np_.stack([g[f"L{l}_cond_{n}"].reshape(CH, P) for l in range(LAYERS)]).transpose(2, 0, 1))
    a["router"] = np_.ascontiguousarray(np_.concatenate([g["L0_ffn_router_w"].T, g["L0_ffn_sh_gate_w"]], axis=1))

    def rows(e, sh):
        w = np_.zeros((C, CHUNKS * P), np_.float32)
        w[:, :E0 * I_MOE] = e.transpose(1, 0, 2).reshape(C, E0 * I_MOE)
        w[:, E0 * I_MOE:ROWS0] = sh
        return w.reshape(CH, P, CHUNKS, P)

    w0 = np_.zeros((CHUNKS, P, RAWCOLS), np_.float32)
    for k in range(CH):
        for j, (e, sh) in enumerate((("w_gate", "sh_gate"), ("w_up", "sh_up"))):
            w0[:, :, (k * 2 + j) * P:(k * 2 + j + 1) * P] = rows(g["L0_ffn_" + e], g["L0_ffn_" + sh])[k].transpose(1, 0, 2)
    down = np_.zeros((CHUNKS * P, C), np_.float32)
    down[:E0 * I_MOE] = g["L0_ffn_w_down"].reshape(E0 * I_MOE, C)
    down[E0 * I_MOE:ROWS0] = g["L0_ffn_sh_down"]
    w0[:, :, 2 * CH * P:WCOLS] = down.reshape(CHUNKS, P, C)
    for r in range(ROWS0):
        e = min(r // I_MOE, E0)
        w0[r // P, e, WCOLS + r % P] = 1.0
        w0[r // P, GATES + e, WCOLS + r % P] = 1.0
    a["w0"] = w0
    a["w1"] = np_.ascontiguousarray(g["L1_ffn_W_qkv"].T)
    sel = np_.zeros((P, 2, 4, P), np_.float32)
    for m in range(4):
        for r in range(2):
            for d in range(HD):
                row, at = (2 * m + r) * HD + d, r * HROWS + d
                sel[row, 0, m, [at, at + HD]] = 1.0
                sel[row, 1, m, at + 2 * HD] = 1.0
    a["spread"] = sel
    a["wg1"] = np_.ascontiguousarray(g["L1_ffn_W_gate"].T)
    a["w2"] = np_.ascontiguousarray(g["L2_ffn_weight"].T)
    a["b2"] = np_.ascontiguousarray(g["L2_ffn_bias"].reshape(CH, P).T)
    a["wg3"] = g["L3_ffn_wg"]
    a["w3a"] = np_.ascontiguousarray(g["L3_ffn_w1"].transpose(2, 0, 1).reshape(C, E3 * H3))
    a["w3b"] = np_.ascontiguousarray(g["L3_ffn_w2"].transpose(0, 2, 1))
    a["sel3"] = np_.ascontiguousarray(np_.tile(np_.repeat(np_.eye(E3, dtype=np_.float32)[:, :, None], P, axis=2), (2, 1, 1)))
    return a


def kernel(**inputs):
    import numpy as _np
    import concourse.bacc as _bacc
    from concourse.bass_utils import run_bass_kernel_spmd as _run

    nc = _bacc.Bacc("TRN2", target_bir_lowering=False, num_devices=1)
    arrays = lay_out(_np, inputs)
    aps = {k: nc.dram_tensor("in_" + k, v.shape, mybir.dt.from_np(v.dtype), kind="ExternalInput").ap() for k, v in arrays.items()}
    res = nc.dram_tensor("res", (C, N), F32, kind="ExternalOutput").ap()
    build(nc, aps, res)
    r = _run(nc, [{"in_" + k: v for k, v in arrays.items()}], core_ids=[0])
    return _np.ascontiguousarray(r.results[0]["res"].T).reshape(OUT_SHAPE)
```
